# Optimizing a Trainium2 kernel written in Bass

```python
import numpy as np
import jax
import jax.numpy as jnp

def _softmax(x, axis=-1):
    return jax.nn.softmax(x, axis=axis)

def _gelu(x):
    return jax.nn.gelu(x, approximate=True)

def _silu(x):
    return jax.nn.silu(x)

def _sigmoid(x):
    return jax.nn.sigmoid(x)

def _layernorm(x, axis=-1, eps=1e-05):
    m = jnp.mean(x, axis=axis, keepdims=True)
    v = jnp.var(x, axis=axis, keepdims=True)
    return (x - m) / jnp.sqrt(v + eps)

def _scatter_add(tgt, idx, src, axis=0):
    return tgt.at[idx].add(src)

def _segment_sum(src, seg, n):
    return jax.ops.segment_sum(src, seg, n)
kernel_name = 'mk_seq_preln_d1_jaxref_r8_fcbe02'

def setup_inputs(seed: int=0):
    np.random.seed(seed)
    _w = jnp.asarray

    def _L0_attn_setup():
        import jax, jax.numpy as jnp
        import numpy as np
        B, S, D = (2, 256, 256)
        H = 16
        Q_LORA, KV_LORA = (192, 64)
        ROPE_DIM, NOPE_DIM, V_DIM = (64, 64, 128)
        Q_HEAD_DIM = NOPE_DIM + ROPE_DIM
        ROPE_THETA, ROPE_RATIO = (10000.0, 1.0)

        def _rope_tables(seq_len):
            half = ROPE_DIM // 2
            inv_freq = ROPE_RATIO / ROPE_THETA ** (jnp.arange(half, dtype=jnp.float32) * 2.0 / ROPE_DIM)
            freqs = jnp.arange(seq_len, dtype=jnp.float32)[:, None] * inv_freq[None, :]
            return (jnp.cos(freqs), jnp.sin(freqs))

        def _apply_rope(x, cos, sin):
            x_even = x[..., 0::2]
            x_odd = x[..., 1::2]
            r_even = x_even * cos - x_odd * sin
            r_odd = x_odd * cos + x_even * sin
            return jnp.stack([r_even, r_odd], axis=-1).reshape(x.shape)
        key = jax.random.key(seed)
        ks = jax.random.split(key, 6)
        std = 0.02
        return {'hidden_states': jax.random.normal(ks[0], (B, S, D), jnp.float32), 'Wqa': jax.random.normal(ks[1], (D, Q_LORA), jnp.float32) * std, 'Wqb': jax.random.normal(ks[2], (Q_LORA, H * Q_HEAD_DIM), jnp.float32) * std, 'Wkva': jax.random.normal(ks[3], (D, KV_LORA + ROPE_DIM), jnp.float32) * std, 'Wkvb': jax.random.normal(ks[4], (KV_LORA, H * (NOPE_DIM + V_DIM)), jnp.float32) * std, 'Wo': jax.random.normal(ks[5], (H * V_DIM, D), jnp.float32) * std}
    _L0_attn_in = _L0_attn_setup()

    def _L0_ffn_setup():
        import jax, jax.numpy as jnp
        import numpy as np
        H = 256
        I = 176
        E = 16
        K = 2
        SI = I * 2

        def _swiglu(gu, inter):
            g, u = (gu[..., :inter], gu[..., inter:])
            return jax.nn.silu(g) * u
        key = jax.random.key(seed)
        ks = jax.random.split(key, 6)
        s = 0.02
        hidden_states = jax.random.normal(ks[0], (1, 128, H), dtype=jnp.float32)
        gate_w = jax.random.normal(ks[1], (E, H), dtype=jnp.float32) * s
        w_gate_up = jax.random.normal(ks[2], (E, H, 2 * I), dtype=jnp.float32) * s
        w_down = jax.random.normal(ks[3], (E, I, H), dtype=jnp.float32) * s
        shared_gate_up = jax.random.normal(ks[4], (H, 2 * SI), dtype=jnp.float32) * s
        shared_down = jax.random.normal(ks[5], (SI, H), dtype=jnp.float32) * s
        return {'hidden_states': hidden_states, 'gate_w': gate_w, 'w_gate_up': w_gate_up, 'w_down': w_down, 'shared_gate_up': shared_gate_up, 'shared_down': shared_down}
    _L0_ffn_in = _L0_ffn_setup()
    _d = {'L0_attn_hidden_states': _L0_attn_in['hidden_states'], 'L0_attn_Wqa': _L0_attn_in['Wqa'], 'L0_attn_Wqb': _L0_attn_in['Wqb'], 'L0_attn_Wkva': _L0_attn_in['Wkva'], 'L0_attn_Wkvb': _L0_attn_in['Wkvb'], 'L0_attn_Wo': _L0_attn_in['Wo'], 'L0_ffn_gate_w': _L0_ffn_in['gate_w'], 'L0_ffn_w_gate_up': _L0_ffn_in['w_gate_up'], 'L0_ffn_w_down': _L0_ffn_in['w_down'], 'L0_ffn_shared_gate_up': _L0_ffn_in['shared_gate_up'], 'L0_ffn_shared_down': _L0_ffn_in['shared_down']}
    _x0 = _d['L0_attn_hidden_states']
    _d['L0_attn_hidden_states'] = jax.random.normal(jax.random.fold_in(jax.random.key(seed), 1), (4, 1024, 256), dtype=_x0.dtype)
    del _x0
    return _d

def reference(L0_attn_hidden_states, L0_attn_Wqa, L0_attn_Wqb, L0_attn_Wkva, L0_attn_Wkvb, L0_attn_Wo, L0_ffn_gate_w, L0_ffn_w_gate_up, L0_ffn_w_down, L0_ffn_shared_gate_up, L0_ffn_shared_down):

    def _L0_attn_ref(hidden_states, Wqa, Wqb, Wkva, Wkvb, Wo):
        import jax, jax.numpy as jnp
        import numpy as np
        B, S, D = (2, 256, 256)
        H = 16
        Q_LORA, KV_LORA = (192, 64)
        ROPE_DIM, NOPE_DIM, V_DIM = (64, 64, 128)
        Q_HEAD_DIM = NOPE_DIM + ROPE_DIM
        ROPE_THETA, ROPE_RATIO = (10000.0, 1.0)

        def _rope_tables(seq_len):
            half = ROPE_DIM // 2
            inv_freq = ROPE_RATIO / ROPE_THETA ** (jnp.arange(half, dtype=jnp.float32) * 2.0 / ROPE_DIM)
            freqs = jnp.arange(seq_len, dtype=jnp.float32)[:, None] * inv_freq[None, :]
            return (jnp.cos(freqs), jnp.sin(freqs))

        def _apply_rope(x, cos, sin):
            x_even = x[..., 0::2]
            x_odd = x[..., 1::2]
            r_even = x_even * cos - x_odd * sin
            r_odd = x_odd * cos + x_even * sin
            return jnp.stack([r_even, r_odd], axis=-1).reshape(x.shape)
        b, s, _ = hidden_states.shape
        scale = Q_HEAD_DIM ** (-0.5)
        q_latent = hidden_states @ Wqa
        q = (q_latent @ Wqb).reshape(b, s, H, Q_HEAD_DIM)
        q = jnp.transpose(q, (0, 2, 1, 3))
        q_nope, q_pe = (q[..., :NOPE_DIM], q[..., NOPE_DIM:])
        kv_comp = hidden_states @ Wkva
        c_kv, k_pe = (kv_comp[..., :KV_LORA], kv_comp[..., KV_LORA:])
        cos, sin = _rope_tables(s)
        q_pe = _apply_rope(q_pe, cos, sin)
        k_pe = _apply_rope(k_pe, cos, sin)
        kv = (c_kv @ Wkvb).reshape(b, s, H, NOPE_DIM + V_DIM)
        kv = jnp.transpose(kv, (0, 2, 1, 3))
        k_nope, v = (kv[..., :NOPE_DIM], kv[..., NOPE_DIM:])
        k_pe_b = jnp.broadcast_to(k_pe[:, None], (b, H, s, ROPE_DIM))
        q_full = jnp.concatenate([q_nope, q_pe], axis=-1)
        k_full = jnp.concatenate([k_nope, k_pe_b], axis=-1)
        scores = jnp.einsum('bhqd,bhkd->bhqk', q_full, k_full) * scale
        causal = jnp.tril(jnp.ones((s, s), dtype=bool))
        scores = jnp.where(causal[None, None], scores, jnp.finfo(scores.dtype).min)
        probs = jax.nn.softmax(scores, axis=-1)
        attn = jnp.einsum('bhqk,bhkd->bhqd', probs, v)
        out = jnp.transpose(attn, (0, 2, 1, 3)).reshape(b, s, H * V_DIM)
        return out @ Wo

    def _L0_ffn_ref(hidden_states, gate_w, w_gate_up, w_down, shared_gate_up, shared_down):
        import jax, jax.numpy as jnp
        import numpy as np
        H = 256
        I = 176
        E = 16
        K = 2
        SI = I * 2

        def _swiglu(gu, inter):
            g, u = (gu[..., :inter], gu[..., inter:])
            return jax.nn.silu(g) * u
        orig_shape = hidden_states.shape
        x = hidden_states.reshape(-1, H)
        logits = jnp.einsum('th,eh->te', x, gate_w)
        scores = jax.nn.softmax(logits, axis=-1)
        topk_w, topk_idx = jax.lax.top_k(scores, K)
        combine = jnp.sum(jax.nn.one_hot(topk_idx, E, dtype=x.dtype) * topk_w[..., None], axis=1)
        gu = jnp.einsum('th,ehj->etj', x, w_gate_up)
        h = _swiglu(gu, I)
        y = jnp.einsum('eti,eih,te->th', h, w_down, combine)
        gu_s = x @ shared_gate_up
        y = y + _swiglu(gu_s, SI) @ shared_down
        return y.reshape(orig_shape)
    x = L0_attn_hidden_states
    x = x + _L0_attn_ref(_layernorm(x, axis=-1), L0_attn_Wqa, L0_attn_Wqb, L0_attn_Wkva, L0_attn_Wkvb, L0_attn_Wo)
    x = x + _L0_ffn_ref(_layernorm(x, axis=-1), L0_ffn_gate_w, L0_ffn_w_gate_up, L0_ffn_w_down, L0_ffn_shared_gate_up, L0_ffn_shared_down)
    return x

_drawn_inputs = setup_inputs


def setup_inputs(seed=0):
    import zlib

    import numpy as np

    out = dict(_drawn_inputs(seed))
    spreads = {}
    factors = {'L0_attn_Wqa': 8.0,
     'L0_attn_Wqb': 8.0,
     'L0_attn_Wkva': 8.0,
     'L0_attn_Wkvb': 8.0,
     'L0_attn_Wo': 8.0,
     'L0_ffn_gate_w': 8.0,
     'L0_ffn_w_gate_up': 8.0,
     'L0_ffn_w_down': 8.0,
     'L0_ffn_shared_gate_up': 2.836,
     'L0_ffn_shared_down': 2.841}
    for name, (base, spread) in spreads.items():
        noise = np.random.default_rng([zlib.crc32(name.encode()), seed]).standard_normal(out[name].shape)
        drawn = base * np.exp(spread * noise) if base else spread * noise
        out[name] = jnp.asarray(drawn.astype(out[name].dtype))
    for name, factor in factors.items():
        out[name] = (out[name] * factor).astype(out[name].dtype)
    return out
```

```python
from collections import namedtuple
from contextlib import ExitStack

import numpy as np

import concourse.bass as bass
from concourse import mybir

ALU = mybir.AluOpType
ACT = mybir.ActivationFunctionType
AX_X = mybir.AxisListType.X
F32, F16, BF16 = mybir.dt.float32, mybir.dt.float16, mybir.dt.bfloat16
I32, U32 = mybir.dt.int32, mybir.dt.uint32
ds = bass.ds

P = 128
B, S, D = 4, 1024, 256
H, QL, NOPE, ROPE, VD = 16, 192, 64, 64, 128
C = 64
HD = NOPE + ROPE
TB = S // P
NT = B * TB
KD = D // P
NQ = H * HD
E, I_E, TOPK = 16, 176, 2
SI = 2 * I_E
KE = 88
EPS = 1e-5
LIST = NT * P + P
DUMMY = E * LIST
NMT = (NT * P * TOPK) // P + E
ROW = 2 * D + 2
NY = TOPK * NT * P
WMAX = 64.0
HSCALE = 2.0 ** -15
GROUP = [8, 4, 2, 2, 1, 1, 1, 1]
UNITS = [H // g for g in GROUP]
UB = sum(UNITS)
UPRE = [sum(UNITS[:i]) for i in range(TB)]
LN_STEPS = 15
NEWTON = 3
SEED = 1597463007.0
A_Q, A_KV, A_O, A_SG, A_SD, A_R, A_GU, A_D = range(8)


class Tile:

    def __init__(self, off, b=None):
        self.off, self.b = off, b
        self.i = off % TB

    def at(self, k):
        return Tile(self.off + k, self.b)

    def count(self, per, k):
        return per * self.off + k if self.b is None else self.b * (per * TB) + (per * self.off + k)

    def pair(self, per):
        n = per * (self.off // 2 + 1)
        return n if self.b is None else self.b * (per * TB // 2) + n

    def units(self, per, u, k):
        n = per * (UB * (self.off // TB) + UPRE[self.i]) + k
        n = n + per * u
        return n if self.b is None else self.b * (per * UB) + n

    def row(self):
        return P * self.off if self.b is None else self.b * (P * TB) + P * self.off

    def exists(self):
        return self.b is not None or 0 <= self.off < NT


class Steps:

    def __init__(self, eng, sem, per, first):
        self.eng, self.sem, self.per, self.first, self.n = eng, sem, per, first, 0

    def do(self, ins, after_wait=None):
        self.n += 1
        assert self.n <= self.per
        ins.then_inc(self.sem, 1)
        self.eng.wait_ge(self.sem, self.first(self.per, self.n))
        if after_wait is not None:
            after_wait(self.eng)


PEEL = 4


def sections(eng, emit):
    for off in range(PEEL):
        emit(Tile(off))
    with eng.Fori(0, B - 1) as b:
        for off in range(PEEL, PEEL + TB):
            emit(Tile(off, b))
    for off in range((B - 1) * TB + PEEL, NT + 2):
        emit(Tile(off))


def build(nc, x, wqaT, wqb_peT, wqb_nopeT, wkva, wkT, wvT, wo, gateT, wgu, wd, wsg, wsd,
          cos_t, sin_t, ident, causal, tri, iota_e, iota_k, iota_n, tok_ids, out):
    nc.disable_value_cache = True
    ctx = ExitStack()
    with ctx:
        def sb(name, shape, dt):
            return ctx.enter_context(nc.sbuf_tensor(name, shape, dt))

        def sem(name):
            return ctx.enter_context(nc.semaphore(name))

        lists = nc.dram_tensor("lists", [DUMMY + P, ROW], F16, kind="Internal").ap()
        y_exp = nc.dram_tensor("y_exp", [NY, D], F32, kind="Internal").ap()
        dense = nc.dram_tensor("dense", [NT * P, D], F32, kind="Internal").ap()

        cos_sb = sb("cos_sb", [P, TB, ROPE], F32)
        sin_sb = sb("sin_sb", [P, TB, ROPE], F32)
        id32 = sb("id32", [P, P], F32)
        id16 = sb("id16", [P, P], F16)
        idbf = sb("idbf", [P, P], BF16)
        mask32 = sb("mask32", [P, P], F32)
        maskbf = sb("maskbf", [P, P], BF16)
        tri16 = sb("tri16", [P, P], F16)
        ones16 = sb("ones16", [P, P], F16)
        iota_e_sb = sb("iota_e_sb", [P, E], F32)
        iota_k_sb = sb("iota_k_sb", [P, E, NT], F32)
        iota_n_sb = sb("iota_n_sb", [1, NMT], F32)
        wq = sb("wq", [P, 2, KD, NQ + 2 * C], F16)
        wout = sb("wout", [P, 2, H // 2, D], F16)
        wsg_sb = sb("wsg_sb", [P, 2, KD, 2 * SI], F16)
        wsd_sb = sb("wsd_sb", [P, 2, 3, D], F16)
        wr_sb = sb("wr_sb", [P, 2, KD, E], F16)
        wgu_sb = sb("wgu_sb", [P, KD, E, 2, 2 * I_E], F16)
        wd_sb = sb("wd_sb", [P, 2, E, 2, D], F16)
        amax = sb("amax", [P, 8], F32)
        amax_all = sb("amax_all", [P, 8], F32)
        winv = sb("winv", [P, 8], F32)
        wamp = sb("wamp", [P, 8], F32)
        fac = sb("fac", [P, 8], F32)
        f_att, f_natt, f_out, f_sgh, f_sd, f_guh, f_ed = (fac[:, k:k + 1] for k in range(7))
        amax_gu = sb("amax_gu", [P, 4], F32)

        x_sb = sb("x_sb", [P, 4, D], F32)
        ln_st = sb("ln_st", [P, 2, 8], F32)
        ln_mv = sb("ln_mv", [P, 2, 2], F32)
        ln_w = sb("ln_w", [P, 2, 4], F32)
        ln_i = sb("ln_i", [P, 2, 1], I32)
        xn = sb("xn", [P, 2, D], F32)
        xs = sb("xs", [P, 2, 2, D], F16)
        xT = sb("xT", [P, 2, KD, P], F16)
        NPE = (H + 1) * ROPE
        work = sb("work", [P, 3 * NPE + H * HD + HD], F32)
        pe = work[:, 0:NPE].rearrange("p (h r) -> p h r", r=ROPE)
        rot = work[:, NPE:2 * NPE].rearrange("p (h r) -> p h r", r=ROPE)
        rot2 = work[:, 2 * NPE:3 * NPE].rearrange("p (h r) -> p h r", r=ROPE)
        qs = work[:, 3 * NPE:3 * NPE + H * HD].bitcast(F16).rearrange("p (s h d) -> p s h d", s=2, h=H)
        ks = work[:, 3 * NPE + H * HD:].bitcast(F16).rearrange("p (s d) -> p s d", s=2)
        qT = sb("qT", [P, 2, 2, H * P], F16)
        kT = sb("kT", [P, 2, S], F16)
        ckv = sb("ckv", [P, 2, TB, C], F16)
        probs = sb("probs", [P, S], F32)
        pT = sb("pT", [P, 2, 2, 512], F16)
        smax = sb("smax", [P, 2, 8], F32)
        nmax = sb("nmax", [P, 2, 8], F32)
        ssum = sb("ssum", [P, 2, H], F32)
        rsum = sb("rsum", [P, H], F32)
        o_sb = probs
        os_ = sb("os_", [P, 2, H * C], F16)
        oT = sb("oT", [P, 2, H // 2, P], F16)
        x1 = sb("x1", [P, 2, D], F32)
        xs2 = sb("xs2", [P, 2, TOPK, ROW], F16)
        x2T = sb("x2T", [P, 2, KD, P], F16)
        gate = sb("gate", [P, SI], F32)
        hid = sb("hid", [P, SI], F32)
        hs = sb("hs", [P, 2, SI], F16)
        hT = sb("hT", [P, 2, 3, P], F16)
        den = sb("den", [P, 2, D], F32)
        lg_all = sb("lg_all", [P, NT, E], F32)
        top_all = sb("top_all", [P, NT, TOPK], F32)
        lg = sb("lg", [P, 2, E], F32)
        top8 = sb("top8", [P, 2, 8], F32)
        top_ix = sb("top_ix", [P, 2, 8], U32)
        ixf = sb("ixf", [P, 2], F32)
        pick = sb("pick", [P, 2, TOPK, E], F32)
        picked = sb("picked", [P, 2, E], F16)
        place = sb("place", [P, E], F32)
        place_k = sb("place_k", [P, E], F32)
        slot_f = sb("slot_f", [P, TOPK], F32)
        slot = sb("slot", [P, 2, TOPK], I32)
        used = sb("used", [P, E], F32)
        dest_f = sb("dest_f", [P, TOPK], F32)

        s_ps = ctx.enter_context(nc.psum_tensor("s_ps", [P, 4, 512], F32))
        t_ps = ctx.enter_context(nc.psum_tensor("t_ps", [P, 2, 512], F32))
        o_ps = ctx.enter_context(nc.psum_tensor("o_ps", [P, 2, 512], F32))
        tt = [t_ps[:, g, :].bitcast(F16) for g in range(2)]
        st = [s_ps[:, g, :].bitcast(F16) for g in range(4)]
        ot = [o_ps[:, g, :].bitcast(F16) for g in range(2)]
        o_flat = o_ps[:, :, :].rearrange("p a n -> p (a n)")

        names = """c_in w_a w_b w_x0 c_ready qb_made qb_copied wq_made wq_copied wo_made wo_copied prep
                   amax_ready amax_reduced scales hi_made lo_made w_gu w_d
                   ln1s ln1_done xT_made xT_ready q_made hi_q lo_q pe_ready rope_s rope_done hi_rope lo_rope
                   qT_made qT_act qT_dve ckv_ready s_made maxs max_ready exp_done p_made hi_p lo_p o_made
                   o_evs o_ready hi_o lo_o oT_made oT_act oT_dve proj_made x1_done ln2s ln2_done x2T_made x2T_ready
                   gu_made lgt_made gate_done hids hid_done hi_h lo_h route_s mask_ready rank_made slot_s slot_done
                   hT_made hT_ready down_made dense_done listed
                   used_ready pads tail_s tab_ready gu_prep gu_hi gu_lo gu_amax gu_red gu_scale
                   m_xT m_xTs m_gu m_gate m_q m_hid m_hi m_lo m_hT m_hTs m_down m_y
                   passed c_w w_exp c_sum c_y0""".split()
        s = namedtuple("Signals", names)(*(sem(n) for n in names))
        xin = [sem(f"x_in{k}") for k in range(4)]
        scattered = [sem(f"scattered{k}") for k in range(2)]
        stored = [sem(f"stored{k}") for k in range(2)]
        xg_in = [sem(f"xg_in{k}") for k in range(8)]
        m_out = [sem(f"m_out{k}") for k in range(8)]
        c_loaded = [sem(f"c_loaded{k}") for k in range(2)]
        c_out = [sem(f"c_out{k}") for k in range(2)]

        ga = wgu_sb[:, :, :, :, :].rearrange("p k e s j -> p (k e s j)").bitcast(F32)
        gb = wd_sb[:, :, :, :, :].rearrange("p k e s j -> p (k e s j)").bitcast(F32)

        def cut(view, at, *shape):
            n = int(np.prod(shape))
            v = view[:, at:at + n]
            return (v.rearrange("p (a b) -> p a b", a=shape[0]) if len(shape) == 2 else v), at + n

        r_wqaT, at = cut(ga, 0, 2, D)
        r_pe, at = cut(ga, at, 2, H * ROPE)
        r_nopeT, at = cut(ga, at, H, QL)
        r_wkT, at = cut(ga, at, H, C)
        r_qb, at = cut(ga, at, 2, H * C)
        r_wvT, at = cut(ga, at, H, C)
        r_wsd, at = cut(ga, at, 3, D)
        r_wo, at = cut(gb, 0, H, D)
        r_out, at = cut(gb, at, H // 2, D)
        r_wsg, at = cut(gb, at, KD, 2 * SI)
        r_wr, at = cut(gb, at, KD, E)
        r_wq = work[:, 0:KD * (NQ + 2 * C)].rearrange("p (k n) -> p k n", k=KD)
        QLB = QL - P
        SPLITS = [
            (r_wq[:, :, 0:NQ], wq[:, 0, :, 0:NQ], wq[:, 1, :, 0:NQ], P, A_Q),
            (r_wq[:, :, NQ:], wq[:, 0, :, NQ:], wq[:, 1, :, NQ:], P, A_KV),
            (r_out, wout[:, 0], wout[:, 1], P, A_O),
            (r_wsg, wsg_sb[:, 0], wsg_sb[:, 1], P, A_SG),
            (r_wsd, wsd_sb[:, 0], wsd_sb[:, 1], P, A_SD),
            (r_wr, wr_sb[:, 0], wr_sb[:, 1], P, A_R),
        ]
        N_EARLY = 8
        wgu_v = wgu.rearrange("e (k p) j -> p k e j", k=KD)
        wd_v = wd.rearrange("e (k p) n -> p k e n", p=KE)
        gu_raw = ga.rearrange("p (k e j) -> p k e j", k=KD, e=E)
        d_raw = gb.rearrange("p (k e j) -> p k e j", k=2, e=E)
        GC = 4
        gu_w = work[:, 0:GC * 2 * I_E].rearrange("p (e j) -> p e j", e=GC)
        d_w = work[:, GC * 2 * I_E:GC * (2 * I_E + D)].rearrange("p (e j) -> p e j", e=GC)

        XB, YB = 8, 4
        def carve(view, at, shape, dt):
            words = int(np.prod(shape)) * (2 if dt == F16 else 4) // 4
            v = view[:, at:at + words]
            v = v if dt == F32 else v.bitcast(dt)
            names_ = "abcd"[:len(shape)]
            sizes = dict(zip(names_, shape))
            return v.rearrange(f"p ({' '.join(names_)}) -> p {' '.join(names_)}", **sizes), at + words

        q_mem = qT[:, :, :, :].rearrange("p t a n -> p (t a n)").bitcast(F32)
        os_mem = os_[:, :, :].rearrange("p a n -> p (a n)").bitcast(F32)
        xg, w_at = carve(work, GC * (2 * I_E + D), (XB, ROW), F16)
        pT_mem = pT[:, :, :, :].rearrange("p a g n -> p (a g n)").bitcast(F32)
        xgT, p_at = carve(pT_mem, 0, (2, 2, KD, P), F16)
        m_hs, p_at = carve(pT_mem, p_at, (2, 2, I_E), F16)
        m_hT_sb, w_at = carve(work, w_at, (2, 2, P), F16)
        m_hT_sb = m_hT_sb[0:KE]
        m_g, m_m = gate[:, 0:I_E], hid[:, 0:I_E]
        m_h, _ = carve(x1[:, :, :].rearrange("p a n -> p (a n)"), 0, (2, I_E), F32)
        m_ys, _ = carve(o_sb, 0, (YB, D), F32)
        CT = 2
        c_in, q_at = carve(q_mem, 0, (2, 3, CT * D), F32)
        c_in = c_in.rearrange("p q k (c n) -> p q k c n", c=CT)
        c_o, q_at = carve(q_mem, q_at, (2, CT, D), F32)
        ge, ge_at = carve(q_mem, 0, (NMT, E), F32)
        ge2, ge_at = carve(q_mem, ge_at, (NMT, E), F32)
        ge, ge2 = ge[0:1], ge2[0:1]
        cmp_k, _ = carve(probs, 0, (E, NT), F32)
        w_e, os_at = carve(os_mem, 0, (NT, E), F32)
        w_d, os_at = carve(os_mem, os_at, (NT, E), F32)
        cnt = sb("cnt", [P, E], F32)
        tiles_e = sb("tiles_e", [P, E], F32)
        ends = sb("ends", [P, E], F32)
        ones_e = sb("ones_e", [P, E], F32)
        jump = sb("jump", [P, E], F32)
        t_row = sb("t_row", [1, NMT], F32)
        t_exp = sb("t_exp", [1, NMT], F32)
        tab = sb("tab", [1, 2, NMT], I32)
        free_i = sb("free_i", [1, E], I32)
        pad, _ = carve(hT[:, :, :, :].rearrange("p a k n -> p (a k n)").bitcast(F32), 0, (ROW,), F16)
        w_s = sb("w_s", [P, NT], F32)
        w_k = sb("w_k", [P, NT, TOPK], F32)
        w_t = sb("w_t", [P, NT], F32)

        def own_wait(eng):
            eng.sem_inc(s.passed, 1)

        block = ctx.enter_context(nc.Block())

        @block.sync
        def _(sp):
            def load(dst, src, done):
                sp.dma_start(dst, src).then_inc(done, 16)

            load(r_nopeT[0:NOPE], wqb_nopeT, s.w_a)
            load(r_wkT[0:NOPE], wkT, s.w_a)
            load(r_wqaT[:, 0, :], wqaT[0:P, :], s.w_a)
            load(r_wqaT[0:QLB, 1, :], wqaT[P:QL, :], s.w_a)
            load(r_pe[:, 0, :], wqb_peT[0:P, :], s.w_a)
            load(r_pe[0:QLB, 1, :], wqb_peT[P:QL, :], s.w_a)
            load(r_wvT, wvT, s.w_a)
            load(r_wo, wo.rearrange("(h d) n -> d h n", d=VD), s.w_a)
            load(r_wq[:, :, NQ:], wkva.rearrange("(k p) n -> p k n", p=P), s.w_b)
            load(r_wsg, wsg.rearrange("(k p) n -> p k n", p=P), s.w_b)
            load(r_wsd[:, 0:2, :], wsd[0:2 * P, :].rearrange("(k p) n -> p k n", p=P), s.w_b)
            load(r_wsd[0:SI - 2 * P, 2, :], wsd[2 * P:SI, :], s.w_b)
            load(r_wr, gateT.rearrange("(k p) n -> p k n", p=P), s.w_b)
            for dst, src in ((id32[:, :], ident), (mask32[:, :], causal), (probs[:, 0:P], tri),
                             (cos_sb[:, :, :], cos_t), (sin_sb[:, :, :], sin_t), (iota_e_sb[:, :], iota_e),
                             (iota_k_sb[:, :, :], iota_k), (iota_n_sb[:, :], iota_n), (dest_f[:, :], tok_ids)):
                load(dst, src, s.c_in)
            for k in range(3):
                load(x_sb[:, k, :], x[k * P:(k + 1) * P, :], xin[k])

            def store_dense(t):
                sp.wait_ge(s.dense_done, t.count(1, 1))
                own_wait(sp)
                sp.dma_start(dense[ds(t.row(), P), :], den[:, t.off % 2, :]).then_inc(stored[t.off % 2], 16)

            def section(t):
                p, n3 = t.at(-1), t.at(3)
                if p.exists() and n3.exists():
                    sp.wait_ge(s.x1_done, p.count(1, 1))
                    own_wait(sp)
                if n3.exists():
                    sp.dma_start(x_sb[:, n3.off % 4, :], x[ds(n3.row(), P), :]).then_inc(xin[n3.off % 4], 16)
                if t.at(-2).exists():
                    store_dense(t.at(-2))
            sp.wait_ge(s.lo_made, len(SPLITS))
            for k in range(KD):
                load(gu_raw[:, k], wgu_v[:, k], s.w_gu)
            for k in range(2):
                load(d_raw[0:KE, k], wd_v[:, k], s.w_d)
            sections(sp, section)

            sp.wait_ge(s.used_ready, 1)
            sp.dma_start(lists[DUMMY:DUMMY + P, :], pad[:, :]).then_inc(s.pads, 16)
            for e in range(E):
                row = sp.value_load(free_i[0:1, e:e + 1], min_val=0, max_val=DUMMY - P)
                sp.dma_start(lists[ds(row, P), :], pad[:, :]).then_inc(s.pads, 16)
            sp.wait_ge(s.pads, 16 * (E + 1))
            for par in range(2):
                sp.wait_ge(scattered[par], 16 * TOPK * NT // 2)
            sp.wait_ge(s.tab_ready, 1)

            def expert_rows(n, q):
                row = sp.value_load(tab[0:1, 0, ds(n, 1)], min_val=0, max_val=DUMMY)
                sp.dma_start(xg[:, q, :], lists[ds(row, P), :]).then_inc(xg_in[q], 16)
            for q in range(XB):
                expert_rows(q, q)
            with sp.Fori(1, NMT // XB) as m:
                for q in range(XB):
                    sp.wait_ge(m_out[q], m * 16)
                    own_wait(sp)
                    expert_rows(m * XB + q, q)
            for q in range(XB):
                sp.wait_ge(m_out[q], 16 * (NMT // XB))
            for par in range(2):
                sp.wait_ge(stored[par], 16 * NT // 2)

            def rows(a, first):
                return a[ds(first, CT * P), :].rearrange("(c p) n -> p c n", p=P)

            NC = NT // CT
            with sp.Fori(0, NC // 2) as m:
                for q in range(2):
                    first = m * (2 * CT * P) + q * CT * P
                    sp.wait_ge(s.c_sum, m * 2 + q + 1)
                    own_wait(sp)
                    sp.dma_start(c_in[:, q, 0], rows(dense, first)).then_inc(c_loaded[q], 16)
                    sp.dma_start(c_in[:, q, 1], rows(y_exp, first)).then_inc(c_loaded[q], 16)
                    sp.dma_start(c_in[:, q, 2], rows(y_exp, first + NT * P)).then_inc(c_loaded[q], 16)

        def rank_pairs(i):
            return [(g, j) for g in range(GROUP[i]) for j in range(i + 1)]

        def s_off(i, g):
            return g * (P if i == 0 else 2 * P if i == 1 else 512)

        def att_loop(eng, t, unit):
            n = UNITS[t.i]
            rounds = n // 2 - 1
            if rounds == 1:
                unit(0, 0, True)
                unit(1, 1, True)
            elif rounds > 1:
                with eng.Fori(0, rounds) as k:
                    unit(k * 2, 0, True)
                    unit(k * 2 + 1, 1, True)
            unit(n - 2, 0, False)
            unit(n - 1, 1, False)

        @block.tensor
        def _(pe_):
            def mm(o, a, b, start, stop):
                return pe_.matmul(o, a, b, start=start, stop=stop)

            pe_.wait_ge(s.w_a, 16 * N_EARLY)
            for h in range(H):
                mm(o_ps[:, h // 8, (h % 8) * C:(h % 8 + 1) * C], r_nopeT[0:NOPE, h, 0:P], r_wkT[0:NOPE, h, :], True, True)
                last = mm(t_ps[0:QLB, h // 8, (h % 8) * C:(h % 8 + 1) * C], r_nopeT[0:NOPE, h, P:QL],
                          r_wkT[0:NOPE, h, :], True, True)
            last.then_inc(s.qb_made, 1)
            pe_.wait_ge(s.qb_copied, 1)
            for m in range(KD):
                for c in range(NQ // 512):
                    src = r_qb if c < 2 else r_pe
                    cc = slice((c % 2) * 512, (c % 2) * 512 + 512)
                    if m:
                        pe_.wait_ge(s.wq_copied, c + 1)
                    mm(s_ps[:, c, :], r_wqaT[:, 0, m * P:(m + 1) * P], src[:, 0, cc], True, False)
                    mm(s_ps[:, c, :], r_wqaT[0:QLB, 1, m * P:(m + 1) * P], src[0:QLB, 1, cc], False,
                       True).then_inc(s.wq_made, 1)
            for hp in range(H // 2):
                bank = (o_ps if hp % 4 < 2 else t_ps)[:, hp % 2, 0:D]
                if hp >= 4:
                    pe_.wait_ge(s.wo_copied, hp - 3)
                for e in range(2):
                    last = mm(bank[e * C:(e + 1) * C], r_wvT[:, 2 * hp + e, :], r_wo[:, 2 * hp + e, :], True, True)
                last.then_inc(s.wo_made, 1)

            def x_transposes(n):
                if n.off > 0 or n.b is not None:
                    pe_.wait_ge(s.qT_act, n.at(-1).count(3, 3))
                    pe_.wait_ge(s.qT_dve, n.at(-1).count(2, 2))
                pe_.wait_ge(s.ln1_done, n.count(2, 2))
                for sp_ in range(2):
                    for k in range(KD):
                        last = pe_.transpose(tt[0][:, (2 * sp_ + k) * P:(2 * sp_ + k + 1) * P],
                                             xs[:, n.off % 2, sp_, k * P:(k + 1) * P], id16[:, :])
                last.then_inc(s.xT_made, 1)

            def split_product(o, lhs, rhs, done):
                n = len(done)
                first = True
                for k in done:
                    for a, b in ((0, 0), (0, 1), (1, 0)):
                        last = mm(o, lhs(a, k), rhs(b, k), first, k == done[-1] and a == 1)
                        first = False
                return last

            def projections(n):
                if n.at(-3).exists():
                    pe_.wait_ge(s.hid_done, n.at(-3).count(1, 1))
                    pe_.wait_ge(s.mask_ready, n.at(-3).count(1, 1))
                pe_.wait_ge(s.xT_ready, n.count(1, 1))
                for bank, c0, w in ((t_ps[:, 1, 0:P], NQ, 2 * C), (s_ps[:, 2, :], H * NOPE, 512),
                                    (s_ps[:, 3, :], H * NOPE + 512, 512), (s_ps[:, 0, :], 0, 512), (s_ps[:, 1, :], 512, 512)):
                    split_product(bank, lambda a, k: xT[:, a, k, :], lambda b, k: wq[:, b, k, c0:c0 + w],
                                  list(range(KD))).then_inc(s.q_made, 1)

            def q_transposes(n):
                pe_.wait_ge(s.lo_q, n.count(3, 3))
                pe_.wait_ge(s.hi_rope, n.count(1, 1))
                pe_.wait_ge(s.lo_rope, n.count(1, 1))
                for g, bank in enumerate((tt[0], tt[1], st[2], st[3])):
                    for h in range(8):
                        last = pe_.transpose(bank[:, h * P:(h + 1) * P], qs[:, g // 2, (g % 2) * 8 + h, :], id16[:, :])
                    last.then_inc(s.qT_made, 1)
                pe_.wait_ge(s.qT_act, n.count(3, 1))
                for a in range(2):
                    last = pe_.transpose(tt[0][:, a * P:(a + 1) * P], ks[:, a, :], id16[:, :])
                last.then_inc(s.qT_made, 1)

            def out_projection(p):
                pe_.wait_ge(s.hi_o, p.count(1, 1))
                for a in range(2):
                    if a:
                        pe_.wait_ge(s.lo_o, p.count(1, 1))
                    for hp in range(H // 2):
                        last = pe_.transpose(ot[a][:, hp * P:(hp + 1) * P], os_[:, a, hp * P:(hp + 1) * P], id16[:, :])
                    last.then_inc(s.oT_made, 1)
                pe_.wait_ge(s.oT_act, p.count(1, 1))
                pe_.wait_ge(s.oT_dve, p.count(1, 1))
                split_product(t_ps[:, 0, 0:D], lambda a, k: oT[:, a, k, :], lambda b, k: wout[:, b, k, :],
                              list(range(H // 2))).then_inc(s.proj_made, 1)

            def scores(t, u, par):
                i, G = t.i, GROUP[t.i]
                L = (i + 1) * P
                for g in range(G):
                    base = 1024 * par + s_off(i, g)
                    flat = s_ps[:, :, :].rearrange("p a n -> p (a n)")
                    for c0 in range(0, L, 512):
                        c1 = min(L, c0 + 512)
                        o = flat[:, base + c0:base + c1]
                        for a, b in ((0, 0), (0, 1), (1, 0)):
                            stop = a == 1 and c1 < L
                            last = mm(o, qT[:, t.off % 2, a, ds((u * G + g) * P, P)], kT[:, b, c0:c1], a + b == 0, stop)
                    last = mm(flat[:, base + L - P:base + L], idbf[:, :], maskbf[:, :], False, True)
                last.then_inc(s.s_made, 1)

            def attention(t):
                n, p = t.at(1), t.at(-1)
                i, G = t.i, GROUP[t.i]
                L = (i + 1) * P
                pairs = rank_pairs(i)
                pe_.wait_ge(s.qT_act, t.count(3, 3))
                pe_.wait_ge(s.qT_dve, t.count(2, 2))
                pe_.wait_ge(s.ckv_ready, t.count(1, 1))
                if n.exists():
                    pe_.wait_ge(s.pe_ready, n.count(1, 1))
                    pe_.wait_ge(s.lo_q, n.count(3, 3))
                if p.exists():
                    pe_.wait_ge(s.x1_done, p.count(1, 1))
                if t.at(-2).exists():
                    pe_.wait_ge(s.slot_done, t.at(-2).count(1, 1))
                scores(t, 0, 0)
                scores(t, 1, 1)

                def unit(u, par, more):
                    pe_.wait_ge(s.exp_done, t.units(1, u, 1))
                    for g in range(2):
                        for c, (hg, j) in enumerate(pairs[4 * g:4 * g + 4]):
                            last = pe_.transpose(t_ps[:, g, c * P:(c + 1) * P],
                                                 probs[:, hg * L + j * P:hg * L + (j + 1) * P], id32[:, :])
                        last.then_inc(s.p_made, 1)
                    if more:
                        scores(t, u + 2, par)
                    for g in range(2):
                        pe_.wait_ge(s.lo_p, t.units(2, u, g + 1))
                        for c, (hg, j) in enumerate(pairs[4 * g:4 * g + 4]):
                            o = o_flat[:, ds((u * G + hg) * C, C)]
                            for a, b in ((0, 0), (0, 1), (1, 0)):
                                last = mm(o, pT[:, a, g, c * P:(c + 1) * P], ckv[:, b, j, :],
                                          j == 0 and a + b == 0, j == i and a == 1)
                    if not more and par:
                        last.then_inc(s.o_made, 1)
                att_loop(pe_, t, unit)

            def shared_up(p):
                if p.at(2).exists():
                    pe_.wait_ge(s.qT_act, p.at(2).count(3, 3))
                    pe_.wait_ge(s.qT_dve, p.at(2).count(2, 2))
                pe_.wait_ge(s.ln2_done, p.count(3, 3))
                for a in range(2):
                    for k in range(KD):
                        last = pe_.transpose(tt[0][:, (2 * a + k) * P:(2 * a + k + 1) * P],
                                             xs2[:, p.off % 2, 0, a * D + k * P:a * D + (k + 1) * P], id16[:, :])
                last.then_inc(s.x2T_made, 1)
                pe_.wait_ge(s.x2T_ready, p.count(1, 1))
                for g in range(2):
                    last = split_product(s_ps[:, g, 0:SI], lambda a, k: x2T[:, a, k, :],
                                         lambda b, k: wsg_sb[:, b, k, g * SI:(g + 1) * SI], list(range(KD)))
                last.then_inc(s.gu_made, 1)
                split_product(t_ps[:, 1, 0:E], lambda a, k: x2T[:, a, k, :], lambda b, k: wr_sb[:, b, k, :],
                              list(range(KD))).then_inc(s.lgt_made, 1)

            def shared_down(q):
                pe_.wait_ge(s.mask_ready, q.count(1, 1))
                if q.at(3).exists():
                    pe_.wait_ge(s.pe_ready, q.at(3).count(1, 1))
                    pe_.wait_ge(s.lo_q, q.at(3).count(3, 1))
                mm(t_ps[:, 1, 0:E], tri16[:, :], picked[:, q.off % 2, :], True, True)
                mm(t_ps[:, 1, E:2 * E], ones16[:, :], picked[:, q.off % 2, :], True, True)
                pe_.wait_ge(s.hi_h, q.count(1, 1))
                pe_.wait_ge(s.lo_h, q.count(1, 1))
                for a in range(2):
                    for k in range(3):
                        w = min(P, SI - k * P)
                        last = pe_.transpose(tt[0][0:w, (3 * a + k) * P:(3 * a + k + 1) * P],
                                             hs[:, a, k * P:k * P + w], id16[:, :])
                last.then_inc(s.hT_made, 1)
                pe_.wait_ge(s.hT_ready, q.count(2, 2))

                def rows(k):
                    return min(P, SI - k * P)
                split_product(t_ps[:, 1, D:2 * D], lambda a, k: hT[0:rows(k), a, k, :],
                              lambda b, k: wsd_sb[0:rows(k), b, k, :], list(range(3))).then_inc(s.down_made, 1)

            pe_.wait_ge(s.c_ready, 1)
            pe_.wait_ge(s.lo_made, len(SPLITS))
            x_transposes(Tile(0))
            projections(Tile(0))
            q_transposes(Tile(0))

            def section(t):
                n = t.at(1)
                if n.exists():
                    x_transposes(n)
                    projections(n)
                if t.at(-2).exists():
                    shared_down(t.at(-2))
                if t.at(-1).exists():
                    out_projection(t.at(-1))
                if t.exists():
                    attention(t)
                if n.exists():
                    q_transposes(n)
                if t.at(-1).exists():
                    shared_up(t.at(-1))
            sections(pe_, section)

            pe_.wait_ge(s.gu_lo, 1)
            pe_.wait_ge(s.tab_ready, 1)

            def xg_transposes(n, q, par, m):
                pe_.wait_ge(xg_in[q], m * 16 + 16)
                for a in range(2):
                    for k in range(KD):
                        last = pe_.transpose(tt[par][:, (2 * a + k) * P:(2 * a + k + 1) * P],
                                             xg[:, q, a * D + k * P:a * D + (k + 1) * P], id16[:, :])
                last.then_inc(s.m_xT, 1)

            def expert_up(n, par):
                e = pe_.value_load(tab[0:1, 1, ds(n, 1)], min_val=0, max_val=E - 1)
                pe_.wait_ge(s.m_xTs, n + 1)
                for g in range(2):
                    last = split_product(s_ps[:, 2 * par + g, 0:I_E], lambda a, k: xgT[:, par, a, k, :],
                                         lambda b, k: wgu_sb[:, k, ds(e, 1), b, g * I_E:(g + 1) * I_E], list(range(KD)))
                last.then_inc(s.m_gu, 1)

            def h_transposes(n, par):
                pe_.wait_ge(s.m_hi, n + 1)
                pe_.wait_ge(s.m_lo, n + 1)
                for a in range(2):
                    for k in range(2):
                        last = pe_.transpose(ot[0][0:KE, (2 * a + k) * P:(2 * a + k + 1) * P],
                                             m_hs[:, par, a, k * KE:(k + 1) * KE], id16[:, :])
                last.then_inc(s.m_hT, 1)

            def expert_down(n):
                e = pe_.value_load(tab[0:1, 1, ds(n, 1)], min_val=0, max_val=E - 1)
                pe_.wait_ge(s.m_hTs, n + 1)
                pe_.wait_ge(s.m_y, n + 1)
                split_product(o_ps[:, 1, 0:D], lambda a, k: m_hT_sb[:, a, k, :],
                              lambda b, k: wd_sb[0:KE, k, ds(e, 1), b, :], list(range(2))).then_inc(s.m_down, 1)

            xg_transposes(0, 0, 0, 0)
            xg_transposes(1, 1, 1, 0)
            expert_up(0, 0)
            xg_transposes(2, 2, 0, 0)
            expert_up(1, 1)
            xg_transposes(3, 3, 1, 0)
            with pe_.Fori(0, NMT // XB - 1) as m:
                for q in range(XB):
                    n = m * XB + q
                    h_transposes(n, q % 2)
                    expert_up(n + 2, q % 2)
                    xg_transposes(n + 4, (q + 4) % XB, q % 2, m + (q + 4) // XB)
                    expert_down(n)
            for n in range(NMT - XB, NMT):
                h_transposes(n, n % 2)
                if n + 2 < NMT:
                    expert_up(n + 2, n % 2)
                if n + 4 < NMT:
                    xg_transposes(n + 4, (n + 4) % XB, n % 2, (n + 4) // XB)
                expert_down(n)

        @block.scalar
        def _(act):
            def copy(o, i):
                return act.copy(o, i)

            act.wait_ge(s.qb_made, 1)
            copy(r_qb[:, 0, :], o_flat)
            copy(r_qb[0:QLB, 1, :], t_ps[0:QLB, :, :].rearrange("p a n -> p (a n)")).then_inc(s.qb_copied, 1)
            for m in range(KD):
                for c in range(NQ // 512):
                    act.wait_ge(s.wq_made, m * 4 + c + 1)
                    copy(r_wq[:, m, c * 512:(c + 1) * 512], s_ps[:, c, :]).then_inc(s.wq_copied, 1)
            for hp in range(H // 2):
                act.wait_ge(s.wo_made, hp + 1)
                copy(r_out[:, hp, :], (o_ps if hp % 4 < 2 else t_ps)[:, hp % 2, 0:D]).then_inc(s.wo_copied, 1)
            act.wait_ge(s.scales, 1)
            for raw, hi, lo, rows, col in SPLITS:
                act.activation(hi[0:rows], raw[0:rows], ACT.Copy, scale=winv[0:rows, col:col + 1]).then_inc(s.hi_made, 1)

            def x_copy(n):
                act.wait_ge(s.xT_made, n.count(1, 1))
                copy(xT[:, :, :, :].rearrange("p a k n -> p (a k n)"), tt[0][:, 0:4 * P]).then_inc(s.xT_ready, 1)

            def q_copies(n):
                act.wait_ge(s.q_made, n.count(5, 1))
                copy(pe[:, H, :], t_ps[:, 1, C:2 * C])
                copy(ks[:, 0, 0:C], t_ps[:, 1, 0:C]).then_inc(s.hi_q, 1)
                for g in range(2):
                    act.wait_ge(s.q_made, n.count(5, 2 + g))
                    last = copy(pe[:, 8 * g:8 * g + 8, :], s_ps[:, 2 + g, :].rearrange("p (h r) -> p h r", r=ROPE))
                last.then_inc(s.pe_ready, 1)
                for g in range(2):
                    act.wait_ge(s.q_made, n.count(5, 4 + g))
                    copy(qs[:, 0, 8 * g:8 * g + 8, 0:NOPE],
                         s_ps[:, g, :].rearrange("p (h r) -> p h r", r=NOPE)).then_inc(s.hi_q, 1)

            def rope_hi(n):
                act.wait_ge(s.rope_done, n.count(1, 1))
                copy(ks[:, 0, C:HD], rot[:, H, :])
                copy(qs[:, 0, :, NOPE:HD], rot[:, 0:H, :]).then_inc(s.hi_rope, 1)

            def qT_copies(n):
                par = n.off % 2
                act.wait_ge(s.qT_made, n.count(5, 1))
                copy(qT[:, par, 0, 0:1024], tt[0]).then_inc(s.qT_act, 1)
                act.wait_ge(s.qT_made, n.count(5, 3))
                copy(qT[:, par, 1, 0:1024], st[2]).then_inc(s.qT_act, 1)
                act.wait_ge(s.qT_made, n.count(5, 5))
                copy(kT[:, :, n.i * P:(n.i + 1) * P], tt[0][:, 0:2 * P].rearrange("p (a n) -> p a n", a=2)).then_inc(s.qT_act, 1)

            def out_hi(p):
                act.wait_ge(s.o_ready, p.count(1, 1))
                copy(os_[:, 0, :], o_sb[:, :]).then_inc(s.hi_o, 1)

            def oT_copy(p):
                act.wait_ge(s.oT_made, p.count(2, 1))
                copy(oT[:, 0, :, :].rearrange("p k n -> p (k n)"), ot[0]).then_inc(s.oT_act, 1)

            def attention(t):
                i, G = t.i, GROUP[t.i]
                L = (i + 1) * P
                n_p = len(rank_pairs(i))
                flat = s_ps[:, :, :].rearrange("p a n -> p (a n)")

                def exps(u, par):
                    act.wait_ge(s.max_ready, t.units(1, u, 1))
                    for g in range(G):
                        base = 1024 * par + s_off(i, g)
                        last = act.activation(probs[:, g * L:(g + 1) * L], flat[:, base:base + L], ACT.Exp,
                                              bias=nmax[:, par, g:g + 1], scale=f_att,
                                              accum_out=ssum[:, t.off % 2, ds(u * G + g, 1)])
                    last.then_inc(s.exp_done, 1)

                def unit(u, par, more):
                    for g in range(2):
                        w = P * min(4, n_p - 4 * g)
                        act.wait_ge(s.p_made, t.units(2, u, g + 1))
                        copy(pT[:, 0, g, 0:w], t_ps[:, g, 0:w]).then_inc(s.hi_p, 1)
                    if more or par == 0:
                        exps(u + 1, 1 - par)
                exps(0, 0)
                att_loop(act, t, unit)

            def shared_act(p):
                act.wait_ge(s.x2T_made, p.count(1, 1))
                copy(x2T[:, :, :, :].rearrange("p a k n -> p (a k n)"), tt[0][:, 0:4 * P]).then_inc(s.x2T_ready, 1)
                act.wait_ge(s.gu_made, p.count(1, 1))
                act.activation(gate[:, :], s_ps[:, 0, 0:SI], ACT.Tanh, scale=f_sgh).then_inc(s.gate_done, 1)
                act.wait_ge(s.hid_done, p.count(1, 1))
                copy(hs[:, 0, :], hid[:, :]).then_inc(s.hi_h, 1)

            def hT_copy(q):
                act.wait_ge(s.hT_made, q.count(1, 1))
                w = SI - 2 * P
                src = tt[0][:, 0:6 * P].rearrange("p (a k n) -> p a k n", a=2, k=3)
                copy(hT[:, :, 0:2, :], src[:, :, 0:2, :]).then_inc(s.hT_ready, 1)
                copy(hT[0:w, :, 2, :], src[0:w, :, 2, :]).then_inc(s.hT_ready, 1)

            act.wait_ge(s.lo_made, len(SPLITS))
            x_copy(Tile(0))
            q_copies(Tile(0))
            rope_hi(Tile(0))
            qT_copies(Tile(0))

            def section(t):
                n = t.at(1)
                if n.exists():
                    x_copy(n)
                if t.at(-1).exists():
                    out_hi(t.at(-1))
                if n.exists():
                    q_copies(n)
                if t.at(-2).exists():
                    hT_copy(t.at(-2))
                if t.at(-1).exists():
                    oT_copy(t.at(-1))
                if t.exists():
                    attention(t)
                if n.exists():
                    rope_hi(n)
                    qT_copies(n)
                if t.at(-1).exists():
                    shared_act(t.at(-1))
            sections(act, section)

            act.wait_ge(s.gu_scale, 1)
            for k in range(KD):
                with act.Fori(0, E // GC) as m:
                    act.wait_ge(s.gu_hi, m + (1 + k * (E // GC)))
                    act.activation(gu_w, gu_raw[:, k, ds(m * GC, GC), :], ACT.Copy, scale=winv[:, A_GU:A_GU + 1])
                    act.activation(d_w[0:KE], d_raw[0:KE, k, ds(m * GC, GC), :], ACT.Copy,
                                   scale=winv[0:KE, A_D:A_D + 1]).then_inc(s.gu_prep, 1)
            act.wait_ge(s.c_w, 1)
            act.activation(w_e[:, :, :].rearrange("p t e -> p (t e)"), w_d[:, :, :].rearrange("p t e -> p (t e)"),
                           ACT.Exp).then_inc(s.w_exp, 1)
            act.activation(w_t[:, :], w_t[:, :], ACT.Exp).then_inc(s.w_exp, 1)

            def xg_copy(n, par):
                act.wait_ge(s.m_xT, n + 1)
                copy(xgT[:, par, :, :, :].rearrange("p a k n -> p (a k n)"), tt[par][:, 0:4 * P]).then_inc(s.m_xTs, 1)

            def expert_gate(n, par):
                act.wait_ge(s.m_gu, n + 1)
                act.activation(m_g[:, :], s_ps[:, 2 * par, 0:I_E], ACT.Tanh, scale=f_guh).then_inc(s.m_gate, 1)
                act.wait_ge(s.m_hid, n + 1)
                copy(m_hs[:, par, 0, :], m_h[:, par, :]).then_inc(s.m_hi, 1)

            def y_copy(n, q, m):
                act.wait_ge(s.m_down, n + 1)
                if not (isinstance(m, int) and n < YB):
                    act.wait_ge(m_out[(q + YB) % XB], m * 16 + (0 if q < YB else 16))
                act.activation(m_ys[:, q % YB, :], o_ps[:, 1, 0:D], ACT.Copy, scale=f_ed).then_inc(s.m_y, 1)

            xg_copy(0, 0)
            xg_copy(1, 1)
            expert_gate(0, 0)
            xg_copy(2, 0)
            expert_gate(1, 1)
            xg_copy(3, 1)

            def expert_round(m, q, n):
                last = isinstance(n, int)
                if not last or n + 2 < NMT:
                    expert_gate(n + 2, q % 2)
                if not last or n + 4 < NMT:
                    xg_copy(n + 4, q % 2)
                y_copy(n, q, m)
            for q in range(XB):
                expert_round(0, q, q)
            with act.Fori(1, NMT // XB - 1) as m:
                for q in range(XB):
                    expert_round(m, q, m * XB + q)
            for q in range(XB):
                expert_round(NMT // XB - 1, q, NMT - XB + q)

            NC = NT // CT
            with act.Fori(0, NC // 2) as m:
                for q in range(2):
                    act.wait_ge(s.c_sum, m * 2 + q + 3)
                    first = m * (2 * CT * P) + q * CT * P
                    act.dma_start(out[ds(first, CT * P), :].rearrange("(c p) n -> p c n", p=P),
                                  c_o[:, q]).then_inc(c_out[q], 16)
            for q in range(2):
                act.wait_ge(c_out[q], 16 * (NC // 2 + 1))

        @block.vector
        def _(dve):
            def link(ins):
                link.n += 1
                ins.then_inc(s.prep, 1)
                dve.wait_ge(s.prep, link.n)
            link.n = 0

            def at(per, k):
                return k

            dve.wait_ge(s.c_in, 16 * 9)
            dve.tensor_copy(id16[:, :], id32[:, :])
            dve.tensor_copy(idbf[:, :], id32[:, :])
            dve.tensor_copy(maskbf[:, :], mask32[:, :])
            dve.tensor_copy(tri16[:, :], probs[:, 0:P])
            dve.memset(ones16[:, :], 1.0)
            dve.memset(ones_e[:, :], 1.0)
            dve.memset(amax[:, :], 0.0)
            link(dve.memset(amax_gu[:, :], 0.0))
            dve.tensor_scalar(used[:, :], iota_e_sb[:, :], float(LIST), None, ALU.mult)
            dve.memset(lg_all[:, :, :], 0.0).then_inc(s.c_ready, 1)
            for q in range(2):
                dve.sem_inc(c_out[q], 16)
            dve.sem_inc(s.m_y, 1)
            dve.sem_inc(s.c_sum, 2)
            dve.sem_inc(s.gu_hi, 1)

            dve.wait_ge(s.w_b, 16 * 5)
            dve.wait_ge(s.wq_copied, 8)
            dve.wait_ge(s.wo_copied, 8)
            for raw, rows, col in ((r_wq[:, :, 0:NQ], P, A_Q), (r_wq[:, :, NQ:], P, A_KV), (r_out, P, A_O),
                                   (r_wsg, P, A_SG), (r_wr, P, A_R)):
                link(dve.tensor_reduce(amax[0:rows, col:col + 1], raw.rearrange("p k n -> p (k n)") if col != A_Q and col != A_KV else raw,
                                       mybir.AxisListType.XY if col in (A_Q, A_KV) else AX_X, ALU.max, apply_absolute_value=True))
            link(dve.memset(r_wsd[SI - 2 * P:P, 2, :], 0.0))
            link(dve.tensor_reduce(amax[:, A_SD:A_SD + 1], r_wsd.rearrange("p k n -> p (k n)"), AX_X, ALU.max,
                                   apply_absolute_value=True))
            dve.sem_inc(s.amax_ready, 1)

            def scales(cols):
                link(dve.tensor_scalar(amax_all[:, cols], amax_all[:, cols], 1e-30, None, ALU.max))
                link(dve.tensor_scalar(wamp[:, cols], amax_all[:, cols], 1.0 / WMAX, None, ALU.mult))
                link(dve.reciprocal(winv[:, cols], wamp[:, cols]))

            dve.wait_ge(s.amax_reduced, 1)
            scales(slice(0, 6))
            link(dve.tensor_scalar(f_att, wamp[:, A_Q:A_Q + 1], wamp[:, A_KV:A_KV + 1], HD ** -0.5, ALU.mult, ALU.mult))
            dve.tensor_scalar(f_natt, f_att, -1.0, None, ALU.mult)
            dve.tensor_scalar(f_out, wamp[:, A_KV:A_KV + 1], wamp[:, A_O:A_O + 1], None, ALU.mult)
            dve.tensor_scalar(f_sgh, wamp[:, A_SG:A_SG + 1], 0.5, None, ALU.mult)
            link(dve.tensor_scalar(f_sd, wamp[:, A_SG:A_SG + 1], wamp[:, A_SG:A_SG + 1], 0.5 / HSCALE, ALU.mult, ALU.mult))
            link(dve.tensor_scalar(f_sd, f_sd, wamp[:, A_SD:A_SD + 1], None, ALU.mult))
            dve.sem_inc(s.scales, 1)
            for k, (raw, hi, lo, rows, col) in enumerate(SPLITS):
                dve.wait_ge(s.hi_made, k + 1)
                dve.scalar_tensor_tensor(lo[0:rows], raw[0:rows], winv[0:rows, col:col + 1], hi[0:rows],
                                         ALU.mult, ALU.subtract).then_inc(s.lo_made, 1)

            def layernorm(t, src, k, steps_sem, done, write):
                st_ = Steps(dve, steps_sem, LN_STEPS, t.count)
                w = ln_w[:, k, :]
                st_.do(dve.bn_stats(ln_st[:, k, 0:6], src), own_wait)
                st_.do(dve.bn_aggr(ln_mv[:, k, :], ln_st[:, k, 0:6]))
                var, y, u = w[:, 0:1], w[:, 1:2], w[:, 2:3]
                st_.do(dve.tensor_scalar(var, ln_mv[:, k, 1:2], EPS, None, ALU.add))
                st_.do(dve.tensor_scalar(ln_i[:, k, :], var.bitcast(I32), 1, None, ALU.arith_shift_right))
                st_.do(dve.tensor_scalar(y.bitcast(I32), ln_i[:, k, :], -1.0, SEED, ALU.mult, ALU.add))
                for _ in range(NEWTON):
                    st_.do(dve.scalar_tensor_tensor(u, y, var, y, ALU.mult, ALU.mult))
                    st_.do(dve.tensor_scalar(u, u, -0.5, 1.5, ALU.mult, ALU.add))
                    st_.do(dve.tensor_tensor(y, y, u, ALU.mult))
                st_.do(dve.tensor_scalar(xn[:, k, :], src, ln_mv[:, k, 0:1], y, ALU.subtract, ALU.mult))
                assert st_.n == LN_STEPS
                write(xn[:, k, :])

            def ln1(t):
                par = t.off % 2
                if t.at(-2).exists():
                    dve.wait_ge(s.xT_made, t.at(-2).count(1, 1))
                dve.wait_ge(xin[t.off % 4], 16 * (t.off // 4 + 1) if t.b is None else t.b * 32 + 16 * (t.off // 4 + 1))

                def write(v):
                    dve.tensor_copy(xs[:, par, 0, :], v).then_inc(s.ln1_done, 1)
                    dve.wait_ge(s.ln1_done, t.count(2, 1))
                    dve.tensor_tensor(xs[:, par, 1, :], v, xs[:, par, 0, :], ALU.subtract).then_inc(s.ln1_done, 1)
                layernorm(t, x_sb[:, t.off % 4, :], 0, s.ln1s, s.ln1_done, write)

            def q_lo(n):
                dve.wait_ge(s.hi_q, n.count(3, 1))
                dve.tensor_tensor(ks[:, 1, 0:C], t_ps[:, 1, 0:C], ks[:, 0, 0:C], ALU.subtract).then_inc(s.lo_q, 1)
                for g in range(2):
                    dve.wait_ge(s.hi_q, n.count(3, 2 + g))
                    hs_ = slice(8 * g, 8 * g + 8)
                    dve.tensor_tensor(qs[:, 1, hs_, 0:NOPE], s_ps[:, g, :].rearrange("p (h r) -> p h r", r=NOPE),
                                      qs[:, 0, hs_, 0:NOPE], ALU.subtract).then_inc(s.lo_q, 1)

            def qT_copies(n):
                par = n.off % 2
                if n.at(-1).exists():
                    dve.wait_ge(s.o_made, n.at(-1).count(1, 1))
                dve.wait_ge(s.lo_q, n.count(3, 3))
                dve.tensor_copy(ckv[:, :, n.i, :], ks[:, :, 0:C]).then_inc(s.ckv_ready, 1)
                dve.wait_ge(s.qT_made, n.count(5, 2))
                dve.tensor_copy(qT[:, par, 0, 1024:2048], tt[1]).then_inc(s.qT_dve, 1)
                dve.wait_ge(s.qT_made, n.count(5, 4))
                dve.tensor_copy(qT[:, par, 1, 1024:2048], st[3]).then_inc(s.qT_dve, 1)

            def out_norm(p):
                dve.wait_ge(s.o_made, p.count(1, 1))
                if p.at(-1).exists():
                    dve.wait_ge(s.lo_o, p.at(-1).count(1, 1))
                dve.reciprocal(rsum[:, :], ssum[:, p.off % 2, :]).then_inc(s.o_evs, 1)
                dve.wait_ge(s.o_evs, p.count(1, 1))
                dve.tensor_tensor(o_sb[:, :].rearrange("p (h c) -> p h c", c=C), o_flat.rearrange("p (h c) -> p h c", c=C),
                                  rsum[:, :].unsqueeze(2).broadcast_to([P, H, C]), ALU.mult).then_inc(s.o_ready, 1)

            def oT_copy(p):
                dve.wait_ge(s.oT_made, p.count(2, 2))
                dve.tensor_copy(oT[:, 1, :, :].rearrange("p k n -> p (k n)"), ot[1]).then_inc(s.oT_dve, 1)

            def residual(p):
                dve.wait_ge(s.proj_made, p.count(1, 1))
                dve.scalar_tensor_tensor(x1[:, p.off % 2, :], t_ps[:, 0, 0:D], f_out, x_sb[:, p.off % 4, :],
                                         ALU.mult, ALU.add).then_inc(s.x1_done, 1)

            def attention(t):
                i, G = t.i, GROUP[t.i]
                L = (i + 1) * P
                n_p = len(rank_pairs(i))
                flat = s_ps[:, :, :].rearrange("p a n -> p (a n)")

                def maxima(u, par):
                    dve.wait_ge(s.s_made, t.units(1, u, 1))
                    w = s_off(i, 1) if G > 1 else L
                    view = flat[:, 1024 * par:1024 * par + G * w].rearrange("p (g n) -> p g n", g=G)[:, :, 0:L]
                    dve.tensor_reduce(smax[:, par, 0:G], view, AX_X, ALU.max).then_inc(s.maxs, 1)
                    dve.wait_ge(s.maxs, t.units(1, u, 1))
                    dve.tensor_scalar(nmax[:, par, 0:G], smax[:, par, 0:G], f_natt, None, ALU.mult).then_inc(s.max_ready, 1)

                def unit(u, par, more):
                    for g in range(2):
                        w = P * min(4, n_p - 4 * g)
                        dve.wait_ge(s.hi_p, t.units(2, u, g + 1))
                        dve.tensor_tensor(pT[:, 1, g, 0:w], t_ps[:, g, 0:w], pT[:, 0, g, 0:w],
                                          ALU.subtract).then_inc(s.lo_p, 1)
                    if more:
                        maxima(u + 2, par)
                maxima(0, 0)
                maxima(1, 1)
                att_loop(dve, t, unit)

            def ln2(p):
                par = p.off % 2
                if p.at(-2).exists():
                    dve.wait_ge(scattered[par], p.at(-2).pair(32))

                def write(v):
                    k = p.count
                    row = xs2[:, par]
                    dve.tensor_copy(row[:, 0, 0:D], v).then_inc(s.ln2_done, 1)
                    dve.wait_ge(s.ln2_done, k(3, 1))
                    dve.tensor_tensor(row[:, 0, D:2 * D], v, row[:, 0, 0:D], ALU.subtract).then_inc(s.ln2_done, 1)
                    dve.wait_ge(s.ln2_done, k(3, 2))
                    dve.tensor_copy(row[:, 1, 0:2 * D], row[:, 0, 0:2 * D])
                    dve.tensor_copy(row[:, :, 2 * D:ROW].bitcast(I32).rearrange("p k o -> p (k o)"), dest_f[:, :]).then_inc(s.ln2_done, 1)
                    dve.wait_ge(s.ln2_done, k(3, 3))
                    dve.tensor_scalar(dest_f[:, :], dest_f[:, :], float(P), None, ALU.add)
                dve.wait_ge(s.x1_done, p.count(1, 1))
                layernorm(p, x1[:, par, :], 1, s.ln2s, s.ln2_done, write)

            def hidden(p):
                dve.wait_ge(s.gate_done, p.count(1, 1))
                dve.scalar_tensor_tensor(hid[:, :], gate[:, :], 1.0, s_ps[:, 0, 0:SI], ALU.add, ALU.mult).then_inc(s.hids, 1)
                dve.wait_ge(s.hids, p.count(1, 1))
                dve.scalar_tensor_tensor(hid[:, :], hid[:, :], HSCALE, s_ps[:, 1, 0:SI], ALU.mult, ALU.mult).then_inc(s.hid_done, 1)
                dve.wait_ge(s.hi_h, p.count(1, 1))
                dve.tensor_tensor(hs[:, 1, :], hid[:, :], hs[:, 0, :], ALU.subtract).then_inc(s.lo_h, 1)

            def tile_at(ap, p):
                return ap[:, ds(p.off if p.b is None else p.b * TB + p.off, 1), :].rearrange("p a n -> p (a n)")

            def router(p):
                par = p.off % 2
                st_ = Steps(dve, s.route_s, 6, p.count)
                lg_t, top_t = lg[:, par, :], top8[:, par, :]
                dve.wait_ge(s.lgt_made, p.count(1, 1))
                st_.do(dve.tensor_scalar(lg_t, t_ps[:, 1, 0:E], wamp[:, A_R:A_R + 1], None, ALU.mult), own_wait)
                st_.do(dve.max(top_t, lg_t), own_wait)
                st_.do(dve.max_index(top_ix[:, par, :], top_t, lg_t))
                dve.tensor_copy(tile_at(lg_all, p), lg_t)
                dve.tensor_copy(tile_at(top_all, p), top_t[:, 0:TOPK])
                st_.do(dve.tensor_copy(ixf[:, :], top_ix[:, par, 0:2]))
                for k in range(TOPK):
                    st_.do(dve.tensor_scalar(pick[:, par, k, :], iota_e_sb[:, :], ixf[:, k:k + 1], None, ALU.is_equal))
                dve.tensor_tensor(picked[:, par, :], pick[:, par, 0, :], pick[:, par, 1, :], ALU.add).then_inc(s.mask_ready, 1)

            def slots(q):
                par = q.off % 2
                dve.wait_ge(s.down_made, q.count(1, 1))
                if q.at(-2).exists():
                    dve.wait_ge(stored[par], q.at(-2).pair(16))
                dve.scalar_tensor_tensor(den[:, par, :], t_ps[:, 1, D:2 * D], f_sd, x1[:, par, :], ALU.mult, ALU.add).then_inc(s.dense_done, 1)
                st_ = Steps(dve, s.slot_s, 5, q.count)
                st_.do(dve.tensor_tensor(place[:, :], t_ps[:, 1, 0:E], used[:, :], ALU.add))
                st_.do(dve.tensor_tensor(used[:, :], used[:, :], t_ps[:, 1, E:2 * E], ALU.add))
                for k in range(TOPK):
                    st_.do(dve.tensor_tensor_reduce(place_k[:, :], pick[:, par, k, :], place[:, :], 1.0, 0.0, ALU.mult, ALU.add,
                                                    slot_f[:, k:k + 1]))
                if q.at(-2).exists():
                    dve.wait_ge(scattered[par], q.at(-2).pair(32))
                st_.do(dve.tensor_copy(slot[:, par, :], slot_f[:, :]))
                dve.sem_inc(s.slot_done, 1)

            ln1(Tile(0))
            ln1(Tile(1))
            q_lo(Tile(0))
            qT_copies(Tile(0))

            def section(t):
                n = t.at(1)
                if t.at(-1).exists():
                    out_norm(t.at(-1))
                if n.exists():
                    q_lo(n)
                if t.at(-2).exists():
                    slots(t.at(-2))
                if t.at(-1).exists():
                    oT_copy(t.at(-1))
                    residual(t.at(-1))
                if t.exists():
                    attention(t)
                if t.at(-1).exists():
                    ln2(t.at(-1))
                if n.exists():
                    qT_copies(n)
                if t.at(-1).exists():
                    hidden(t.at(-1))
                    router(t.at(-1))
                if t.at(2).exists():
                    ln1(t.at(2))
            sections(dve, section)

            dve.memset(pad[:, 0:2 * D], 0.0)
            dve.memset(pad[:, 2 * D:ROW].bitcast(I32), 2 * NY)
            dve.tensor_copy(free_i[:, :], used[0:1, :]).then_inc(s.used_ready, 1)
            st_ = Steps(dve, s.tail_s, 15, at)
            st_.do(dve.tensor_scalar(cnt[:, :], iota_e_sb[:, :], -float(LIST), None, ALU.mult))
            st_.do(dve.tensor_tensor(cnt[:, :], cnt[:, :], used[:, :], ALU.add))
            st_.do(dve.tensor_tensor(cmp_k[:, :, :], cnt[:, :].unsqueeze(2).broadcast_to([P, E, NT]), iota_k_sb[:, :, :], ALU.is_gt))
            st_.do(dve.tensor_reduce(tiles_e[:, :], cmp_k[:, :, :], AX_X, ALU.add))
            st_.do(dve.tensor_tensor_scan(ends[:, :], ones_e[:, :], tiles_e[:, :], 0.0, ALU.mult, ALU.add))
            st_.do(dve.tensor_scalar(jump[:, :], tiles_e[:, :], -float(P), float(LIST), ALU.mult, ALU.add))
            st_.do(dve.tensor_tensor(ge[:, :, :], iota_n_sb[:, :].unsqueeze(2).broadcast_to([1, NMT, E]),
                                     ends[0:1, :].unsqueeze(1).broadcast_to([1, NMT, E]), ALU.is_ge))
            st_.do(dve.tensor_reduce(t_exp[:, :], ge[:, :, :], AX_X, ALU.add))
            st_.do(dve.tensor_tensor(ge2[:, :, :], ge[:, :, :], jump[0:1, :].unsqueeze(1).broadcast_to([1, NMT, E]), ALU.mult))
            st_.do(dve.tensor_reduce(t_row[:, :], ge2[:, :, :], AX_X, ALU.add))
            st_.do(dve.scalar_tensor_tensor(t_row[:, :], iota_n_sb[:, :], float(P), t_row[:, :], ALU.mult, ALU.add))
            st_.do(dve.tensor_scalar(t_row[:, :], t_row[:, :], float(DUMMY), None, ALU.min))
            st_.do(dve.tensor_scalar(t_exp[:, :], t_exp[:, :], float(E - 1), None, ALU.min))
            st_.do(dve.tensor_copy(tab[:, 0, :], t_row[:, :]))
            st_.do(dve.tensor_copy(tab[:, 1, :], t_exp[:, :]))
            dve.sem_inc(s.tab_ready, 1)

            dve.wait_ge(s.w_gu, 32)
            dve.wait_ge(s.w_d, 32)
            dve.wait_ge(s.c_ready, 1)
            link(dve.tensor_reduce(amax[:, A_GU:A_GU + 1], ga, AX_X, ALU.max, apply_absolute_value=True))
            link(dve.tensor_reduce(amax[0:KE, A_D:A_D + 1], gb[0:KE], AX_X, ALU.max, apply_absolute_value=True))
            dve.sem_inc(s.gu_amax, 1)
            dve.wait_ge(s.gu_red, 1)
            scales(slice(6, 8))
            dve.tensor_scalar(f_guh, wamp[:, A_GU:A_GU + 1], 0.5, None, ALU.mult)
            link(dve.tensor_scalar(f_ed, wamp[:, A_GU:A_GU + 1], wamp[:, A_GU:A_GU + 1], 0.5 / HSCALE, ALU.mult, ALU.mult))
            link(dve.tensor_scalar(f_ed, f_ed, wamp[:, A_D:A_D + 1], None, ALU.mult))
            dve.sem_inc(s.gu_scale, 1)
            NG = E // GC
            for k in range(KD):
                with dve.Fori(0, NG) as m:
                    dve.wait_ge(s.gu_prep, m + (1 + k * NG))
                    dve.tensor_copy(wgu_sb[:, k, ds(m * GC, GC), 0, :], gu_w).then_inc(s.gu_amax, 1)
                    dve.tensor_copy(wd_sb[0:KE, k, ds(m * GC, GC), 0, :], d_w[0:KE]).then_inc(s.gu_amax, 1)
                    dve.wait_ge(s.gu_amax, m * 2 + (3 + k * 2 * NG))
                    dve.tensor_tensor(wgu_sb[:, k, ds(m * GC, GC), 1, :], gu_w, wgu_sb[:, k, ds(m * GC, GC), 0, :], ALU.subtract)
                    dve.tensor_tensor(wd_sb[0:KE, k, ds(m * GC, GC), 1, :], d_w[0:KE],
                                      wd_sb[0:KE, k, ds(m * GC, GC), 0, :], ALU.subtract).then_inc(s.gu_hi, 1)
            dve.wait_ge(s.gu_hi, 1 + KD * NG)
            dve.sem_inc(s.gu_lo, 1)

            link(dve.tensor_tensor(w_d[:, :, :], lg_all[:, :, :], top_all[:, :, 0:1].broadcast_to([P, NT, E]), ALU.subtract))
            link(dve.tensor_tensor(w_t[:, :], top_all[:, :, 1], top_all[:, :, 0], ALU.subtract))
            dve.sem_inc(s.c_w, 1)

            def expert_hidden(n, par):
                dve.wait_ge(s.m_gate, n + 1)
                dve.scalar_tensor_tensor(m_m[:, :], m_g[:, :], 1.0, s_ps[:, 2 * par, 0:I_E], ALU.add, ALU.mult).then_inc(s.m_q, 1)
                dve.wait_ge(s.m_q, n + 1)
                dve.scalar_tensor_tensor(m_h[:, par, :], m_m[:, :], HSCALE, s_ps[:, 2 * par + 1, 0:I_E], ALU.mult,
                                         ALU.mult).then_inc(s.m_hid, 1)
                dve.wait_ge(s.m_hi, n + 1)
                dve.tensor_tensor(m_hs[:, par, 1, :], m_h[:, par, :], m_hs[:, par, 0, :], ALU.subtract).then_inc(s.m_lo, 1)

            def hT_copy(n):
                dve.wait_ge(s.m_hT, n + 1)
                dve.tensor_copy(m_hT_sb[:, :, :, :].rearrange("p a k n -> p (a k n)"), ot[0][0:KE, 0:4 * P]).then_inc(s.m_hTs, 1)

            expert_hidden(0, 0)
            expert_hidden(1, 1)
            with dve.Fori(0, NMT // XB - 1) as m:
                for q in range(XB):
                    n = m * XB + q
                    hT_copy(n)
                    expert_hidden(n + 2, q % 2)
            for n in range(NMT - XB, NMT):
                hT_copy(n)
                if n + 2 < NMT:
                    expert_hidden(n + 2, n % 2)

            dve.wait_ge(s.w_exp, 2)
            link(dve.tensor_reduce(w_s[:, :], w_e[:, :, :], AX_X, ALU.add))
            link(dve.reciprocal(w_k[:, :, 0], w_s[:, :]))
            link(dve.tensor_tensor(w_k[:, :, 1], w_k[:, :, 0], w_t[:, :], ALU.mult))

            NC = NT // CT
            with dve.Fori(0, NC // 2) as m:
                for q in range(2):
                    dve.wait_ge(c_loaded[q], m * 48 + 48)
                    dve.wait_ge(c_out[q], m * 16 + 16)
                    for k in range(TOPK):
                        for c in range(CT):
                            w = w_k[:, ds(m * (2 * CT) + q * CT + c, 1), k]
                            last = dve.scalar_tensor_tensor(c_o[:, q, c, :], c_in[:, q, 1 + k, c, :], w,
                                                            c_in[:, q, 0, c, :] if k == 0 else c_o[:, q, c, :], ALU.mult, ALU.add)
                        if k == 0:
                            last.then_inc(s.c_y0, 1)
                            dve.wait_ge(s.c_y0, m * 2 + q + 1)
                    last.then_inc(s.c_sum, 1)

        @block.gpsimd
        def _(pool):
            pool.wait_ge(s.amax_ready, 1)
            pool.partition_all_reduce(amax_all[:, 0:6], amax[:, 0:6], P, bass.bass_isa.ReduceOp.max).then_inc(s.amax_reduced, 1)

            def rope(n):
                st_ = Steps(pool, s.rope_s, 3, n.count)
                cos_b = cos_sb[:, n.i, :].unsqueeze(1).broadcast_to([P, H + 1, ROPE])
                pool.wait_ge(s.pe_ready, n.count(1, 1))
                st_.do(pool.tensor_tensor(rot, pe, cos_b, ALU.mult))
                for k in range(2):
                    sin_b = sin_sb[:, n.i, k:ROPE:2].unsqueeze(1).broadcast_to([P, H + 1, ROPE // 2])
                    st_.do(pool.tensor_tensor(rot2[:, :, k:ROPE:2], pe[:, :, 1 - k:ROPE:2], sin_b, ALU.mult))
                pool.tensor_tensor(rot, rot, rot2, ALU.add).then_inc(s.rope_done, 1)

            def rope_lo(n):
                pool.wait_ge(s.hi_rope, n.count(1, 1))
                pool.tensor_tensor(ks[:, 1, C:HD], rot[:, H, :], ks[:, 0, C:HD], ALU.subtract)
                pool.tensor_tensor(qs[:, 1, :, NOPE:HD], rot[:, 0:H, :], qs[:, 0, :, NOPE:HD], ALU.subtract).then_inc(s.lo_rope, 1)

            def out_lo(p):
                pool.wait_ge(s.hi_o, p.count(1, 1))
                pool.tensor_tensor(os_[:, 1, :], o_sb[:, :], os_[:, 0, :], ALU.subtract).then_inc(s.lo_o, 1)

            def scatter(q):
                par = q.off % 2
                pool.wait_ge(s.slot_done, q.count(1, 1))
                own_wait(pool)
                for k in range(TOPK):
                    pool.indirect_dma_start(lists, bass.IndirectOffsetOnAxis(slot[:, par, k:k + 1], 0), xs2[:, par, k, :],
                                            None).then_inc(scattered[par], 16)

            rope(Tile(0))
            rope_lo(Tile(0))

            def section(t):
                n = t.at(1)
                if t.at(-1).exists():
                    out_lo(t.at(-1))
                if n.exists():
                    rope(n)
                if t.at(-2).exists():
                    scatter(t.at(-2))
                if n.exists():
                    rope_lo(n)
            sections(pool, section)

            pool.wait_ge(s.gu_amax, 1)
            pool.partition_all_reduce(amax_all[:, 6:8], amax[:, 6:8], P, bass.bass_isa.ReduceOp.max).then_inc(s.gu_red, 1)

            def send(n, q):
                pool.wait_ge(s.m_y, n + 2)
                own_wait(pool)
                pool.indirect_dma_start(y_exp, bass.IndirectOffsetOnAxis(xg[:, q, 2 * D:ROW].bitcast(I32), 0), m_ys[:, q % YB, :],
                                        None, bounds_check=NY - 1, oob_is_err=False).then_inc(m_out[q], 16)
            with pool.Fori(0, NMT // XB) as m:
                for q in range(XB):
                    send(m * XB + q, q)


def kernel(**inputs):
    import concourse.bacc as bacc
    from concourse import mybir as mb
    from concourse.bass_utils import run_bass_kernel_spmd

    g = {n: np.asarray(a) for n, a in inputs.items()}
    tr = lambda a, *ax: np.ascontiguousarray(np.transpose(a, ax))
    wqb = g["L0_attn_Wqb"].reshape(QL, H, HD)
    wkvb = g["L0_attn_Wkvb"].reshape(C, H, NOPE + VD)
    inv_freq = np.float32(1.0) / np.float32(10000.0) ** (np.arange(ROPE // 2, dtype=np.float32) * np.float32(2.0) / np.float32(ROPE))
    ang = np.arange(S, dtype=np.float32)[:, None] * inv_freq[None, :].astype(np.float32)
    cos = np.repeat(np.cos(ang), 2, axis=1).astype(np.float32)
    sin = np.stack([-np.sin(ang), np.sin(ang)], axis=-1).reshape(S, ROPE).astype(np.float32)
    q_at, k_at = np.arange(P)[:, None], np.arange(P)[None, :]
    arrays = {
        "x": np.ascontiguousarray(g["L0_attn_hidden_states"].reshape(NT * P, D)),
        "wqaT": tr(g["L0_attn_Wqa"], 1, 0),
        "wqb_peT": np.ascontiguousarray(wqb[:, :, NOPE:].reshape(QL, H * ROPE)),
        "wqb_nopeT": tr(wqb[:, :, :NOPE], 2, 1, 0),
        "wkva": np.ascontiguousarray(g["L0_attn_Wkva"]),
        "wkT": tr(wkvb[:, :, :NOPE], 2, 1, 0),
        "wvT": tr(wkvb[:, :, NOPE:], 2, 1, 0),
        "wo": np.ascontiguousarray(g["L0_attn_Wo"]),
        "gateT": tr(g["L0_ffn_gate_w"], 1, 0),
        "wgu": np.ascontiguousarray(g["L0_ffn_w_gate_up"]),
        "wd": np.ascontiguousarray(g["L0_ffn_w_down"]),
        "wsg": np.ascontiguousarray(g["L0_ffn_shared_gate_up"]),
        "wsd": np.ascontiguousarray(g["L0_ffn_shared_down"]),
        "cos_t": tr(cos.reshape(TB, P, ROPE), 1, 0, 2),
        "sin_t": tr(sin.reshape(TB, P, ROPE), 1, 0, 2),
        "ident": np.eye(P, dtype=np.float32),
        "causal": np.where(k_at > q_at, np.float32(-3e38), np.float32(0)).astype(np.float32),
        "tri": (q_at < k_at).astype(np.float32),
        "iota_e": np.tile(np.arange(E, dtype=np.float32), (P, 1)),
        "iota_k": np.tile((np.arange(NT, dtype=np.float32) * P), (P, E, 1)),
        "iota_n": np.arange(NMT, dtype=np.float32)[None, :],
        "tok_ids": (np.arange(P)[:, None] + np.arange(TOPK)[None, :] * (NT * P)).astype(np.float32),
    }
    nc = bacc.Bacc("TRN2", target_bir_lowering=False, num_devices=1)
    aps = [nc.dram_tensor(n, a.shape, mb.dt.from_np(a.dtype), kind="ExternalInput").ap() for n, a in arrays.items()]
    out = nc.dram_tensor("layer_out", (NT * P, D), F32, kind="ExternalOutput").ap()
    build(nc, *aps, out)
    r = run_bass_kernel_spmd(nc, [arrays], core_ids=[0])
    return r.results[0]["layer_out"].reshape(B, S, D)
```

```python
from collections import namedtuple
from contextlib import ExitStack

import numpy as np

import concourse.bass as bass
from concourse import mybir

ALU = mybir.AluOpType
ACT = mybir.ActivationFunctionType
AX_X = mybir.AxisListType.X
F32, F16, BF16 = mybir.dt.float32, mybir.dt.float16, mybir.dt.bfloat16
I32, U32 = mybir.dt.int32, mybir.dt.uint32
ds = bass.ds

P = 128
B, S, D = 4, 1024, 256
H, QL, NOPE, ROPE, VD = 16, 192, 64, 64, 128
C = 64
HD = NOPE + ROPE
TB = S // P
NT = B * TB
KD = D // P
NQ = H * HD
E, I_E, TOPK = 16, 176, 2
SI = 2 * I_E
KE = 88
EPS = 1e-5
LIST = NT * P + P
DUMMY = E * LIST
NMT = (NT * P * TOPK) // P + E
ROW = 2 * D + 2
NY = TOPK * NT * P
WMAX = 64.0
HSCALE = 2.0 ** -15
GROUP = [8, 4, 2, 2, 1, 1, 1, 1]
UNITS = [H // g for g in GROUP]
EARLY_NORMS = [u > 4 for u in UNITS]
UB = sum(UNITS)
UPRE = [sum(UNITS[:i]) for i in range(TB)]
LN_STEPS = 14
NEWTON = 3
MAX_AFTER = 0
SEED = 1597463007.0
A_Q, A_KV, A_O, A_SG, A_SD, A_R, A_GU, A_D = range(8)


class Tile:

    def __init__(self, off, b=None):
        self.off, self.b = off, b
        self.i = off % TB

    def at(self, k):
        return Tile(self.off + k, self.b)

    def count(self, per, k):
        return per * self.off + k if self.b is None else self.b * (per * TB) + (per * self.off + k)

    def pair(self, per):
        n = per * (self.off // 2 + 1)
        return n if self.b is None else self.b * (per * TB // 2) + n

    def units(self, per, u, k):
        n = per * (UB * (self.off // TB) + UPRE[self.i]) + k
        n = n + per * u
        return n if self.b is None else self.b * (per * UB) + n

    def row(self):
        return P * self.off if self.b is None else self.b * (P * TB) + P * self.off

    def exists(self):
        return self.b is not None or 0 <= self.off < NT


class Steps:

    def __init__(self, eng, sem, per, first):
        self.eng, self.sem, self.per, self.first, self.n = eng, sem, per, first, 0

    def do(self, ins, after_wait=None):
        self.n += 1
        assert self.n <= self.per
        ins.then_inc(self.sem, 1)
        self.eng.wait_ge(self.sem, self.first(self.per, self.n))
        if after_wait is not None:
            after_wait(self.eng)


PEEL = 4


def sections(eng, emit):
    for off in range(PEEL):
        emit(Tile(off))
    with eng.Fori(0, B - 1) as b:
        for off in range(PEEL, PEEL + TB):
            emit(Tile(off, b))
    for off in range((B - 1) * TB + PEEL, NT + 2):
        emit(Tile(off))


def build(nc, x, wqaT, wqb_peT, wqb_nopeT, wkva, wkT, wvT, wo, gateT, wgu, wd, wsg, wsd,
          cos_t, sin_t, ident, causal, tri, iota_e, iota_k, iota_n, tok_ids, out):
    nc.disable_value_cache = True
    ctx = ExitStack()
    with ctx:
        def sb(name, shape, dt):
            return ctx.enter_context(nc.sbuf_tensor(name, shape, dt))

        def sem(name):
            return ctx.enter_context(nc.semaphore(name))

        lists = nc.dram_tensor("lists", [DUMMY + P, ROW], F16, kind="Internal").ap()
        y_exp = nc.dram_tensor("y_exp", [NY, D], F32, kind="Internal").ap()
        dense = nc.dram_tensor("dense", [NT * P, D], F32, kind="Internal").ap()

        cos_sb = sb("cos_sb", [P, TB, ROPE], F32)
        sin_sb = sb("sin_sb", [P, TB, ROPE], F32)
        id32 = sb("id32", [P, P], F32)
        id16 = sb("id16", [P, P], F16)
        idbf = sb("idbf", [P, P], BF16)
        maskbf = sb("maskbf", [P, P], BF16)
        tri16 = sb("tri16", [P, P], F16)
        ones16 = sb("ones16", [P, P], F16)
        iota_e_sb = sb("iota_e_sb", [P, E], F32)
        iota_k_sb = sb("iota_k_sb", [P, E, NT], F32)
        iota_n_sb = sb("iota_n_sb", [1, NMT], F32)
        wq = sb("wq", [P, 2, KD, NQ + 2 * C], F16)
        wout = sb("wout", [P, 2, H // 2, D], F16)
        wsg_sb = sb("wsg_sb", [P, 2, KD, 2 * SI], F16)
        wsd_sb = sb("wsd_sb", [P, 2, 3, D], F16)
        wr_sb = sb("wr_sb", [P, 2, KD, E], F16)
        wgu_sb = sb("wgu_sb", [P, KD, E, 2, 2 * I_E], F16)
        wd_sb = sb("wd_sb", [P, 2, E, 2, D], F16)
        amax = sb("amax", [P, 8], F32)
        amax_all = sb("amax_all", [P, 8], F32)
        winv = sb("winv", [P, 8], F32)
        wamp = sb("wamp", [P, 8], F32)
        fac = sb("fac", [P, 8], F32)
        f_att, f_natt, f_out, f_sgh, f_sd, f_guh, f_ed = (fac[:, k:k + 1] for k in range(7))
        amax_gu = sb("amax_gu", [P, 4], F32)

        x_sb = sb("x_sb", [P, 4, D], F32)
        ln_st = sb("ln_st", [P, 2, 8], F32)
        ln_mv = sb("ln_mv", [P, 2, 2], F32)
        ln_w = sb("ln_w", [P, 3, 2], F32)
        xn = sb("xn", [P, D], F32)
        xs = sb("xs", [P, 2, 2, D], F16)
        xT = sb("xT", [P, 2, 2, KD, P], F16)
        NPE = (H + 1) * ROPE
        work = sb("work", [P, 3 * NPE + H * HD + HD], F32)
        pe = work[:, 0:NPE].rearrange("p (h r) -> p h r", r=ROPE)
        rot = work[:, NPE:2 * NPE].rearrange("p (h r) -> p h r", r=ROPE)
        rot2 = work[:, 2 * NPE:3 * NPE].rearrange("p (h r) -> p h r", r=ROPE)
        qs = work[:, 3 * NPE:3 * NPE + H * HD].bitcast(F16).rearrange("p (s h d) -> p s h d", s=2, h=H)
        ks = work[:, 3 * NPE + H * HD:].bitcast(F16).rearrange("p (s d) -> p s d", s=2)
        qT = sb("qT", [P, 2, 2, H * P], F16)
        kT = sb("kT", [P, 2, S], F16)
        ckv = sb("ckv", [P, 2, TB, C], F16)
        probs = sb("probs", [P, 2, S], F32)
        pT = sb("pT", [P, 2, 2, 2, 512], F16)
        smax = sb("smax", [P, 2, 8], F32)
        nmax = sb("nmax", [P, 2, 8], F32)
        ssum = sb("ssum", [P, 2, 2, H], F32)
        rsum = sb("rsum", [P, H], F32)
        o_sb = probs[:, 0, :]
        oT = probs[:, 1, :].bitcast(F16).rearrange("p (a k n) -> p a k n", a=2, k=H // 2)
        os_ = pT[:, 1, :, :, :].rearrange("p a g n -> p a (g n)")
        x1 = sb("x1", [P, 2, D], F32)
        xs2 = sb("xs2", [P, 2, TOPK, ROW], F16)
        x2T = sb("x2T", [P, 2, KD, P], F16)
        gate = sb("gate", [P, SI], F32)
        hid = sb("hid", [P, SI], F32)
        hs = sb("hs", [P, 2, SI], F16)
        hT = sb("hT", [P, 2, 3, P], F16)
        den = sb("den", [P, 2, D], F32)
        lg_all = sb("lg_all", [P, NT, E], F32)
        top_all = sb("top_all", [P, NT, TOPK], F32)
        lg = sb("lg", [P, 2, E], F32)
        top8 = sb("top8", [P, 2, 8], F32)
        top_ix = sb("top_ix", [P, 2, 8], U32)
        ixf = sb("ixf", [P, 2], F32)
        pick = sb("pick", [P, 2, TOPK, E], F32)
        picked = sb("picked", [P, 2, E], F16)
        place = sb("place", [P, E], F32)
        place_k = sb("place_k", [P, E], F32)
        slot_f = sb("slot_f", [P, TOPK], F32)
        slot = sb("slot", [P, 2, TOPK], I32)
        used = sb("used", [P, E], F32)
        dest_f = sb("dest_f", [P, TOPK], F32)

        s_ps = ctx.enter_context(nc.psum_tensor("s_ps", [P, 4, 512], F32))
        t_ps = ctx.enter_context(nc.psum_tensor("t_ps", [P, 2, 512], F32))
        o_ps = ctx.enter_context(nc.psum_tensor("o_ps", [P, 2, 512], F32))
        tt = [t_ps[:, g, :].bitcast(F16) for g in range(2)]
        st = [s_ps[:, g, :].bitcast(F16) for g in range(4)]
        ot = [o_ps[:, g, :].bitcast(F16) for g in range(2)]
        o_flat = o_ps[:, :, :].rearrange("p a n -> p (a n)")

        names = """c_in w_a w_b w_x0 c_ready qb_made qb_copied wq_made wq_copied wo_made wo_copied prep
                   amax_ready amax_reduced scales hi_made lo_made w_gu w_d
                   stat_s stats ln_s normed row_s ln1_done xT_made xT_ready q_made hi_q lo_q pe_ready rope_s rope_done
                   qT_made qT_act qT_dve ckv_ready s_made maxs max_ready exp_done p_made hi_p lo_p pv_made
                   o_evs o_ready hi_o lo_o oT_made oT_act oT_dve proj_made x1_done ln2_done x2T_made x2T_ready
                   gu_made lgt_made gate_done hids hid_done hi_h lo_h route_s mask_ready rank_made slot_s slot_done
                   hT_made hT_ready down_made dense_done listed
                   used_ready pads tail_s tab_ready gu_prep gu_hi gu_lo gu_amax gu_red gu_scale
                   m_xT m_xTs m_gu m_gate m_q m_hid m_hi m_lo m_hT m_hTs m_down m_y
                   passed c_w w_exp c_sum c_y0""".split()
        s = namedtuple("Signals", names)(*(sem(n) for n in names))
        xin = [sem(f"x_in{k}") for k in range(4)]
        xn_s = [sem(f"xn_made{k}") for k in range(2)]
        scattered = [sem(f"scattered{k}") for k in range(2)]
        stored = [sem(f"stored{k}") for k in range(2)]
        xg_in = [sem(f"xg_in{k}") for k in range(8)]
        m_out = [sem(f"m_out{k}") for k in range(8)]
        c_loaded = [sem(f"c_loaded{k}") for k in range(2)]
        c_out = [sem(f"c_out{k}") for k in range(2)]

        ga = wgu_sb[:, :, :, :, :].rearrange("p k e s j -> p (k e s j)").bitcast(F32)
        gb = wd_sb[:, :, :, :, :].rearrange("p k e s j -> p (k e s j)").bitcast(F32)

        def cut(view, at, *shape):
            n = int(np.prod(shape))
            v = view[:, at:at + n]
            return (v.rearrange("p (a b) -> p a b", a=shape[0]) if len(shape) == 2 else v), at + n

        r_wqaT, at = cut(ga, 0, 2, D)
        r_pe, at = cut(ga, at, 2, H * ROPE)
        r_nopeT, at = cut(ga, at, H, QL)
        r_wkT, at = cut(ga, at, H, C)
        r_qb, at = cut(ga, at, 2, H * C)
        r_wvT, at = cut(ga, at, H, C)
        r_wsd, at = cut(ga, at, 3, D)
        r_wo, at = cut(gb, 0, H, D)
        r_out, at = cut(gb, at, H // 2, D)
        r_wsg, at = cut(gb, at, KD, 2 * SI)
        r_wr, at = cut(gb, at, KD, E)
        r_wq = work[:, 0:KD * (NQ + 2 * C)].rearrange("p (k n) -> p k n", k=KD)
        QLB = QL - P
        SPLITS = [
            (r_wq[:, :, 0:NQ], wq[:, 0, :, 0:NQ], wq[:, 1, :, 0:NQ], P, A_Q),
            (r_wq[:, :, NQ:], wq[:, 0, :, NQ:], wq[:, 1, :, NQ:], P, A_KV),
            (r_out, wout[:, 0], wout[:, 1], P, A_O),
            (r_wsg, wsg_sb[:, 0], wsg_sb[:, 1], P, A_SG),
            (r_wsd, wsd_sb[:, 0], wsd_sb[:, 1], P, A_SD),
            (r_wr, wr_sb[:, 0], wr_sb[:, 1], P, A_R),
        ]
        N_EARLY = 8
        wgu_v = wgu.rearrange("e (k p) j -> p k e j", k=KD)
        wd_v = wd.rearrange("e (k p) n -> p k e n", p=KE)
        gu_raw = ga.rearrange("p (k e j) -> p k e j", k=KD, e=E)
        d_raw = gb.rearrange("p (k e j) -> p k e j", k=2, e=E)
        GC = 4
        gu_w = work[:, 0:GC * 2 * I_E].rearrange("p (e j) -> p e j", e=GC)
        d_w = work[:, GC * 2 * I_E:GC * (2 * I_E + D)].rearrange("p (e j) -> p e j", e=GC)

        XB, YB = 8, 4
        def carve(view, at, shape, dt):
            words = int(np.prod(shape)) * (2 if dt == F16 else 4) // 4
            v = view[:, at:at + words]
            v = v if dt == F32 else v.bitcast(dt)
            names_ = "abcd"[:len(shape)]
            sizes = dict(zip(names_, shape))
            return v.rearrange(f"p ({' '.join(names_)}) -> p {' '.join(names_)}", **sizes), at + words

        q_mem = qT[:, :, :, :].rearrange("p t a n -> p (t a n)").bitcast(F32)
        os_mem = pT[:, 1, :, :, :].rearrange("p a g n -> p (a g n)").bitcast(F32)
        xg, w_at = carve(work, GC * (2 * I_E + D), (XB, ROW), F16)
        pT_mem = pT[:, 0, :, :, :].rearrange("p a g n -> p (a g n)").bitcast(F32)
        xgT, p_at = carve(pT_mem, 0, (2, 2, KD, P), F16)
        m_hs, p_at = carve(pT_mem, p_at, (2, 2, I_E), F16)
        m_hT_sb, w_at = carve(work, w_at, (2, 2, P), F16)
        m_hT_sb = m_hT_sb[0:KE]
        m_g, m_m = gate[:, 0:I_E], hid[:, 0:I_E]
        m_h, _ = carve(x1[:, :, :].rearrange("p a n -> p (a n)"), 0, (2, I_E), F32)
        m_ys, _ = carve(o_sb, 0, (YB, D), F32)
        CT = 2
        c_in, q_at = carve(q_mem, 0, (2, 3, CT * D), F32)
        c_in = c_in.rearrange("p q k (c n) -> p q k c n", c=CT)
        c_o, q_at = carve(q_mem, q_at, (2, CT, D), F32)
        ge, ge_at = carve(q_mem, 0, (NMT, E), F32)
        ge2, ge_at = carve(q_mem, ge_at, (NMT, E), F32)
        ge, ge2 = ge[0:1], ge2[0:1]
        cmp_k, _ = carve(probs[:, 0, :], 0, (E, NT), F32)
        w_e, os_at = carve(os_mem, 0, (NT, E), F32)
        w_d, os_at = carve(os_mem, os_at, (NT, E), F32)
        cnt = sb("cnt", [P, E], F32)
        tiles_e = sb("tiles_e", [P, E], F32)
        ends = sb("ends", [P, E], F32)
        ones_e = sb("ones_e", [P, E], F32)
        jump = sb("jump", [P, E], F32)
        t_row = sb("t_row", [1, NMT], F32)
        t_exp = sb("t_exp", [1, NMT], F32)
        tab = sb("tab", [1, 2, NMT], I32)
        free_i = sb("free_i", [1, E], I32)
        pad, _ = carve(hT[:, :, :, :].rearrange("p a k n -> p (a k n)").bitcast(F32), 0, (ROW,), F16)
        w_s = sb("w_s", [P, NT], F32)
        w_k = sb("w_k", [P, NT, TOPK], F32)
        w_t = sb("w_t", [P, NT], F32)

        def own_wait(eng):
            eng.sem_inc(s.passed, 1)

        block = ctx.enter_context(nc.Block())

        @block.sync
        def _(sp):
            def load(dst, src, done):
                sp.dma_start(dst, src).then_inc(done, 16)

            load(r_nopeT[0:NOPE], wqb_nopeT, s.w_a)
            load(r_wkT[0:NOPE], wkT, s.w_a)
            load(r_wqaT[:, 0, :], wqaT[0:P, :], s.w_a)
            load(r_wqaT[0:QLB, 1, :], wqaT[P:QL, :], s.w_a)
            load(r_pe[:, 0, :], wqb_peT[0:P, :], s.w_a)
            load(r_pe[0:QLB, 1, :], wqb_peT[P:QL, :], s.w_a)
            load(r_wvT, wvT, s.w_a)
            load(r_wo, wo.rearrange("(h d) n -> d h n", d=VD), s.w_a)
            load(r_wq[:, :, NQ:], wkva.rearrange("(k p) n -> p k n", p=P), s.w_b)
            load(r_wsg, wsg.rearrange("(k p) n -> p k n", p=P), s.w_b)
            load(r_wsd[:, 0:2, :], wsd[0:2 * P, :].rearrange("(k p) n -> p k n", p=P), s.w_b)
            load(r_wsd[0:SI - 2 * P, 2, :], wsd[2 * P:SI, :], s.w_b)
            load(r_wr, gateT.rearrange("(k p) n -> p k n", p=P), s.w_b)
            for dst, src in ((id32[:, :], ident), (probs[:, 1, 0:P], causal), (probs[:, 0, 0:P], tri),
                             (cos_sb[:, :, :], cos_t), (sin_sb[:, :, :], sin_t), (iota_e_sb[:, :], iota_e),
                             (iota_k_sb[:, :, :], iota_k), (iota_n_sb[:, :], iota_n), (dest_f[:, :], tok_ids)):
                load(dst, src, s.c_in)
            for k in range(3):
                load(x_sb[:, k, :], x[k * P:(k + 1) * P, :], xin[k])

            def store_dense(t):
                sp.wait_ge(s.dense_done, t.count(1, 1))
                own_wait(sp)
                sp.dma_start(dense[ds(t.row(), P), :], den[:, t.off % 2, :]).then_inc(stored[t.off % 2], 16)

            def section(t):
                p, n3 = t.at(-1), t.at(3)
                if p.exists() and n3.exists():
                    sp.wait_ge(s.x1_done, p.count(1, 1))
                    own_wait(sp)
                if n3.exists():
                    sp.dma_start(x_sb[:, n3.off % 4, :], x[ds(n3.row(), P), :]).then_inc(xin[n3.off % 4], 16)
                if t.at(-2).exists():
                    store_dense(t.at(-2))
            sp.wait_ge(s.lo_made, len(SPLITS))
            for k in range(KD):
                load(gu_raw[:, k], wgu_v[:, k], s.w_gu)
            for k in range(2):
                load(d_raw[0:KE, k], wd_v[:, k], s.w_d)
            sections(sp, section)

            sp.wait_ge(s.used_ready, 1)
            sp.dma_start(lists[DUMMY:DUMMY + P, :], pad[:, :]).then_inc(s.pads, 16)
            for e in range(E):
                row = sp.value_load(free_i[0:1, e:e + 1], min_val=0, max_val=DUMMY - P)
                sp.dma_start(lists[ds(row, P), :], pad[:, :]).then_inc(s.pads, 16)
            sp.wait_ge(s.pads, 16 * (E + 1))
            for par in range(2):
                sp.wait_ge(scattered[par], 16 * TOPK * NT // 2)
            sp.wait_ge(s.tab_ready, 1)

            def expert_rows(n, q):
                row = sp.value_load(tab[0:1, 0, ds(n, 1)], min_val=0, max_val=DUMMY)
                sp.dma_start(xg[:, q, :], lists[ds(row, P), :]).then_inc(xg_in[q], 16)
            for q in range(XB):
                expert_rows(q, q)
            with sp.Fori(1, NMT // XB) as m:
                for q in range(XB):
                    sp.wait_ge(m_out[q], m * 16)
                    own_wait(sp)
                    expert_rows(m * XB + q, q)
            for q in range(XB):
                sp.wait_ge(m_out[q], 16 * (NMT // XB))
            for par in range(2):
                sp.wait_ge(stored[par], 16 * NT // 2)

            def rows(a, first):
                return a[ds(first, CT * P), :].rearrange("(c p) n -> p c n", p=P)

            NC = NT // CT
            with sp.Fori(0, NC // 2) as m:
                for q in range(2):
                    first = m * (2 * CT * P) + q * CT * P
                    sp.wait_ge(s.c_sum, m * 2 + q + 1)
                    own_wait(sp)
                    sp.dma_start(c_in[:, q, 0], rows(dense, first)).then_inc(c_loaded[q], 16)
                    sp.dma_start(c_in[:, q, 1], rows(y_exp, first)).then_inc(c_loaded[q], 16)
                    sp.dma_start(c_in[:, q, 2], rows(y_exp, first + NT * P)).then_inc(c_loaded[q], 16)

        def halves(i):
            if GROUP[i] == 1:
                return [[(0, 0, 4)], [(0, 4, i + 1)]]
            n = GROUP[i] // 2
            return [[(h * n + g, 0, i + 1) for g in range(n)] for h in range(2)]

        def half_tiles(i, h):
            return [(g, j) for g, j0, j1 in halves(i)[h] for j in range(j0, j1)]

        def s_off(i, g):
            return g * (P if i == 0 else 2 * P if i == 1 else 512)

        def att_loop(eng, t, unit):
            n = UNITS[t.i]
            rounds = (n - 4) // 2
            for u in range(2 if n > 2 else 0):
                unit(u, u % 2)
            if rounds > 0:
                nc.disable_value_cache = False
                with eng.Fori(1, rounds + 1) as k:
                    unit(k * 2, 0)
                    unit(k * 2 + 1, 1)
                nc.disable_value_cache = True
            unit(n - 2, 0)
            unit(n - 1, 1)

        def has_next(t, u, k):
            return not isinstance(u, int) or u + k < UNITS[t.i]

        @block.tensor
        def _(pe_):
            def mm(o, a, b, start, stop):
                return pe_.matmul(o, a, b, start=start, stop=stop)

            pe_.wait_ge(s.w_a, 16 * N_EARLY)
            for h in range(H):
                mm(o_ps[:, h // 8, (h % 8) * C:(h % 8 + 1) * C], r_nopeT[0:NOPE, h, 0:P], r_wkT[0:NOPE, h, :], True, True)
                last = mm(t_ps[0:QLB, h // 8, (h % 8) * C:(h % 8 + 1) * C], r_nopeT[0:NOPE, h, P:QL],
                          r_wkT[0:NOPE, h, :], True, True)
            last.then_inc(s.qb_made, 1)
            pe_.wait_ge(s.qb_copied, 1)
            for m in range(KD):
                for c in range(NQ // 512):
                    src = r_qb if c < 2 else r_pe
                    cc = slice((c % 2) * 512, (c % 2) * 512 + 512)
                    if m:
                        pe_.wait_ge(s.wq_copied, c + 1)
                    mm(s_ps[:, c, :], r_wqaT[:, 0, m * P:(m + 1) * P], src[:, 0, cc], True, False)
                    mm(s_ps[:, c, :], r_wqaT[0:QLB, 1, m * P:(m + 1) * P], src[0:QLB, 1, cc], False,
                       True).then_inc(s.wq_made, 1)
            for hp in range(H // 2):
                bank = (o_ps if hp % 4 < 2 else t_ps)[:, hp % 2, 0:D]
                if hp >= 4:
                    pe_.wait_ge(s.wo_copied, hp - 3)
                for e in range(2):
                    last = mm(bank[e * C:(e + 1) * C], r_wvT[:, 2 * hp + e, :], r_wo[:, 2 * hp + e, :], True, True)
                last.then_inc(s.wo_made, 1)

            def transposes(bank, rows, done):
                for a in range(2):
                    for k in range(KD):
                        last = pe_.transpose(bank[:, (2 * a + k) * P:(2 * a + k + 1) * P], rows(a, k), id16[:, :])
                last.then_inc(done, 1)

            def x_transposes(n):
                pe_.wait_ge(s.ln1_done, n.count(2, 2))
                transposes(st[1], lambda a, k: xs[:, n.off % 2, a, k * P:(k + 1) * P], s.xT_made)

            def x2_transposes(p):
                pe_.wait_ge(s.ln2_done, p.count(2, 2))
                transposes(st[0], lambda a, k: xs2[:, p.off % 2, 0, a * D + k * P:a * D + (k + 1) * P], s.x2T_made)

            def norm_transposes(t):
                if t.at(-1).exists():
                    x2_transposes(t.at(-1))
                if t.at(2).exists():
                    x_transposes(t.at(2))

            def split_product(o, lhs, rhs, done):
                n = len(done)
                first = True
                for k in done:
                    for a, b in ((0, 0), (0, 1), (1, 0)):
                        last = mm(o, lhs(a, k), rhs(b, k), first, k == done[-1] and a == 1)
                        first = False
                return last

            def project(n, bank, c0, w):
                split_product(bank, lambda a, k: xT[:, n.off % 2, a, k, :], lambda b, k: wq[:, b, k, c0:c0 + w],
                              list(range(KD))).then_inc(s.q_made, 1)

            def latent_projections(n):
                pe_.wait_ge(s.xT_ready, n.count(1, 1))
                if n.off > 0 or n.b is not None:
                    pe_.wait_ge(s.qT_act, n.at(-1).count(3, 3))
                    pe_.wait_ge(s.qT_dve, n.at(-1).count(2, 2))
                project(n, t_ps[:, 1, 0:P], NQ, 2 * C)
                for g in range(2):
                    project(n, s_ps[:, 2 + g, :], H * NOPE + g * 512, 512)

            def query_projections(n):
                if n.at(-3).exists():
                    pe_.wait_ge(s.hid_done, n.at(-3).count(1, 1))
                for g in range(2):
                    project(n, s_ps[:, g, :], g * 512, 512)

            def q_transposes(n):
                pe_.wait_ge(s.lo_q, n.count(3, 3))
                pe_.wait_ge(s.rope_done, n.count(1, 1))
                for g, bank in enumerate((tt[0], tt[1], st[2], st[3])):
                    for h in range(8):
                        last = pe_.transpose(bank[:, h * P:(h + 1) * P], qs[:, g // 2, (g % 2) * 8 + h, :], id16[:, :])
                    last.then_inc(s.qT_made, 1)
                pe_.wait_ge(s.qT_act, n.count(3, 1))
                for a in range(2):
                    last = pe_.transpose(tt[0][:, a * P:(a + 1) * P], ks[:, a, :], id16[:, :])
                last.then_inc(s.qT_made, 1)

            def o_transposes(p):
                pe_.wait_ge(s.hi_o, p.count(1, 1))
                for a in range(2):
                    if a:
                        pe_.wait_ge(s.lo_o, p.count(1, 1))
                        if p.at(-1).exists():
                            pe_.wait_ge(s.route_s, p.at(-1).count(6, 1))
                    for hp in range(H // 2):
                        last = pe_.transpose(ot[a][:, hp * P:(hp + 1) * P], os_[:, a, hp * P:(hp + 1) * P], id16[:, :])
                    last.then_inc(s.oT_made, 1)

            def out_projection(p):
                pe_.wait_ge(s.oT_act, p.count(1, 1))
                pe_.wait_ge(s.oT_dve, p.count(1, 1))
                if p.at(-1).exists():
                    pe_.wait_ge(s.hT_ready, p.at(-1).count(2, 2))
                split_product(t_ps[:, 0, 0:D], lambda a, k: oT[:, a, k, :], lambda b, k: wout[:, b, k, :],
                              list(range(H // 2))).then_inc(s.proj_made, 1)

            def scores(t, u, par, h):
                i, G = t.i, GROUP[t.i]
                L = (i + 1) * P
                flat = s_ps[:, :, :].rearrange("p a n -> p (a n)")
                for g, j0, j1 in halves(i)[h]:
                    base = 1024 * par + s_off(i, g)
                    c0, c1 = j0 * P, j1 * P
                    for a, b in ((0, 0), (0, 1), (1, 0)):
                        last = mm(flat[:, base + c0:base + c1], qT[:, t.off % 2, a, ds((u * G + g) * P, P)], kT[:, b, c0:c1],
                                  a + b == 0, a == 1 and c1 < L)
                    if c1 == L:
                        last = mm(flat[:, base + L - P:base + L], idbf[:, :], maskbf[:, :], False, True)
                if h:
                    last.then_inc(s.s_made, 1)

            def attention(t):
                n, p = t.at(1), t.at(-1)
                i, G = t.i, GROUP[t.i]
                L = (i + 1) * P
                pe_.wait_ge(s.qT_act, t.count(3, 3))
                pe_.wait_ge(s.qT_dve, t.count(2, 2))
                pe_.wait_ge(s.ckv_ready, t.count(1, 1))
                if n.exists():
                    pe_.wait_ge(s.pe_ready, n.count(1, 1))
                    pe_.wait_ge(s.lo_q, n.count(3, 3))
                def first_scores(u):
                    for h in range(2):
                        scores(t, u, u, h)
                first_scores(0)
                if t.at(-2).exists():
                    shared_down(t.at(-2))
                first_scores(1)
                if p.exists():
                    pe_.wait_ge(s.x1_done, p.count(1, 1))

                def values(u, par):
                    for h in range(2):
                        pe_.wait_ge(s.lo_p, t.units(2, u, h + 1))
                        for c, (g, j) in enumerate(half_tiles(i, h)):
                            o = o_flat[:, ds((u * G + g) * C, C)]
                            for a, b in ((0, 0), (0, 1), (1, 0)):
                                last = mm(o, pT[:, par, a, h, c * P:(c + 1) * P], ckv[:, b, j, :],
                                          j == 0 and a + b == 0, j == i and a == 1)
                    last.then_inc(s.pv_made, 1)

                def unit(u, par):
                    first = isinstance(u, int) and u == 0
                    for h in range(2):
                        pe_.wait_ge(s.exp_done, t.units(2, u, h + 1))
                        if not first:
                            pe_.wait_ge(s.lo_p, t.units(2, u, h - 1))
                        for c, (g, j) in enumerate(half_tiles(i, h)):
                            last = pe_.transpose(t_ps[:, h, c * P:(c + 1) * P],
                                                 probs[:, par, g * L + j * P:g * L + (j + 1) * P], id32[:, :])
                        last.then_inc(s.p_made, 1)
                        if has_next(t, u, 2):
                            scores(t, u + 2, par, h)
                    if isinstance(u, int) and u == 1 and t.at(-2).exists():
                        pe_.wait_ge(s.slot_done, t.at(-2).count(1, 1))
                    if not first:
                        values(u - 1, 1 - par)
                att_loop(pe_, t, unit)
                if EARLY_NORMS[i]:
                    norm_transposes(t)
                values(UNITS[i] - 1, 1)

            def shared_up(p):
                if p.at(3).exists():
                    pe_.wait_ge(s.xT_ready, p.at(3).count(1, 1))
                pe_.wait_ge(s.x2T_ready, p.count(1, 1))
                for g in range(2):
                    last = split_product(s_ps[:, g, 0:SI], lambda a, k: x2T[:, a, k, :],
                                         lambda b, k: wsg_sb[:, b, k, g * SI:(g + 1) * SI], list(range(KD)))
                last.then_inc(s.gu_made, 1)
                if p.at(1).exists():
                    pe_.wait_ge(s.o_ready, p.at(1).count(1, 1))
                split_product(o_ps[:, 1, 0:E], lambda a, k: x2T[:, a, k, :], lambda b, k: wr_sb[:, b, k, :],
                              list(range(KD))).then_inc(s.lgt_made, 1)

            def hidden_transposes(q):
                pe_.wait_ge(s.hi_h, q.count(1, 1))
                pe_.wait_ge(s.lo_h, q.count(1, 1))
                for a in range(2):
                    for k in range(3):
                        w = min(P, SI - k * P)
                        last = pe_.transpose(tt[0][0:w, (3 * a + k) * P:(3 * a + k + 1) * P],
                                             hs[:, a, k * P:k * P + w], id16[:, :])
                last.then_inc(s.hT_made, 1)

            def shared_down(q):
                pe_.wait_ge(s.mask_ready, q.count(1, 1))
                if q.at(1).exists():
                    pe_.wait_ge(s.oT_act, q.at(1).count(1, 1))
                    pe_.wait_ge(s.oT_dve, q.at(1).count(1, 1))
                mm(o_ps[:, 0, 0:E], tri16[:, :], picked[:, q.off % 2, :], True, True)
                mm(o_ps[:, 0, E:2 * E], ones16[:, :], picked[:, q.off % 2, :], True, True)
                pe_.wait_ge(s.hT_ready, q.count(2, 2))

                def rows(k):
                    return min(P, SI - k * P)
                split_product(o_ps[:, 0, D:2 * D], lambda a, k: hT[0:rows(k), a, k, :],
                              lambda b, k: wsd_sb[0:rows(k), b, k, :], list(range(3))).then_inc(s.down_made, 1)

            pe_.wait_ge(s.c_ready, 1)
            pe_.wait_ge(s.lo_made, len(SPLITS))
            x_transposes(Tile(0))
            latent_projections(Tile(0))
            x_transposes(Tile(1))
            pe_.wait_ge(s.xT_ready, 2)
            query_projections(Tile(0))
            q_transposes(Tile(0))

            def section(t):
                n = t.at(1)
                if n.exists():
                    latent_projections(n)
                if t.at(-2).exists():
                    hidden_transposes(t.at(-2))
                if t.at(-1).exists():
                    o_transposes(t.at(-1))
                if n.exists():
                    query_projections(n)
                if t.at(-1).exists():
                    out_projection(t.at(-1))
                if t.exists():
                    attention(t)
                elif t.at(-2).exists():
                    shared_down(t.at(-2))
                if n.exists():
                    q_transposes(n)
                if not (t.exists() and EARLY_NORMS[t.i]):
                    norm_transposes(t)
                if t.at(-1).exists():
                    shared_up(t.at(-1))
            sections(pe_, section)

            pe_.wait_ge(s.gu_lo, 1)
            pe_.wait_ge(s.tab_ready, 1)

            def xg_transposes(n, q, par, m):
                pe_.wait_ge(xg_in[q], m * 16 + 16)
                for a in range(2):
                    for k in range(KD):
                        last = pe_.transpose(tt[par][:, (2 * a + k) * P:(2 * a + k + 1) * P],
                                             xg[:, q, a * D + k * P:a * D + (k + 1) * P], id16[:, :])
                last.then_inc(s.m_xT, 1)

            def expert_up(n, par):
                e = pe_.value_load(tab[0:1, 1, ds(n, 1)], min_val=0, max_val=E - 1)
                pe_.wait_ge(s.m_xTs, n + 1)
                for g in range(2):
                    last = split_product(s_ps[:, 2 * par + g, 0:I_E], lambda a, k: xgT[:, par, a, k, :],
                                         lambda b, k: wgu_sb[:, k, ds(e, 1), b, g * I_E:(g + 1) * I_E], list(range(KD)))
                last.then_inc(s.m_gu, 1)

            def h_transposes(n, par):
                pe_.wait_ge(s.m_hi, n + 1)
                pe_.wait_ge(s.m_lo, n + 1)
                for a in range(2):
                    for k in range(2):
                        last = pe_.transpose(ot[0][0:KE, (2 * a + k) * P:(2 * a + k + 1) * P],
                                             m_hs[:, par, a, k * KE:(k + 1) * KE], id16[:, :])
                last.then_inc(s.m_hT, 1)

            def expert_down(n):
                e = pe_.value_load(tab[0:1, 1, ds(n, 1)], min_val=0, max_val=E - 1)
                pe_.wait_ge(s.m_hTs, n + 1)
                pe_.wait_ge(s.m_y, n + 1)
                split_product(o_ps[:, 1, 0:D], lambda a, k: m_hT_sb[:, a, k, :],
                              lambda b, k: wd_sb[0:KE, k, ds(e, 1), b, :], list(range(2))).then_inc(s.m_down, 1)

            xg_transposes(0, 0, 0, 0)
            xg_transposes(1, 1, 1, 0)
            expert_up(0, 0)
            xg_transposes(2, 2, 0, 0)
            expert_up(1, 1)
            xg_transposes(3, 3, 1, 0)
            with pe_.Fori(0, NMT // XB - 1) as m:
                for q in range(XB):
                    n = m * XB + q
                    h_transposes(n, q % 2)
                    expert_up(n + 2, q % 2)
                    xg_transposes(n + 4, (q + 4) % XB, q % 2, m + (q + 4) // XB)
                    expert_down(n)
            for n in range(NMT - XB, NMT):
                h_transposes(n, n % 2)
                if n + 2 < NMT:
                    expert_up(n + 2, n % 2)
                if n + 4 < NMT:
                    xg_transposes(n + 4, (n + 4) % XB, n % 2, (n + 4) // XB)
                expert_down(n)

        @block.scalar
        def _(act):
            def copy(o, i):
                return act.copy(o, i)

            act.wait_ge(s.qb_made, 1)
            copy(r_qb[:, 0, :], o_flat)
            copy(r_qb[0:QLB, 1, :], t_ps[0:QLB, :, :].rearrange("p a n -> p (a n)")).then_inc(s.qb_copied, 1)
            for m in range(KD):
                for c in range(NQ // 512):
                    act.wait_ge(s.wq_made, m * 4 + c + 1)
                    copy(r_wq[:, m, c * 512:(c + 1) * 512], s_ps[:, c, :]).then_inc(s.wq_copied, 1)
            for hp in range(H // 2):
                act.wait_ge(s.wo_made, hp + 1)
                copy(r_out[:, hp, :], (o_ps if hp % 4 < 2 else t_ps)[:, hp % 2, 0:D]).then_inc(s.wo_copied, 1)
            act.wait_ge(s.scales, 1)
            for raw, hi, lo, rows, col in SPLITS:
                act.activation(hi[0:rows], raw[0:rows], ACT.Copy, scale=winv[0:rows, col:col + 1]).then_inc(s.hi_made, 1)

            def x_copy(n):
                act.wait_ge(s.xT_made, n.count(1, 1))
                copy(xT[:, n.off % 2].rearrange("p a k n -> p (a k n)"), st[1][:, 0:4 * P]).then_inc(s.xT_ready, 1)

            def norm_copies(t):
                p = t.at(-1)
                if p.exists():
                    act.wait_ge(s.x2T_made, p.count(1, 1))
                    copy(x2T[:, :, :, :].rearrange("p a k n -> p (a k n)"), st[0][:, 0:4 * P]).then_inc(s.x2T_ready, 1)
                if t.at(2).exists():
                    x_copy(t.at(2))

            def latent_copies(n):
                act.wait_ge(s.q_made, n.count(5, 1))
                copy(pe[:, H, :], t_ps[:, 1, C:2 * C])
                copy(ks[:, 0, 0:C], t_ps[:, 1, 0:C]).then_inc(s.hi_q, 1)
                for g in range(2):
                    act.wait_ge(s.q_made, n.count(5, 2 + g))
                    last = copy(pe[:, 8 * g:8 * g + 8, :], s_ps[:, 2 + g, :].rearrange("p (h r) -> p h r", r=ROPE))
                last.then_inc(s.pe_ready, 1)

            def query_copies(n):
                for g in range(2):
                    act.wait_ge(s.q_made, n.count(5, 4 + g))
                    copy(qs[:, 0, 8 * g:8 * g + 8, 0:NOPE],
                         s_ps[:, g, :].rearrange("p (h r) -> p h r", r=NOPE)).then_inc(s.hi_q, 1)

            def qT_copies(n, t):
                par = n.off % 2
                act.wait_ge(s.qT_made, n.count(5, 1))
                copy(qT[:, par, 0, 0:1024], tt[0]).then_inc(s.qT_act, 1)
                if t is not None:
                    out_hi(t)
                act.wait_ge(s.qT_made, n.count(5, 3))
                copy(qT[:, par, 1, 0:1024], st[2]).then_inc(s.qT_act, 1)
                act.wait_ge(s.qT_made, n.count(5, 5))
                copy(kT[:, :, n.i * P:(n.i + 1) * P], tt[0][:, 0:2 * P].rearrange("p (a n) -> p a n", a=2)).then_inc(s.qT_act, 1)

            def out_hi(p):
                act.wait_ge(s.o_ready, p.count(1, 1))
                copy(os_[:, 0, :], o_sb[:, :]).then_inc(s.hi_o, 1)

            def oT_copy(p):
                act.wait_ge(s.oT_made, p.count(2, 1))
                copy(oT[:, 0, :, :].rearrange("p k n -> p (k n)"), ot[0]).then_inc(s.oT_act, 1)

            def attention(t):
                i, G = t.i, GROUP[t.i]
                L = (i + 1) * P
                flat = s_ps[:, :, :].rearrange("p a n -> p (a n)")

                def exps(u, par, h):
                    if h == 0:
                        act.wait_ge(s.max_ready, t.units(1, u, 1))
                    for g, j0, j1 in halves(i)[h]:
                        base = 1024 * par + s_off(i, g)
                        part = h if G == 1 else 0
                        last = act.activation(probs[:, par, g * L + j0 * P:g * L + j1 * P], flat[:, base + j0 * P:base + j1 * P],
                                              ACT.Exp, bias=nmax[:, par, g:g + 1], scale=f_att,
                                              accum_out=ssum[:, t.off % 2, part, ds(u * G + g, 1)])
                    last.then_inc(s.exp_done, 1)

                def unit(u, par):
                    if not (isinstance(u, int) and u < 2):
                        act.wait_ge(s.pv_made, t.units(1, u, -1))
                    for h in range(2):
                        w = P * len(half_tiles(i, h))
                        act.wait_ge(s.p_made, t.units(2, u, h + 1))
                        copy(pT[:, par, 0, h, 0:w], t_ps[:, h, 0:w]).then_inc(s.hi_p, 1)
                        if has_next(t, u, 1):
                            exps(u + 1, 1 - par, h)
                exps(0, 0, 0)
                exps(0, 0, 1)
                att_loop(act, t, unit)

            def shared_act(p):
                act.wait_ge(s.gu_made, p.count(1, 1))
                act.activation(gate[:, :], s_ps[:, 0, 0:SI], ACT.Tanh, scale=f_sgh).then_inc(s.gate_done, 1)
                act.wait_ge(s.hid_done, p.count(1, 1))
                copy(hs[:, 0, :], hid[:, :]).then_inc(s.hi_h, 1)

            def hT_copy(q):
                act.wait_ge(s.hT_made, q.count(1, 1))
                w = SI - 2 * P
                src = tt[0][:, 0:6 * P].rearrange("p (a k n) -> p a k n", a=2, k=3)
                copy(hT[:, :, 0:2, :], src[:, :, 0:2, :]).then_inc(s.hT_ready, 1)
                copy(hT[0:w, :, 2, :], src[0:w, :, 2, :]).then_inc(s.hT_ready, 1)

            act.wait_ge(s.lo_made, len(SPLITS))
            x_copy(Tile(0))
            x_copy(Tile(1))
            latent_copies(Tile(0))
            query_copies(Tile(0))
            qT_copies(Tile(0), None)

            def section(t):
                n = t.at(1)
                if n.exists():
                    latent_copies(n)
                if t.at(-2).exists():
                    hT_copy(t.at(-2))
                if t.at(-1).exists():
                    oT_copy(t.at(-1))
                if n.exists():
                    query_copies(n)
                if t.exists():
                    attention(t)
                early = t.exists() and EARLY_NORMS[t.i]
                if early:
                    norm_copies(t)
                if n.exists():
                    qT_copies(n, t)
                elif t.exists():
                    out_hi(t)
                if not early:
                    norm_copies(t)
                if t.at(-1).exists():
                    shared_act(t.at(-1))
            sections(act, section)

            act.wait_ge(s.gu_scale, 1)
            for k in range(KD):
                with act.Fori(0, E // GC) as m:
                    act.wait_ge(s.gu_hi, m + (1 + k * (E // GC)))
                    act.activation(gu_w, gu_raw[:, k, ds(m * GC, GC), :], ACT.Copy, scale=winv[:, A_GU:A_GU + 1])
                    act.activation(d_w[0:KE], d_raw[0:KE, k, ds(m * GC, GC), :], ACT.Copy,
                                   scale=winv[0:KE, A_D:A_D + 1]).then_inc(s.gu_prep, 1)
            act.wait_ge(s.c_w, 1)
            act.activation(w_e[:, :, :].rearrange("p t e -> p (t e)"), w_d[:, :, :].rearrange("p t e -> p (t e)"),
                           ACT.Exp).then_inc(s.w_exp, 1)
            act.activation(w_t[:, :], w_t[:, :], ACT.Exp).then_inc(s.w_exp, 1)

            def xg_copy(n, par):
                act.wait_ge(s.m_xT, n + 1)
                copy(xgT[:, par, :, :, :].rearrange("p a k n -> p (a k n)"), tt[par][:, 0:4 * P]).then_inc(s.m_xTs, 1)

            def expert_gate(n, par):
                act.wait_ge(s.m_gu, n + 1)
                act.activation(m_g[:, :], s_ps[:, 2 * par, 0:I_E], ACT.Tanh, scale=f_guh).then_inc(s.m_gate, 1)
                act.wait_ge(s.m_hid, n + 1)
                copy(m_hs[:, par, 0, :], m_h[:, par, :]).then_inc(s.m_hi, 1)

            def y_copy(n, q, m):
                act.wait_ge(s.m_down, n + 1)
                if not (isinstance(m, int) and n < YB):
                    act.wait_ge(m_out[(q + YB) % XB], m * 16 + (0 if q < YB else 16))
                act.activation(m_ys[:, q % YB, :], o_ps[:, 1, 0:D], ACT.Copy, scale=f_ed).then_inc(s.m_y, 1)

            xg_copy(0, 0)
            xg_copy(1, 1)
            expert_gate(0, 0)
            xg_copy(2, 0)
            expert_gate(1, 1)
            xg_copy(3, 1)

            def expert_round(m, q, n):
                last = isinstance(n, int)
                if not last or n + 2 < NMT:
                    expert_gate(n + 2, q % 2)
                if not last or n + 4 < NMT:
                    xg_copy(n + 4, q % 2)
                y_copy(n, q, m)
            for q in range(XB):
                expert_round(0, q, q)
            with act.Fori(1, NMT // XB - 1) as m:
                for q in range(XB):
                    expert_round(m, q, m * XB + q)
            for q in range(XB):
                expert_round(NMT // XB - 1, q, NMT - XB + q)

            NC = NT // CT
            with act.Fori(0, NC // 2) as m:
                for q in range(2):
                    act.wait_ge(s.c_sum, m * 2 + q + 3)
                    first = m * (2 * CT * P) + q * CT * P
                    act.dma_start(out[ds(first, CT * P), :].rearrange("(c p) n -> p c n", p=P),
                                  c_o[:, q]).then_inc(c_out[q], 16)
            for q in range(2):
                act.wait_ge(c_out[q], 16 * (NC // 2 + 1))

        @block.vector
        def _(dve):
            def link(ins):
                link.n += 1
                ins.then_inc(s.prep, 1)
                dve.wait_ge(s.prep, link.n)
            link.n = 0

            def at(per, k):
                return k

            dve.wait_ge(s.c_in, 16 * 9)
            dve.tensor_copy(id16[:, :], id32[:, :])
            dve.tensor_copy(idbf[:, :], id32[:, :])
            dve.tensor_copy(maskbf[:, :], probs[:, 1, 0:P])
            dve.tensor_copy(tri16[:, :], probs[:, 0, 0:P])
            dve.memset(ones16[:, :], 1.0)
            dve.memset(ones_e[:, :], 1.0)
            dve.memset(amax[:, :], 0.0)
            link(dve.memset(amax_gu[:, :], 0.0))
            dve.tensor_scalar(used[:, :], iota_e_sb[:, :], float(LIST), None, ALU.mult)
            dve.memset(lg_all[:, :, :], 0.0).then_inc(s.c_ready, 1)
            for q in range(2):
                dve.sem_inc(c_out[q], 16)
            dve.sem_inc(s.m_y, 1)
            dve.sem_inc(s.c_sum, 2)
            dve.sem_inc(s.gu_hi, 1)

            dve.wait_ge(s.w_b, 16 * 5)
            dve.wait_ge(s.wq_copied, 8)
            dve.wait_ge(s.wo_copied, 8)
            for raw, rows, col in ((r_wq[:, :, 0:NQ], P, A_Q), (r_wq[:, :, NQ:], P, A_KV), (r_out, P, A_O),
                                   (r_wsg, P, A_SG), (r_wr, P, A_R)):
                link(dve.tensor_reduce(amax[0:rows, col:col + 1], raw.rearrange("p k n -> p (k n)") if col != A_Q and col != A_KV else raw,
                                       mybir.AxisListType.XY if col in (A_Q, A_KV) else AX_X, ALU.max, apply_absolute_value=True))
            link(dve.memset(r_wsd[SI - 2 * P:P, 2, :], 0.0))
            link(dve.tensor_reduce(amax[:, A_SD:A_SD + 1], r_wsd.rearrange("p k n -> p (k n)"), AX_X, ALU.max,
                                   apply_absolute_value=True))
            dve.sem_inc(s.amax_ready, 1)

            def scales(cols):
                link(dve.tensor_scalar(amax_all[:, cols], amax_all[:, cols], 1e-30, None, ALU.max))
                link(dve.tensor_scalar(wamp[:, cols], amax_all[:, cols], 1.0 / WMAX, None, ALU.mult))
                link(dve.reciprocal(winv[:, cols], wamp[:, cols]))

            dve.wait_ge(s.amax_reduced, 1)
            scales(slice(0, 6))
            link(dve.tensor_scalar(f_att, wamp[:, A_Q:A_Q + 1], wamp[:, A_KV:A_KV + 1], HD ** -0.5, ALU.mult, ALU.mult))
            dve.tensor_scalar(f_natt, f_att, -1.0, None, ALU.mult)
            dve.tensor_scalar(f_out, wamp[:, A_KV:A_KV + 1], wamp[:, A_O:A_O + 1], None, ALU.mult)
            dve.tensor_scalar(f_sgh, wamp[:, A_SG:A_SG + 1], 0.5, None, ALU.mult)
            link(dve.tensor_scalar(f_sd, wamp[:, A_SG:A_SG + 1], wamp[:, A_SG:A_SG + 1], 0.5 / HSCALE, ALU.mult, ALU.mult))
            link(dve.tensor_scalar(f_sd, f_sd, wamp[:, A_SD:A_SD + 1], None, ALU.mult))
            dve.sem_inc(s.scales, 1)
            for k, (raw, hi, lo, rows, col) in enumerate(SPLITS):
                dve.wait_ge(s.hi_made, k + 1)
                dve.scalar_tensor_tensor(lo[0:rows], raw[0:rows], winv[0:rows, col:col + 1], hi[0:rows],
                                         ALU.mult, ALU.subtract).then_inc(s.lo_made, 1)

            def norm_stats(n, p):
                if n.off > 0 or n.b is not None:
                    dve.wait_ge(s.normed, n.at(-1).count(1, 1))
                if n.exists():
                    dve.wait_ge(xin[n.off % 4], 16 * (n.off // 4 + 1) if n.b is None else n.b * 32 + 16 * (n.off // 4 + 1))
                    last = dve.bn_stats(ln_st[:, 0, 0:6], x_sb[:, n.off % 4, :])
                if p is not None and p.exists():
                    dve.wait_ge(s.x1_done, p.count(1, 1))
                    last = dve.bn_stats(ln_st[:, 1, 0:6], x1[:, p.off % 2, :])
                last.then_inc(s.stat_s, 1)
                dve.wait_ge(s.stat_s, n.count(1, 1))
                own_wait(dve)
                if n.exists():
                    last = dve.bn_aggr(ln_mv[:, 0, :], ln_st[:, 0, 0:6])
                if p is not None and p.exists():
                    last = dve.bn_aggr(ln_mv[:, 1, :], ln_st[:, 1, 0:6])
                last.then_inc(s.stats, 1)

            def expert_rows(p):
                row = xs2[:, p.off % 2]
                dve.wait_ge(s.ln2_done, p.count(2, 2))
                dve.tensor_copy(row[:, 1, 0:2 * D], row[:, 0, 0:2 * D])
                dve.tensor_copy(row[:, :, 2 * D:ROW].bitcast(I32).rearrange("p k o -> p (k o)"), dest_f[:, :]).then_inc(s.row_s, 1)
                dve.wait_ge(s.row_s, p.count(2, 1))
                dve.tensor_scalar(dest_f[:, :], dest_f[:, :], float(P), None, ALU.add).then_inc(s.row_s, 1)

            def latent_lo(n):
                dve.wait_ge(s.hi_q, n.count(3, 1))
                dve.tensor_tensor(ks[:, 1, 0:C], t_ps[:, 1, 0:C], ks[:, 0, 0:C], ALU.subtract).then_inc(s.lo_q, 1)

            def query_lo(n):
                for g in range(2):
                    dve.wait_ge(s.hi_q, n.count(3, 2 + g))
                    hs_ = slice(8 * g, 8 * g + 8)
                    dve.tensor_tensor(qs[:, 1, hs_, 0:NOPE], s_ps[:, g, :].rearrange("p (h r) -> p h r", r=NOPE),
                                      qs[:, 0, hs_, 0:NOPE], ALU.subtract).then_inc(s.lo_q, 1)

            def qT_copies(n):
                par = n.off % 2
                if n.at(-1).exists():
                    dve.wait_ge(s.pv_made, n.at(-1).units(1, UNITS[n.at(-1).i] - 1, 1))
                dve.wait_ge(s.lo_q, n.count(3, 3))
                dve.tensor_copy(ckv[:, :, n.i, :], ks[:, :, 0:C]).then_inc(s.ckv_ready, 1)
                dve.wait_ge(s.qT_made, n.count(5, 2))
                dve.tensor_copy(qT[:, par, 0, 1024:2048], tt[1]).then_inc(s.qT_dve, 1)
                dve.wait_ge(s.qT_made, n.count(5, 4))
                dve.tensor_copy(qT[:, par, 1, 1024:2048], st[3]).then_inc(s.qT_dve, 1)

            def out_norm(p):
                dve.wait_ge(s.pv_made, p.units(1, UNITS[p.i] - 1, 1))
                if p.at(-1).exists():
                    dve.wait_ge(s.lo_o, p.at(-1).count(1, 1))
                sums = ssum[:, p.off % 2, 0, :]
                if GROUP[p.i] == 1:
                    dve.tensor_tensor(sums, sums, ssum[:, p.off % 2, 1, :], ALU.add).then_inc(s.o_evs, 1)
                else:
                    dve.sem_inc(s.o_evs, 1)
                dve.wait_ge(s.o_evs, p.count(2, 1))
                dve.reciprocal(rsum[:, :], sums).then_inc(s.o_evs, 1)
                dve.wait_ge(s.o_evs, p.count(2, 2))
                dve.tensor_tensor(o_sb[:, :].rearrange("p (h c) -> p h c", c=C), o_flat.rearrange("p (h c) -> p h c", c=C),
                                  rsum[:, :].unsqueeze(2).broadcast_to([P, H, C]), ALU.mult).then_inc(s.o_ready, 1)

            def oT_copy(p):
                dve.wait_ge(s.oT_made, p.count(2, 2))
                dve.tensor_copy(oT[:, 1, :, :].rearrange("p k n -> p (k n)"), ot[1]).then_inc(s.oT_dve, 1)

            def residual(p):
                dve.wait_ge(s.proj_made, p.count(1, 1))
                dve.scalar_tensor_tensor(x1[:, p.off % 2, :], t_ps[:, 0, 0:D], f_out, x_sb[:, p.off % 4, :],
                                         ALU.mult, ALU.add).then_inc(s.x1_done, 1)

            def maxima(t, u, par):
                i, G = t.i, GROUP[t.i]
                L = (i + 1) * P
                w = s_off(i, 1) if G > 1 else L
                flat = s_ps[:, :, :].rearrange("p a n -> p (a n)")
                view = flat[:, 1024 * par:1024 * par + G * w].rearrange("p (g n) -> p g n", g=G)[:, :, 0:L]
                dve.wait_ge(s.s_made, t.units(1, u, 1))
                dve.tensor_reduce(smax[:, par, 0:G], view, AX_X, ALU.max).then_inc(s.maxs, 1)
                dve.wait_ge(s.maxs, t.units(1, u, 1))
                dve.tensor_scalar(nmax[:, par, 0:G], smax[:, par, 0:G], f_natt, None, ALU.mult).then_inc(s.max_ready, 1)

            def attention(t):
                def unit(u, par):
                    for h in range(2):
                        w = P * len(half_tiles(t.i, h))
                        dve.wait_ge(s.hi_p, t.units(2, u, h + 1))
                        dve.tensor_tensor(pT[:, par, 1, h, 0:w], t_ps[:, h, 0:w], pT[:, par, 0, h, 0:w],
                                          ALU.subtract).then_inc(s.lo_p, 1)
                        if h == MAX_AFTER and has_next(t, u, 2):
                            maxima(t, u + 2, par)
                    if isinstance(u, int) and u == 0:
                        early_steps(t)
                for u in range(2):
                    maxima(t, u, u)
                att_loop(dve, t, unit)

            def early_steps(t):
                if t.at(-2).exists():
                    slots(t.at(-2))
                if t.at(2).exists() or t.at(-1).exists():
                    norm_stats(t.at(2), t.at(-1))

            def hidden(p):
                dve.wait_ge(s.gate_done, p.count(1, 1))
                dve.scalar_tensor_tensor(hid[:, :], gate[:, :], 1.0, s_ps[:, 0, 0:SI], ALU.add, ALU.mult).then_inc(s.hids, 1)
                dve.wait_ge(s.hids, p.count(1, 1))
                dve.scalar_tensor_tensor(hid[:, :], hid[:, :], HSCALE, s_ps[:, 1, 0:SI], ALU.mult, ALU.mult).then_inc(s.hid_done, 1)
                dve.wait_ge(s.hi_h, p.count(1, 1))
                dve.tensor_tensor(hs[:, 1, :], hid[:, :], hs[:, 0, :], ALU.subtract).then_inc(s.lo_h, 1)

            def tile_at(ap, p):
                return ap[:, ds(p.off if p.b is None else p.b * TB + p.off, 1), :].rearrange("p a n -> p (a n)")

            def logits(p, st_):
                dve.wait_ge(s.lgt_made, p.count(1, 1))
                st_.do(dve.tensor_scalar(lg[:, p.off % 2, :], o_ps[:, 1, 0:E], wamp[:, A_R:A_R + 1], None, ALU.mult), own_wait)

            def router(p, st_):
                par = p.off % 2
                lg_t, top_t = lg[:, par, :], top8[:, par, :]
                st_.do(dve.max(top_t, lg_t), own_wait)
                st_.do(dve.max_index(top_ix[:, par, :], top_t, lg_t))
                dve.tensor_copy(tile_at(lg_all, p), lg_t)
                dve.tensor_copy(tile_at(top_all, p), top_t[:, 0:TOPK])
                st_.do(dve.tensor_copy(ixf[:, :], top_ix[:, par, 0:2]))
                for k in range(TOPK):
                    st_.do(dve.tensor_scalar(pick[:, par, k, :], iota_e_sb[:, :], ixf[:, k:k + 1], None, ALU.is_equal))
                dve.tensor_tensor(picked[:, par, :], pick[:, par, 0, :], pick[:, par, 1, :], ALU.add).then_inc(s.mask_ready, 1)

            def slots(q):
                par = q.off % 2
                dve.wait_ge(s.down_made, q.count(1, 1))
                if q.at(-2).exists():
                    dve.wait_ge(stored[par], q.at(-2).pair(16))
                dve.scalar_tensor_tensor(den[:, par, :], o_ps[:, 0, D:2 * D], f_sd, x1[:, par, :], ALU.mult, ALU.add).then_inc(s.dense_done, 1)
                st_ = Steps(dve, s.slot_s, 5, q.count)
                st_.do(dve.tensor_tensor(place[:, :], o_ps[:, 0, 0:E], used[:, :], ALU.add))
                st_.do(dve.tensor_tensor(used[:, :], used[:, :], o_ps[:, 0, E:2 * E], ALU.add))
                for k in range(TOPK):
                    st_.do(dve.tensor_tensor_reduce(place_k[:, :], pick[:, par, k, :], place[:, :], 1.0, 0.0, ALU.mult, ALU.add,
                                                    slot_f[:, k:k + 1]))
                if q.at(-2).exists():
                    dve.wait_ge(scattered[par], q.at(-2).pair(32))
                st_.do(dve.tensor_copy(slot[:, par, :], slot_f[:, :]))
                dve.sem_inc(s.slot_done, 1)

            norm_stats(Tile(0), None)
            norm_stats(Tile(1), None)
            latent_lo(Tile(0))
            query_lo(Tile(0))
            qT_copies(Tile(0))

            def section(t):
                n = t.at(1)
                if n.exists():
                    latent_lo(n)
                if t.at(-1).exists():
                    oT_copy(t.at(-1))
                if n.exists():
                    query_lo(n)
                if t.at(-1).exists():
                    residual(t.at(-1))
                if t.exists():
                    attention(t)
                    out_norm(t)
                else:
                    early_steps(t)
                if n.exists():
                    qT_copies(n)
                if t.at(-1).exists():
                    steps = Steps(dve, s.route_s, 6, t.at(-1).count)
                    logits(t.at(-1), steps)
                    hidden(t.at(-1))
                    expert_rows(t.at(-1))
                    router(t.at(-1), steps)
            sections(dve, section)

            dve.memset(pad[:, 0:2 * D], 0.0)
            dve.memset(pad[:, 2 * D:ROW].bitcast(I32), 2 * NY)
            dve.tensor_copy(free_i[:, :], used[0:1, :]).then_inc(s.used_ready, 1)
            st_ = Steps(dve, s.tail_s, 15, at)
            st_.do(dve.tensor_scalar(cnt[:, :], iota_e_sb[:, :], -float(LIST), None, ALU.mult))
            st_.do(dve.tensor_tensor(cnt[:, :], cnt[:, :], used[:, :], ALU.add))
            st_.do(dve.tensor_tensor(cmp_k[:, :, :], cnt[:, :].unsqueeze(2).broadcast_to([P, E, NT]), iota_k_sb[:, :, :], ALU.is_gt))
            st_.do(dve.tensor_reduce(tiles_e[:, :], cmp_k[:, :, :], AX_X, ALU.add))
            st_.do(dve.tensor_tensor_scan(ends[:, :], ones_e[:, :], tiles_e[:, :], 0.0, ALU.mult, ALU.add))
            st_.do(dve.tensor_scalar(jump[:, :], tiles_e[:, :], -float(P), float(LIST), ALU.mult, ALU.add))
            st_.do(dve.tensor_tensor(ge[:, :, :], iota_n_sb[:, :].unsqueeze(2).broadcast_to([1, NMT, E]),
                                     ends[0:1, :].unsqueeze(1).broadcast_to([1, NMT, E]), ALU.is_ge))
            st_.do(dve.tensor_reduce(t_exp[:, :], ge[:, :, :], AX_X, ALU.add))
            st_.do(dve.tensor_tensor(ge2[:, :, :], ge[:, :, :], jump[0:1, :].unsqueeze(1).broadcast_to([1, NMT, E]), ALU.mult))
            st_.do(dve.tensor_reduce(t_row[:, :], ge2[:, :, :], AX_X, ALU.add))
            st_.do(dve.scalar_tensor_tensor(t_row[:, :], iota_n_sb[:, :], float(P), t_row[:, :], ALU.mult, ALU.add))
            st_.do(dve.tensor_scalar(t_row[:, :], t_row[:, :], float(DUMMY), None, ALU.min))
            st_.do(dve.tensor_scalar(t_exp[:, :], t_exp[:, :], float(E - 1), None, ALU.min))
            st_.do(dve.tensor_copy(tab[:, 0, :], t_row[:, :]))
            st_.do(dve.tensor_copy(tab[:, 1, :], t_exp[:, :]))
            dve.sem_inc(s.tab_ready, 1)

            dve.wait_ge(s.w_gu, 32)
            dve.wait_ge(s.w_d, 32)
            dve.wait_ge(s.c_ready, 1)
            link(dve.tensor_reduce(amax[:, A_GU:A_GU + 1], ga, AX_X, ALU.max, apply_absolute_value=True))
            link(dve.tensor_reduce(amax[0:KE, A_D:A_D + 1], gb[0:KE], AX_X, ALU.max, apply_absolute_value=True))
            dve.sem_inc(s.gu_amax, 1)
            dve.wait_ge(s.gu_red, 1)
            scales(slice(6, 8))
            dve.tensor_scalar(f_guh, wamp[:, A_GU:A_GU + 1], 0.5, None, ALU.mult)
            link(dve.tensor_scalar(f_ed, wamp[:, A_GU:A_GU + 1], wamp[:, A_GU:A_GU + 1], 0.5 / HSCALE, ALU.mult, ALU.mult))
            link(dve.tensor_scalar(f_ed, f_ed, wamp[:, A_D:A_D + 1], None, ALU.mult))
            dve.sem_inc(s.gu_scale, 1)
            NG = E // GC
            for k in range(KD):
                with dve.Fori(0, NG) as m:
                    dve.wait_ge(s.gu_prep, m + (1 + k * NG))
                    dve.tensor_copy(wgu_sb[:, k, ds(m * GC, GC), 0, :], gu_w).then_inc(s.gu_amax, 1)
                    dve.tensor_copy(wd_sb[0:KE, k, ds(m * GC, GC), 0, :], d_w[0:KE]).then_inc(s.gu_amax, 1)
                    dve.wait_ge(s.gu_amax, m * 2 + (3 + k * 2 * NG))
                    dve.tensor_tensor(wgu_sb[:, k, ds(m * GC, GC), 1, :], gu_w, wgu_sb[:, k, ds(m * GC, GC), 0, :], ALU.subtract)
                    dve.tensor_tensor(wd_sb[0:KE, k, ds(m * GC, GC), 1, :], d_w[0:KE],
                                      wd_sb[0:KE, k, ds(m * GC, GC), 0, :], ALU.subtract).then_inc(s.gu_hi, 1)
            dve.wait_ge(s.gu_hi, 1 + KD * NG)
            dve.sem_inc(s.gu_lo, 1)

            link(dve.tensor_tensor(w_d[:, :, :], lg_all[:, :, :], top_all[:, :, 0:1].broadcast_to([P, NT, E]), ALU.subtract))
            link(dve.tensor_tensor(w_t[:, :], top_all[:, :, 1], top_all[:, :, 0], ALU.subtract))
            dve.sem_inc(s.c_w, 1)

            def expert_hidden(n, par):
                dve.wait_ge(s.m_gate, n + 1)
                dve.scalar_tensor_tensor(m_m[:, :], m_g[:, :], 1.0, s_ps[:, 2 * par, 0:I_E], ALU.add, ALU.mult).then_inc(s.m_q, 1)
                dve.wait_ge(s.m_q, n + 1)
                dve.scalar_tensor_tensor(m_h[:, par, :], m_m[:, :], HSCALE, s_ps[:, 2 * par + 1, 0:I_E], ALU.mult,
                                         ALU.mult).then_inc(s.m_hid, 1)
                dve.wait_ge(s.m_hi, n + 1)
                dve.tensor_tensor(m_hs[:, par, 1, :], m_h[:, par, :], m_hs[:, par, 0, :], ALU.subtract).then_inc(s.m_lo, 1)

            def hT_copy(n):
                dve.wait_ge(s.m_hT, n + 1)
                dve.tensor_copy(m_hT_sb[:, :, :, :].rearrange("p a k n -> p (a k n)"), ot[0][0:KE, 0:4 * P]).then_inc(s.m_hTs, 1)

            expert_hidden(0, 0)
            expert_hidden(1, 1)
            with dve.Fori(0, NMT // XB - 1) as m:
                for q in range(XB):
                    n = m * XB + q
                    hT_copy(n)
                    expert_hidden(n + 2, q % 2)
            for n in range(NMT - XB, NMT):
                hT_copy(n)
                if n + 2 < NMT:
                    expert_hidden(n + 2, n % 2)

            dve.wait_ge(s.w_exp, 2)
            link(dve.tensor_reduce(w_s[:, :], w_e[:, :, :], AX_X, ALU.add))
            link(dve.reciprocal(w_k[:, :, 0], w_s[:, :]))
            link(dve.tensor_tensor(w_k[:, :, 1], w_k[:, :, 0], w_t[:, :], ALU.mult))

            NC = NT // CT
            with dve.Fori(0, NC // 2) as m:
                for q in range(2):
                    dve.wait_ge(c_loaded[q], m * 48 + 48)
                    dve.wait_ge(c_out[q], m * 16 + 16)
                    for k in range(TOPK):
                        for c in range(CT):
                            w = w_k[:, ds(m * (2 * CT) + q * CT + c, 1), k]
                            last = dve.scalar_tensor_tensor(c_o[:, q, c, :], c_in[:, q, 1 + k, c, :], w,
                                                            c_in[:, q, 0, c, :] if k == 0 else c_o[:, q, c, :], ALU.mult, ALU.add)
                        if k == 0:
                            last.then_inc(s.c_y0, 1)
                            dve.wait_ge(s.c_y0, m * 2 + q + 1)
                    last.then_inc(s.c_sum, 1)

        @block.gpsimd
        def _(pool):
            pool.wait_ge(s.amax_ready, 1)
            pool.partition_all_reduce(amax_all[:, 0:6], amax[:, 0:6], P, bass.bass_isa.ReduceOp.max).then_inc(s.amax_reduced, 1)

            def rope(n):
                st_ = Steps(pool, s.rope_s, 6, n.count)
                cos_b = cos_sb[:, n.i, :].unsqueeze(1).broadcast_to([P, H + 1, ROPE])
                pool.wait_ge(s.pe_ready, n.count(1, 1))
                st_.do(pool.tensor_tensor(rot, pe, cos_b, ALU.mult))
                for k in range(2):
                    sin_b = sin_sb[:, n.i, k:ROPE:2].unsqueeze(1).broadcast_to([P, H + 1, ROPE // 2])
                    st_.do(pool.tensor_tensor(rot2[:, :, k:ROPE:2], pe[:, :, 1 - k:ROPE:2], sin_b, ALU.mult))
                st_.do(pool.tensor_tensor(rot, rot, rot2, ALU.add), own_wait)
                st_.do(pool.tensor_copy(ks[:, 0, C:HD], rot[:, H, :]), own_wait)
                st_.do(pool.tensor_copy(qs[:, 0, :, NOPE:HD], rot[:, 0:H, :]))
                pool.tensor_tensor(ks[:, 1, C:HD], rot[:, H, :], ks[:, 0, C:HD], ALU.subtract)
                pool.tensor_tensor(qs[:, 1, :, NOPE:HD], rot[:, 0:H, :], qs[:, 0, :, NOPE:HD], ALU.subtract).then_inc(s.rope_done, 1)

            def norm(n, p):
                has_p = p is not None and p.exists()
                k0, k1 = (0 if n.exists() else 1), (2 if has_p else 1)
                w = [ln_w[:, a, k0:k1] for a in range(3)]
                var, y, u = w
                st_ = Steps(pool, s.ln_s, LN_STEPS, n.count)
                pool.wait_ge(s.stats, n.count(1, 1))
                own_wait(pool)
                st_.do(pool.tensor_scalar(var, ln_mv[:, k0:k1, 1], EPS, None, ALU.add), own_wait)
                st_.do(pool.tensor_scalar(y.bitcast(I32), var.bitcast(I32), -0.5, SEED, ALU.mult, ALU.add))
                for _ in range(NEWTON):
                    st_.do(pool.tensor_tensor(u, y, var, ALU.mult))
                    st_.do(pool.tensor_tensor(u, u, y, ALU.mult), own_wait)
                    st_.do(pool.tensor_scalar(u, u, -0.5, 1.5, ALU.mult, ALU.add))
                    st_.do(pool.tensor_tensor(y, y, u, ALU.mult))
                parts = []
                if n.exists():
                    pool.wait_ge(s.xT_made, n.at(-2).count(1, 1)) if n.at(-2).exists() else None
                    parts.append((0, x_sb[:, n.off % 4, :], xs[:, n.off % 2, 0, :], xs[:, n.off % 2, 1, :], n, s.ln1_done))
                if has_p:
                    if p.at(-2).exists():
                        pool.wait_ge(scattered[p.off % 2], p.at(-2).pair(32))
                    row = xs2[:, p.off % 2, 0]
                    parts.append((1, x1[:, p.off % 2, :], row[:, 0:D], row[:, D:2 * D], p, s.ln2_done))
                own_wait(pool)
                for k, src, hi, lo, tile, done in parts:
                    pool.tensor_scalar(xn[:, :], src, ln_mv[:, k, 0:1], ln_w[:, 1, k:k + 1], ALU.subtract, ALU.mult).then_inc(xn_s[k], 1)
                    pool.wait_ge(xn_s[k], tile.count(1, 1))
                    own_wait(pool)
                    pool.tensor_copy(hi, xn[:, :]).then_inc(done, 1)
                    pool.wait_ge(done, tile.count(2, 1))
                    pool.tensor_tensor(lo, xn[:, :], hi, ALU.subtract).then_inc(done, 1)
                    pool.wait_ge(done, tile.count(2, 2))
                    own_wait(pool)
                pool.sem_inc(s.normed, 1)

            def out_lo(p):
                pool.wait_ge(s.hi_o, p.count(1, 1))
                pool.tensor_tensor(os_[:, 1, :], o_sb[:, :], os_[:, 0, :], ALU.subtract).then_inc(s.lo_o, 1)

            def scatter(q):
                par = q.off % 2
                pool.wait_ge(s.slot_done, q.count(1, 1))
                own_wait(pool)
                for k in range(TOPK):
                    pool.indirect_dma_start(lists, bass.IndirectOffsetOnAxis(slot[:, par, k:k + 1], 0), xs2[:, par, k, :],
                                            None).then_inc(scattered[par], 16)

            norm(Tile(0), None)
            norm(Tile(1), None)
            rope(Tile(0))

            def section(t):
                n = t.at(1)
                if n.exists():
                    rope(n)
                if t.at(2).exists() or t.at(-1).exists():
                    norm(t.at(2), t.at(-1))
                if t.at(-2).exists():
                    scatter(t.at(-2))
                if t.exists():
                    out_lo(t)
            sections(pool, section)

            pool.wait_ge(s.gu_amax, 1)
            pool.partition_all_reduce(amax_all[:, 6:8], amax[:, 6:8], P, bass.bass_isa.ReduceOp.max).then_inc(s.gu_red, 1)

            def send(n, q):
                pool.wait_ge(s.m_y, n + 2)
                own_wait(pool)
                pool.indirect_dma_start(y_exp, bass.IndirectOffsetOnAxis(xg[:, q, 2 * D:ROW].bitcast(I32), 0), m_ys[:, q % YB, :],
                                        None, bounds_check=NY - 1, oob_is_err=False).then_inc(m_out[q], 16)
            with pool.Fori(0, NMT // XB) as m:
                for q in range(XB):
                    send(m * XB + q, q)


def kernel(**inputs):
    import concourse.bacc as bacc
    from concourse import mybir as mb
    from concourse.bass_utils import run_bass_kernel_spmd

    g = {n: np.asarray(a) for n, a in inputs.items()}
    tr = lambda a, *ax: np.ascontiguousarray(np.transpose(a, ax))
    wqb = g["L0_attn_Wqb"].reshape(QL, H, HD)
    wkvb = g["L0_attn_Wkvb"].reshape(C, H, NOPE + VD)
    inv_freq = np.float32(1.0) / np.float32(10000.0) ** (np.arange(ROPE // 2, dtype=np.float32) * np.float32(2.0) / np.float32(ROPE))
    ang = np.arange(S, dtype=np.float32)[:, None] * inv_freq[None, :].astype(np.float32)
    cos = np.repeat(np.cos(ang), 2, axis=1).astype(np.float32)
    sin = np.stack([-np.sin(ang), np.sin(ang)], axis=-1).reshape(S, ROPE).astype(np.float32)
    q_at, k_at = np.arange(P)[:, None], np.arange(P)[None, :]
    arrays = {
        "x": np.ascontiguousarray(g["L0_attn_hidden_states"].reshape(NT * P, D)),
        "wqaT": tr(g["L0_attn_Wqa"], 1, 0),
        "wqb_peT": np.ascontiguousarray(wqb[:, :, NOPE:].reshape(QL, H * ROPE)),
        "wqb_nopeT": tr(wqb[:, :, :NOPE], 2, 1, 0),
        "wkva": np.ascontiguousarray(g["L0_attn_Wkva"]),
        "wkT": tr(wkvb[:, :, :NOPE], 2, 1, 0),
        "wvT": tr(wkvb[:, :, NOPE:], 2, 1, 0),
        "wo": np.ascontiguousarray(g["L0_attn_Wo"]),
        "gateT": tr(g["L0_ffn_gate_w"], 1, 0),
        "wgu": np.ascontiguousarray(g["L0_ffn_w_gate_up"]),
        "wd": np.ascontiguousarray(g["L0_ffn_w_down"]),
        "wsg": np.ascontiguousarray(g["L0_ffn_shared_gate_up"]),
        "wsd": np.ascontiguousarray(g["L0_ffn_shared_down"]),
        "cos_t": tr(cos.reshape(TB, P, ROPE), 1, 0, 2),
        "sin_t": tr(sin.reshape(TB, P, ROPE), 1, 0, 2),
        "ident": np.eye(P, dtype=np.float32),
        "causal": np.where(k_at > q_at, np.float32(-3e38), np.float32(0)).astype(np.float32),
        "tri": (q_at < k_at).astype(np.float32),
        "iota_e": np.tile(np.arange(E, dtype=np.float32), (P, 1)),
        "iota_k": np.tile((np.arange(NT, dtype=np.float32) * P), (P, E, 1)),
        "iota_n": np.arange(NMT, dtype=np.float32)[None, :],
        "tok_ids": (np.arange(P)[:, None] + np.arange(TOPK)[None, :] * (NT * P)).astype(np.float32),
    }
    nc = bacc.Bacc("TRN2", target_bir_lowering=False, num_devices=1)
    aps = [nc.dram_tensor(n, a.shape, mb.dt.from_np(a.dtype), kind="ExternalInput").ap() for n, a in arrays.items()]
    out = nc.dram_tensor("layer_out", (NT * P, D), F32, kind="ExternalOutput").ap()
    build(nc, *aps, out)
    r = run_bass_kernel_spmd(nc, [arrays], core_ids=[0])
    return r.results[0]["layer_out"].reshape(B, S, D)
```

```python
from collections import namedtuple
from contextlib import ExitStack

import numpy as np

import concourse.bass as bass
from concourse import mybir

ALU = mybir.AluOpType
ACT = mybir.ActivationFunctionType
AX_X = mybir.AxisListType.X
F32, F16, BF16 = mybir.dt.float32, mybir.dt.float16, mybir.dt.bfloat16
I32, U32 = mybir.dt.int32, mybir.dt.uint32
ds = bass.ds

P = 128
B, S, D = 4, 1024, 256
H, QL, NOPE, ROPE, VD = 16, 192, 64, 64, 128
C = 64
HD = NOPE + ROPE
TB = S // P
NT = B * TB
KD = D // P
NQ = H * HD
E, I_E, TOPK = 16, 176, 2
SI = 2 * I_E
KE = 88
EPS = 1e-5
LIST = NT * P + P
DUMMY = E * LIST
NMT = (NT * P * TOPK) // P + E
ROW = 2 * D + 2
NY = TOPK * NT * P
WMAX = 64.0
HSCALE = 2.0 ** -15
GROUP = [8, 4, 2, 2, 1, 1, 1, 1]
UNITS = [H // g for g in GROUP]


def shares_rope(n):
    return n.i in (1, 2) or (n.b is None and n.off == 0)


def shifted(i, u):
    return UNITS[i] == 2 and isinstance(u, int) and u == 0


SHORT = [u <= 4 for u in UNITS]
EARLY_NORMS = [u > 2 for u in UNITS]
UB = sum(UNITS)
UPRE = [sum(UNITS[:i]) for i in range(TB)]
LN_STEPS = 14
NEWTON = 3
SPLIT_MAX = [g > 1 or i >= 6 for i, g in enumerate(GROUP)]
SEED = 1597463007.0
A_Q, A_KV, A_O, A_SG, A_SD, A_R, A_GU, A_D = range(8)


class Tile:

    def __init__(self, off, b=None):
        self.off, self.b = off, b
        self.i = off % TB

    def at(self, k):
        return Tile(self.off + k, self.b)

    def count(self, per, k):
        return per * self.off + k if self.b is None else self.b * (per * TB) + (per * self.off + k)

    def pair(self, per):
        n = per * (self.off // 2 + 1)
        return n if self.b is None else self.b * (per * TB // 2) + n

    def units(self, per, u, k):
        n = per * (UB * (self.off // TB) + UPRE[self.i]) + k
        n = n + per * u
        return n if self.b is None else self.b * (per * UB) + n

    def row(self):
        return P * self.off if self.b is None else self.b * (P * TB) + P * self.off

    def exists(self):
        return self.b is not None or 0 <= self.off < NT


class Steps:

    def __init__(self, eng, sem, per, first):
        self.eng, self.sem, self.per, self.first, self.n = eng, sem, per, first, 0

    def do(self, ins, after_wait=None):
        self.n += 1
        assert self.n <= self.per
        ins.then_inc(self.sem, 1)
        self.eng.wait_ge(self.sem, self.first(self.per, self.n))
        if after_wait is not None:
            after_wait(self.eng)


PEEL = 4


def sections(eng, emit):
    for off in range(PEEL):
        emit(Tile(off))
    with eng.Fori(0, B - 1) as b:
        for off in range(PEEL, PEEL + TB):
            emit(Tile(off, b))
    for off in range((B - 1) * TB + PEEL, NT + 2):
        emit(Tile(off))


def build(nc, x, wqaT, wqb_peT, wqb_nopeT, wkva, wkT, wvT, wo, gateT, wgu, wd, wsg, wsd,
          cos_t, sin_t, ident, causal, tri, iota_e, iota_k, iota_p, tok_ids, out):
    nc.disable_value_cache = True
    ctx = ExitStack()
    with ctx:
        def sb(name, shape, dt):
            return ctx.enter_context(nc.sbuf_tensor(name, shape, dt))

        def sem(name):
            return ctx.enter_context(nc.semaphore(name))

        lists = nc.dram_tensor("lists", [DUMMY + P, ROW], F16, kind="Internal").ap()
        y_exp = nc.dram_tensor("y_exp", [NY, D], F32, kind="Internal").ap()
        dense = nc.dram_tensor("dense", [NT * P, D], F32, kind="Internal").ap()

        cos_sb = sb("cos_sb", [P, TB, ROPE], F32)
        sin_sb = sb("sin_sb", [P, TB, ROPE], F32)
        id32 = sb("id32", [P, P], F32)
        id16 = sb("id16", [P, P], F16)
        idbf = sb("idbf", [P, P], BF16)
        maskbf = sb("maskbf", [P, P], BF16)
        tri16 = sb("tri16", [P, P], F16)
        ones16 = sb("ones16", [P, P], F16)
        iota_e_sb = sb("iota_e_sb", [P, E], F32)
        iota_k_sb = sb("iota_k_sb", [P, E, NT], F32)
        iota_p_sb = sb("iota_p_sb", [P, 1], F32)
        shapes = [(2, KD, NQ + 2 * C), (2, H // 2, D), (2, KD, 2 * SI), (2, 3, D)]
        sizes = [int(np.prod(sh)) for sh in shapes]
        weights = sb("weights", [P, sum(sizes)], F16)
        starts = [sum(sizes[:k]) for k in range(len(sizes))]
        wq, wout, wsg_sb, wsd_sb = (weights[:, a:a + n].rearrange("p (s k n) -> p s k n", s=2, k=sh[1])
                                    for a, n, sh in zip(starts, sizes, shapes))
        dense_sb = weights[:, 0:2 * NT * D].bitcast(F32).rearrange("p (t n) -> p t n", t=NT)
        wr_sb = sb("wr_sb", [P, 2, KD, E], F16)
        wgu_sb = sb("wgu_sb", [P, KD, E, 2, 2 * I_E], F16)
        wd_sb = sb("wd_sb", [P, 2, E, 2, D], F16)
        amax = sb("amax", [P, 8], F32)
        amax_all = sb("amax_all", [P, 8], F32)
        winv = sb("winv", [P, 8], F32)
        wamp = sb("wamp", [P, 8], F32)
        fac = sb("fac", [P, 8], F32)
        f_att, f_natt, f_out, f_sgh, f_sd, f_guh, f_ed = (fac[:, k:k + 1] for k in range(7))
        amax_kv = sb("amax_kv", [P, KD], F32)
        amax_q = sb("amax_q", [P, 8], F32)
        amax_e = sb("amax_e", [P, 16], F32)
        amax_o = sb("amax_o", [P, 8], F32)

        x_sb = sb("x_sb", [P, 4, D], F32)
        ln_st = sb("ln_st", [P, 2, 8], F32)
        ln_mv = sb("ln_mv", [P, 2, 2], F32)
        ln_w = sb("ln_w", [P, 3, 2], F32)
        xn = sb("xn", [P, D], F32)
        xs = sb("xs", [P, 2, 2, D], F16)
        xT = sb("xT", [P, 2, 2, KD, P], F16)
        NPE = (H + 1) * ROPE
        work = sb("work", [P, 3 * NPE + H * HD + HD], F32)
        pe = work[:, 0:NPE].rearrange("p (h r) -> p h r", r=ROPE)
        rot = work[:, NPE:2 * NPE].rearrange("p (h r) -> p h r", r=ROPE)
        rot2 = work[:, 2 * NPE:3 * NPE].rearrange("p (h r) -> p h r", r=ROPE)
        qs = work[:, 3 * NPE:3 * NPE + H * HD].bitcast(F16).rearrange("p (s h d) -> p s h d", s=2, h=H)
        ks = work[:, 3 * NPE + H * HD:].bitcast(F16).rearrange("p (s d) -> p s d", s=2)
        qT = sb("qT", [P, 2, 2, H * P], F16)
        kT = sb("kT", [P, 2, S], F16)
        ckv = sb("ckv", [P, 2, TB, C], F16)
        probs = sb("probs", [P, 2, S], F32)
        pT = sb("pT", [P, 2, 2, 2, 512], F16)
        smax = sb("smax", [P, 2, 8], F32)
        nmax = sb("nmax", [P, 2, 8], F32)
        ssum = sb("ssum", [P, 2, 2, H], F32)
        rsum = sb("rsum", [P, H], F32)
        o_sb = probs[:, 0, :]
        oT = probs[:, 1, :].bitcast(F16).rearrange("p (a k n) -> p a k n", a=2, k=H // 2)
        os_ = pT[:, 1, :, :, :].rearrange("p a g n -> p a (g n)")
        x1 = sb("x1", [P, 2, D], F32)
        xs2 = sb("xs2", [P, 2, TOPK, ROW], F16)
        x2T = sb("x2T", [P, 2, KD, P], F16)
        gate = sb("gate", [P, SI], F32)
        hid = sb("hid", [P, SI], F32)
        hs = sb("hs", [P, 2, SI], F16)
        hT = sb("hT", [P, 2, 3, P], F16)
        den = sb("den", [P, 2, D], F32)
        lg_all = sb("lg_all", [P, NT, E], F32)
        top_all = sb("top_all", [P, NT, TOPK], F32)
        lg = sb("lg", [P, 2, E], F32)
        top8 = sb("top8", [P, 2, 8], F32)
        top_ix = sb("top_ix", [P, 2, 8], U32)
        ixf = sb("ixf", [P, 2], F32)
        pick = sb("pick", [P, 2, TOPK, E], F32)
        picked = sb("picked", [P, 2, E], F16)
        place = sb("place", [P, E], F32)
        place_k = sb("place_k", [P, TOPK, E], F32)
        slot_f = sb("slot_f", [P, TOPK], F32)
        slot = sb("slot", [P, 2, TOPK], I32)
        used = sb("used", [P, E], F32)
        dest_f = sb("dest_f", [P, TOPK], F32)

        s_ps = ctx.enter_context(nc.psum_tensor("s_ps", [P, 4, 512], F32))
        t_ps = ctx.enter_context(nc.psum_tensor("t_ps", [P, 2, 512], F32))
        o_ps = ctx.enter_context(nc.psum_tensor("o_ps", [P, 2, 512], F32))
        tt = [t_ps[:, g, :].bitcast(F16) for g in range(2)]
        st = [s_ps[:, g, :].bitcast(F16) for g in range(4)]
        ot = [o_ps[:, g, :].bitcast(F16) for g in range(2)]
        o_flat = o_ps[:, :, :].rearrange("p a n -> p (a n)")

        names = """c_in w_k w_a w_o w_b c_ready qb_made qb_copied wq_made wq_copied wo_made wo_copied prep
                   amax_ready amax_reduced scales hi_made lo_made w_gu w_d
                   stat_s stats ln_s normed row_s ln1_done xT_made xT_ready q_made hi_q lo_q pe_ready rope_s rot_s rope_done
                   qT_made qT_act qT_dve ckv_ready s_made maxs max_ready exp_done p_made hi_p lo_p pv_made
                   o_evs o_ready hi_o lo_o oT_made oT_act oT_dve proj_made x1_done ln2_done x2T_made x2T_ready
                   gu_made lgt_made gate_done hids hid_done hi_h lo_h route_s mask_ready rank_made slot_s slot_done
                   hT_made hT_ready down_made dense_done
                   used_ready pads tail_s tab_ready tab_made tab_turned gu_amax gu_red gu_scale split
                   m_xT m_xTs m_gu m_gate m_q m_hid m_hi m_lo m_hT m_hTs m_down m_y
                   passed c_w w_exp c_sum c_y0 c_out dense_in""".split()
        s = namedtuple("Signals", names)(*(sem(n) for n in names))
        xin = [sem(f"x_in{k}") for k in range(4)]
        xn_s = [sem(f"xn_made{k}") for k in range(2)]
        scattered = [sem(f"scattered{k}") for k in range(2)]
        stored = [sem(f"stored{k}") for k in range(2)]
        xg_in = [sem(f"xg_in{k}") for k in range(8)]
        m_out = [sem(f"m_out{k}") for k in range(8)]
        c_loaded = [sem(f"c_loaded{k}") for k in range(8)]

        ga = wgu_sb[:, :, :, :, :].rearrange("p k e s j -> p (k e s j)").bitcast(F32)
        gb = wd_sb[:, :, :, :, :].rearrange("p k e s j -> p (k e s j)").bitcast(F32)

        def cut(view, at, *shape):
            n = int(np.prod(shape))
            v = view[:, at:at + n]
            return (v.rearrange("p (a b) -> p a b", a=shape[0]) if len(shape) == 2 else v), at + n

        r_wqaT, at = cut(ga, 0, 2, D)
        r_pe, at = cut(ga, at, 2, H * ROPE)
        r_nopeT, at = cut(ga, at, H, QL)
        r_wkT, at = cut(ga, at, H, C)
        r_qb, at = cut(ga, at, 2, H * C)
        r_wvT, at = cut(ga, at, H, C)
        r_wsd, at = cut(ga, at, 3, D)
        r_wo, at = cut(gb, 0, H, D)
        r_out, at = cut(gb, at, H // 2, D)
        r_wsg, at = cut(gb, at, KD, 2 * SI)
        r_wr, at = cut(gb, at, KD, E)
        r_wq = work[:, 0:KD * (NQ + 2 * C)].rearrange("p (k n) -> p k n", k=KD)
        QLB = QL - P
        WQ_ORDER = (2, 3, 0, 1)
        SPLITS = [
            *((r_wq[:, k, 0:NQ], wq[:, 0, k, 0:NQ], wq[:, 1, k, 0:NQ], P, A_Q) for k in range(KD)),
            (r_wq[:, :, NQ:], wq[:, 0, :, NQ:], wq[:, 1, :, NQ:], P, A_KV),
            (r_out, wout[:, 0], wout[:, 1], P, A_O),
            (r_wsg, wsg_sb[:, 0], wsg_sb[:, 1], P, A_SG),
            (r_wsd, wsd_sb[:, 0], wsd_sb[:, 1], P, A_SD),
            (r_wr, wr_sb[:, 0], wr_sb[:, 1], P, A_R),
        ]
        FIRST = KD + 1
        wgu_v = wgu.rearrange("e (k p) j -> p k e j", k=KD)
        wd_v = wd.rearrange("e (k p) n -> p k e n", p=KE)
        gu_raw = ga.rearrange("p (k e j) -> p k e j", k=KD, e=E)
        d_raw = gb.rearrange("p (k e j) -> p k e j", k=2, e=E)
        gu_w, d_w = work[:, 2 * NPE:2 * NPE + 2 * I_E], work[:, 2 * NPE + 2 * I_E:2 * NPE + 2 * I_E + D]
        SPLIT_STEPS = 3 * KD
        E4 = 4
        PIECES = [(ga[:, n * E4 * 2 * I_E:(n + 1) * E4 * 2 * I_E], P) for n in range(KD * E // E4)]
        PIECES += [(gb[0:KE, n * E4 * D:(n + 1) * E4 * D], KE) for n in range(2 * E // E4)]

        XB, YB = 8, 4
        def carve(view, at, shape, dt):
            words = int(np.prod(shape)) * (2 if dt == F16 else 4) // 4
            v = view[:, at:at + words]
            v = v if dt == F32 else v.bitcast(dt)
            names_ = "abcd"[:len(shape)]
            sizes = dict(zip(names_, shape))
            return v.rearrange(f"p ({' '.join(names_)}) -> p {' '.join(names_)}", **sizes), at + words

        q_mem = qT[:, :, :, :].rearrange("p t a n -> p (t a n)").bitcast(F32)
        os_mem = pT[:, 1, :, :, :].rearrange("p a g n -> p (a g n)").bitcast(F32)
        xg, w_at = carve(work, 0, (XB, ROW), F16)
        pT_mem = pT[:, 0, :, :, :].rearrange("p a g n -> p (a g n)").bitcast(F32)
        xgT, p_at = carve(pT_mem, 0, (2, 2, KD, P), F16)
        m_hs, p_at = carve(pT_mem, p_at, (2, 2, I_E), F16)
        m_hT_sb, w_at = carve(work, w_at, (2, 2, P), F16)
        m_hT_sb = m_hT_sb[0:KE]
        m_g, m_m = gate[:, 0:I_E], hid[:, 0:I_E]
        m_h, _ = carve(x1[:, :, :].rearrange("p a n -> p (a n)"), 0, (2, I_E), F32)
        m_ys, _ = carve(o_sb, 0, (YB, D), F32)
        CT = 2
        CB = 8
        NC = NT // CT
        c_in = [carve(q_mem if q < CB // 2 else work, (q % (CB // 2)) * TOPK * CT * D, (TOPK, CT, D), F32)[0] for q in range(CB)]
        cmp_k, _ = carve(probs[:, 0, :], 0, (E, NT), F32)
        w_e, os_at = carve(os_mem, 0, (NT, E), F32)
        w_d, os_at = carve(os_mem, os_at, (NT, E), F32)
        cnt = sb("cnt", [P, E], F32)
        tiles_e = sb("tiles_e", [P, E], F32)
        ends = sb("ends", [P, E], F32)
        ones_e = sb("ones_e", [P, E], F32)
        jump = sb("jump", [P, E], F32)
        ge = sb("ge", [P, E], F32)
        jumped = sb("jumped", [P, E], F32)
        t_tab = sb("t_tab", [P, 2], F32)
        t_row, t_exp = t_tab[:, 0:1], t_tab[:, 1:2]
        tab = sb("tab", [1, 2, NMT], I32)
        free_i = sb("free_i", [1, E], I32)
        pad = sb("pad", [P, ROW], F16)
        w_s = sb("w_s", [P, NT], F32)
        w_k = sb("w_k", [P, NT, TOPK], F32)
        w_t = sb("w_t", [P, NT], F32)

        def own_wait(eng):
            eng.sem_inc(s.passed, 1)

        block = ctx.enter_context(nc.Block())

        def write_pads(eng, half):
            rows = nc.values_load_multi_w_load_instructions(free_i[0:1, half * E // 2:(half + 1) * E // 2],
                                                            engines=[eng.engine], min_val=0, max_val=DUMMY - P)[1]
            for row in rows:
                eng.dma_start(lists[ds(row, P), :], pad[:, :]).then_inc(s.pads, 16)

        @block.sync
        def _(sp):
            def load(dst, src, done):
                sp.dma_start(dst, src).then_inc(done, 16)

            load(r_nopeT[0:NOPE], wqb_nopeT, s.w_k)
            load(r_wkT[0:NOPE], wkT, s.w_k)
            load(r_wqaT[:, 0, :], wqaT[0:P, :], s.w_a)
            load(r_wqaT[0:QLB, 1, :], wqaT[P:QL, :], s.w_a)
            load(r_pe[:, 0, :], wqb_peT[0:P, :], s.w_a)
            load(r_pe[0:QLB, 1, :], wqb_peT[P:QL, :], s.w_a)
            for k in range(3):
                load(x_sb[:, k, :], x[k * P:(k + 1) * P, :], xin[k])
            load(r_wvT, wvT, s.w_o)
            load(r_wo, wo.rearrange("(h d) n -> d h n", d=VD), s.w_o)

            def store_dense(t):
                sp.wait_ge(s.dense_done, t.count(1, 1))
                own_wait(sp)
                sp.dma_start(dense[ds(t.row(), P), :], den[:, t.off % 2, :]).then_inc(stored[t.off % 2], 16)

            def section(t):
                p, n3 = t.at(-1), t.at(3)
                if p.exists() and n3.exists():
                    sp.wait_ge(s.x1_done, p.count(1, 1))
                    own_wait(sp)
                if n3.exists():
                    sp.dma_start(x_sb[:, n3.off % 4, :], x[ds(n3.row(), P), :]).then_inc(xin[n3.off % 4], 16)
                if t.at(-2).exists() and (t.b is not None or t.off < NT + 1):
                    store_dense(t.at(-2))
            sp.wait_ge(s.lo_made, len(SPLITS))
            for k in range(KD):
                load(gu_raw[:, k], wgu_v[:, k], s.w_gu)
            for k in range(2):
                load(d_raw[0:KE, k], wd_v[:, k], s.w_d)
            sections(sp, section)

            sp.wait_ge(s.used_ready, 1)
            write_pads(sp, 0)
            sp.dma_start(lists[DUMMY:DUMMY + P, :], pad[:, :]).then_inc(s.pads, 16)
            store_dense(Tile(NT - 1))
            sp.wait_ge(s.pads, 16 * (E + 1))
            for par in range(2):
                sp.wait_ge(scattered[par], 16 * TOPK * NT // 2)
            sp.wait_ge(s.tab_ready, 1)

            def expert_rows(n, q):
                row = sp.value_load(tab[0:1, 0, ds(n, 1)], min_val=0, max_val=DUMMY)
                sp.dma_start(xg[:, q, :], lists[ds(row, P), :]).then_inc(xg_in[q], 16)
            for q in range(XB):
                expert_rows(q, q)
            for par in range(2):
                sp.wait_ge(stored[par], 16 * NT // 2)
            sp.wait_ge(s.down_made, NT)
            load(dense_sb, dense.rearrange("(t p) n -> p t n", p=P), s.dense_in)
            with sp.Fori(1, NMT // XB) as m:
                for q in range(XB):
                    sp.wait_ge(m_out[q], m * 16)
                    own_wait(sp)
                    expert_rows(m * XB + q, q)
            for q in range(XB):
                sp.wait_ge(m_out[q], 16 * (NMT // XB))

            def rows(a, first):
                return a[ds(first, CT * P), :].rearrange("(c p) n -> p c n", p=P)

            with sp.Fori(0, NC // CB) as m:
                for q in range(CB):
                    first = m * (CB * CT * P) + q * CT * P
                    sp.wait_ge(s.c_sum, m * CB + q + 1)
                    own_wait(sp)
                    for k in range(TOPK):
                        sp.dma_start(c_in[q][:, k], rows(y_exp, first + k * NT * P)).then_inc(c_loaded[q], 16)

        def halves(i):
            if GROUP[i] == 1:
                return [[(0, 0, 4)], [(0, 4, i + 1)]]
            n = GROUP[i] // 2
            return [[(h * n + g, 0, i + 1) for g in range(n)] for h in range(2)]

        def half_tiles(i, h):
            return [(g, j) for g, j0, j1 in halves(i)[h] for j in range(j0, j1)]

        def s_off(i, g):
            return g * (P if i == 0 else 2 * P if i == 1 else 512)

        def att_loop(eng, t, unit):
            n = UNITS[t.i]
            rounds = (n - 4) // 2
            for u in range(2 if n > 2 else 0):
                unit(u, u % 2)
            if rounds > 0:
                nc.disable_value_cache = False
                with eng.Fori(1, rounds + 1) as k:
                    unit(k * 2, 0)
                    unit(k * 2 + 1, 1)
                nc.disable_value_cache = True
            unit(n - 2, 0)
            unit(n - 1, 1)

        def has_next(t, u, k):
            return not isinstance(u, int) or u + k < UNITS[t.i]

        def norm(eng, n, p):
            has_p = p is not None and p.exists()
            k0, k1 = (0 if n.exists() else 1), (2 if has_p else 1)
            w = [ln_w[:, a, k0:k1] for a in range(3)]
            var, y, u = w
            st_ = Steps(eng, s.ln_s, LN_STEPS, n.count)
            eng.wait_ge(s.stats, n.count(1, 1))
            own_wait(eng)
            st_.do(eng.tensor_scalar(var, ln_mv[:, k0:k1, 1], EPS, None, ALU.add), own_wait)
            st_.do(eng.tensor_scalar(y.bitcast(I32), var.bitcast(I32), -0.5, SEED, ALU.mult, ALU.add))
            for _ in range(NEWTON):
                st_.do(eng.tensor_tensor(u, y, var, ALU.mult))
                st_.do(eng.tensor_tensor(u, u, y, ALU.mult), own_wait)
                st_.do(eng.tensor_scalar(u, u, -0.5, 1.5, ALU.mult, ALU.add))
                st_.do(eng.tensor_tensor(y, y, u, ALU.mult))
            parts = []
            if n.exists():
                eng.wait_ge(s.xT_made, n.at(-2).count(1, 1)) if n.at(-2).exists() else None
                parts.append((0, x_sb[:, n.off % 4, :], xs[:, n.off % 2, 0, :], xs[:, n.off % 2, 1, :], n, s.ln1_done))
            if has_p:
                if p.at(-2).exists():
                    eng.wait_ge(scattered[p.off % 2], p.at(-2).pair(32))
                row = xs2[:, p.off % 2, 0]
                parts.append((1, x1[:, p.off % 2, :], row[:, 0:D], row[:, D:2 * D], p, s.ln2_done))
            own_wait(eng)
            for k, src, hi, lo, tile, done in parts:
                eng.tensor_scalar(xn[:, :], src, ln_mv[:, k, 0:1], ln_w[:, 1, k:k + 1], ALU.subtract, ALU.mult).then_inc(xn_s[k], 1)
                eng.wait_ge(xn_s[k], tile.count(1, 1))
                own_wait(eng)
                eng.tensor_copy(hi, xn[:, :]).then_inc(done, 1)
                eng.wait_ge(done, tile.count(2, 1))
                eng.tensor_tensor(lo, xn[:, :], hi, ALU.subtract).then_inc(done, 1)
                eng.wait_ge(done, tile.count(2, 2))
                own_wait(eng)
            eng.sem_inc(s.normed, 1)

        def rope_cos(n):
            return cos_sb[:, n.i, :].unsqueeze(1).broadcast_to([P, H + 1, ROPE])

        @block.tensor
        def _(pe_):
            def mm(o, a, b, start, stop):
                return pe_.matmul(o, a, b, start=start, stop=stop)

            pe_.wait_ge(s.w_k, 16 * 2)
            for h in range(H):
                mm(o_ps[:, h // 8, (h % 8) * C:(h % 8 + 1) * C], r_nopeT[0:NOPE, h, 0:P], r_wkT[0:NOPE, h, :], True, True)
                last = mm(t_ps[0:QLB, h // 8, (h % 8) * C:(h % 8 + 1) * C], r_nopeT[0:NOPE, h, P:QL],
                          r_wkT[0:NOPE, h, :], True, True)
            last.then_inc(s.qb_made, 1)
            pe_.wait_ge(s.w_a, 16 * 4)
            for m in range(KD):
                for n, c in enumerate(WQ_ORDER):
                    src = r_qb if c < 2 else r_pe
                    cc = slice((c % 2) * 512, (c % 2) * 512 + 512)
                    if m:
                        pe_.wait_ge(s.wq_copied, n + 1)
                    elif n == 2:
                        pe_.wait_ge(s.qb_copied, 1)
                    mm(s_ps[:, c, :], r_wqaT[:, 0, m * P:(m + 1) * P], src[:, 0, cc], True, False)
                    mm(s_ps[:, c, :], r_wqaT[0:QLB, 1, m * P:(m + 1) * P], src[0:QLB, 1, cc], False,
                       True).then_inc(s.wq_made, 1)
            pe_.wait_ge(s.w_o, 16 * 2)
            for hp in range(H // 2):
                bank = (o_ps if hp % 4 < 2 else t_ps)[:, hp % 2, 0:D]
                if hp >= 4:
                    pe_.wait_ge(s.wo_copied, hp - 3)
                for e in range(2):
                    last = mm(bank[e * C:(e + 1) * C], r_wvT[:, 2 * hp + e, :], r_wo[:, 2 * hp + e, :], True, True)
                last.then_inc(s.wo_made, 1)

            def transposes(bank, rows, done):
                for a in range(2):
                    for k in range(KD):
                        last = pe_.transpose(bank[:, (2 * a + k) * P:(2 * a + k + 1) * P], rows(a, k), id16[:, :])
                last.then_inc(done, 1)

            def x_transposes(n):
                pe_.wait_ge(s.ln1_done, n.count(2, 2))
                transposes(st[1], lambda a, k: xs[:, n.off % 2, a, k * P:(k + 1) * P], s.xT_made)

            def x2_transposes(p):
                pe_.wait_ge(s.ln2_done, p.count(2, 2))
                transposes(st[0], lambda a, k: xs2[:, p.off % 2, 0, a * D + k * P:a * D + (k + 1) * P], s.x2T_made)

            def norm_transposes(t):
                if t.at(-1).exists():
                    x2_transposes(t.at(-1))
                if t.at(2).exists():
                    x_transposes(t.at(2))

            def split_product(o, lhs, rhs, done):
                n = len(done)
                first = True
                for k in done:
                    for a, b in ((0, 0), (0, 1), (1, 0)):
                        last = mm(o, lhs(a, k), rhs(b, k), first, k == done[-1] and a == 1)
                        first = False
                return last

            def project(n, bank, c0, w):
                split_product(bank, lambda a, k: xT[:, n.off % 2, a, k, :], lambda b, k: wq[:, b, k, c0:c0 + w],
                              list(range(KD))).then_inc(s.q_made, 1)

            def latent_projections(n):
                pe_.wait_ge(s.xT_ready, n.count(1, 1))
                if n.off > 0 or n.b is not None:
                    pe_.wait_ge(s.qT_act, n.at(-1).count(3, 3))
                    pe_.wait_ge(s.qT_dve, n.at(-1).count(2, 2))
                project(n, t_ps[:, 1, 0:P], NQ, 2 * C)
                for g in range(2):
                    project(n, s_ps[:, 2 + g, :], H * NOPE + g * 512, 512)

            def query_projections(n):
                if n.at(-3).exists():
                    pe_.wait_ge(s.hid_done, n.at(-3).count(1, 1))
                for g in range(2):
                    project(n, s_ps[:, g, :], g * 512, 512)

            def q_transposes(n):
                pe_.wait_ge(s.lo_q, n.count(3, 3))
                pe_.wait_ge(s.rope_done, n.count(1, 1))
                for g, bank in enumerate((tt[0], tt[1], st[2], st[3])):
                    for h in range(8):
                        last = pe_.transpose(bank[:, h * P:(h + 1) * P], qs[:, g // 2, (g % 2) * 8 + h, :], id16[:, :])
                    last.then_inc(s.qT_made, 1)
                pe_.wait_ge(s.qT_act, n.count(3, 1))
                for a in range(2):
                    last = pe_.transpose(tt[0][:, a * P:(a + 1) * P], ks[:, a, :], id16[:, :])
                last.then_inc(s.qT_made, 1)

            def o_transposes(p):
                pe_.wait_ge(s.hi_o, p.count(1, 1))
                for a in range(2):
                    if a:
                        pe_.wait_ge(s.lo_o, p.count(1, 1))
                        if p.at(-1).exists():
                            pe_.wait_ge(s.route_s, p.at(-1).count(6, 1))
                    for hp in range(H // 2):
                        last = pe_.transpose(ot[a][:, hp * P:(hp + 1) * P], os_[:, a, hp * P:(hp + 1) * P], id16[:, :])
                    last.then_inc(s.oT_made, 1)

            def out_projection(p):
                if p.b is None and p.off == 0:
                    pe_.wait_ge(s.lo_made, FIRST + 1)
                pe_.wait_ge(s.oT_act, p.count(1, 1))
                pe_.wait_ge(s.oT_dve, p.count(1, 1))
                if p.at(-1).exists():
                    pe_.wait_ge(s.hT_ready, p.at(-1).count(2, 2))
                split_product(t_ps[:, 0, 0:D], lambda a, k: oT[:, a, k, :], lambda b, k: wout[:, b, k, :],
                              list(range(H // 2))).then_inc(s.proj_made, 1)

            def scores(t, u, par, h):
                i, G = t.i, GROUP[t.i]
                L = (i + 1) * P
                flat = s_ps[:, :, :].rearrange("p a n -> p (a n)")
                for g, j0, j1 in halves(i)[h]:
                    base = 1024 * par + s_off(i, g)
                    c0, c1 = j0 * P, j1 * P
                    for a, b in ((0, 0), (0, 1), (1, 0)):
                        last = mm(flat[:, base + c0:base + c1], qT[:, t.off % 2, a, ds((u * G + g) * P, P)], kT[:, b, c0:c1],
                                  a + b == 0, a == 1 and c1 < L)
                    if c1 == L:
                        last = mm(flat[:, base + L - P:base + L], idbf[:, :], maskbf[:, :], False, True)
                last.then_inc(s.s_made, 1)

            def attention(t):
                n, p = t.at(1), t.at(-1)
                i, G = t.i, GROUP[t.i]
                L = (i + 1) * P
                pe_.wait_ge(s.qT_act, t.count(3, 3))
                pe_.wait_ge(s.qT_dve, t.count(2, 2))
                pe_.wait_ge(s.ckv_ready, t.count(1, 1))
                if n.exists():
                    pe_.wait_ge(s.pe_ready, n.count(1, 1))
                    pe_.wait_ge(s.lo_q, n.count(3, 3))
                def first_scores(u):
                    for h in range(2):
                        scores(t, u, u, h)
                first_scores(0)
                if t.at(-2).exists():
                    shared_down(t.at(-2))
                first_scores(1)
                if p.exists():
                    pe_.wait_ge(s.x1_done, p.count(1, 1))

                def values(u, par):
                    for h in range(2):
                        pe_.wait_ge(s.lo_p, t.units(2, u, h + 1))
                        for c, (g, j) in enumerate(half_tiles(i, h)):
                            o = o_flat[:, ds((u * G + g) * C, C)]
                            for a, b in ((0, 0), (0, 1), (1, 0)):
                                last = mm(o, pT[:, par, a, h, c * P:(c + 1) * P], ckv[:, b, j, :],
                                          j == 0 and a + b == 0, j == i and a == 1)
                    last.then_inc(s.pv_made, 1)

                def unit(u, par):
                    first = isinstance(u, int) and u == 0
                    for h in range(2):
                        pe_.wait_ge(s.exp_done, t.units(2, u, h + 1))
                        if not first:
                            pe_.wait_ge(s.lo_p, t.units(2, u, h - 1))
                        for c, (g, j) in enumerate(half_tiles(i, h)):
                            last = pe_.transpose(t_ps[:, h, c * P:(c + 1) * P],
                                                 probs[:, par, g * L + j * P:g * L + (j + 1) * P], id32[:, :])
                        last.then_inc(s.p_made, 1)
                        if has_next(t, u, 2):
                            scores(t, u + 2, par, h)
                    if isinstance(u, int) and u == 1 and t.at(-2).exists():
                        pe_.wait_ge(s.dense_done, t.at(-2).count(1, 1))
                    if not first:
                        values(u - 1, 1 - par)
                att_loop(pe_, t, unit)
                if EARLY_NORMS[i]:
                    norm_transposes(t)
                values(UNITS[i] - 1, 1)

            def shared_up(p):
                if p.at(3).exists():
                    pe_.wait_ge(s.xT_ready, p.at(3).count(1, 1))
                pe_.wait_ge(s.x2T_ready, p.count(1, 1))
                if p.b is None and p.off == 0:
                    pe_.wait_ge(s.lo_made, len(SPLITS))
                if p.at(1).exists():
                    pe_.wait_ge(s.o_ready, p.at(1).count(1, 1))
                split_product(o_ps[:, 1, 0:E], lambda a, k: x2T[:, a, k, :], lambda b, k: wr_sb[:, b, k, :],
                              list(range(KD))).then_inc(s.lgt_made, 1)
                for g in range(2):
                    last = split_product(s_ps[:, g, 0:SI], lambda a, k: x2T[:, a, k, :],
                                         lambda b, k: wsg_sb[:, b, k, g * SI:(g + 1) * SI], list(range(KD)))
                last.then_inc(s.gu_made, 1)

            def hidden_transposes(q):
                pe_.wait_ge(s.hi_h, q.count(1, 1))
                pe_.wait_ge(s.lo_h, q.count(1, 1))
                for a in range(2):
                    for k in range(3):
                        w = min(P, SI - k * P)
                        last = pe_.transpose(tt[0][0:w, (3 * a + k) * P:(3 * a + k + 1) * P],
                                             hs[:, a, k * P:k * P + w], id16[:, :])
                last.then_inc(s.hT_made, 1)

            def shared_down(q):
                pe_.wait_ge(s.mask_ready, q.count(1, 1))
                if q.at(1).exists():
                    pe_.wait_ge(s.oT_act, q.at(1).count(1, 1))
                    pe_.wait_ge(s.oT_dve, q.at(1).count(1, 1))
                mm(o_ps[:, 1, 0:E], tri16[:, :], picked[:, q.off % 2, :], True, True)
                mm(o_ps[:, 1, E:2 * E], ones16[:, :], picked[:, q.off % 2, :], True, True).then_inc(s.rank_made, 1)
                pe_.wait_ge(s.hT_ready, q.count(2, 2))

                def rows(k):
                    return min(P, SI - k * P)
                split_product(o_ps[:, 0, 0:D], lambda a, k: hT[0:rows(k), a, k, :],
                              lambda b, k: wsd_sb[0:rows(k), b, k, :], list(range(3))).then_inc(s.down_made, 1)

            pe_.wait_ge(s.c_ready, 1)
            x_transposes(Tile(0))
            pe_.wait_ge(s.xT_ready, 1)
            x_transposes(Tile(1))
            pe_.wait_ge(s.lo_made, FIRST)
            pe_.wait_ge(s.wo_copied, H // 2)
            latent_projections(Tile(0))
            pe_.wait_ge(s.xT_ready, 2)
            query_projections(Tile(0))
            q_transposes(Tile(0))

            def section(t):
                n = t.at(1)
                if n.exists():
                    latent_projections(n)
                if t.at(-2).exists():
                    hidden_transposes(t.at(-2))
                if t.at(-1).exists():
                    o_transposes(t.at(-1))
                if n.exists():
                    query_projections(n)
                if t.at(-1).exists():
                    out_projection(t.at(-1))
                if t.exists():
                    attention(t)
                elif t.at(-2).exists():
                    shared_down(t.at(-2))
                if n.exists():
                    q_transposes(n)
                if not (t.exists() and EARLY_NORMS[t.i]):
                    norm_transposes(t)
                if t.at(-1).exists():
                    shared_up(t.at(-1))
            sections(pe_, section)

            pe_.wait_ge(s.tab_made, 1)
            for k in range(2):
                last = pe_.transpose(s_ps[0:1, 0, k * P:(k + 1) * P], t_tab[:, k:k + 1], id32[:, :])
            last.then_inc(s.tab_turned, 1)

            pe_.wait_ge(s.split, E * SPLIT_STEPS)
            pe_.wait_ge(s.tab_ready, 1)

            def xg_transposes(n, q, par, m):
                pe_.wait_ge(xg_in[q], m * 16 + 16)
                for a in range(2):
                    for k in range(KD):
                        last = pe_.transpose(tt[par][:, (2 * a + k) * P:(2 * a + k + 1) * P],
                                             xg[:, q, a * D + k * P:a * D + (k + 1) * P], id16[:, :])
                last.then_inc(s.m_xT, 1)

            def expert_of(n):
                return pe_.value_load(tab[0:1, 1, ds(n, 1)], min_val=0, max_val=E - 1)

            def expert_up(n, par, e):
                pe_.wait_ge(s.m_xTs, n + 1)
                split_product(s_ps[:, par, 0:2 * I_E], lambda a, k: xgT[:, par, a, k, :],
                              lambda b, k: wgu_sb[:, k, ds(e, 1), b, :], list(range(KD))).then_inc(s.m_gu, 1)

            def h_transposes(n, par):
                pe_.wait_ge(s.m_hi, n + 1)
                pe_.wait_ge(s.m_lo, n + 1)
                for a in range(2):
                    for k in range(2):
                        last = pe_.transpose(ot[0][0:KE, (2 * a + k) * P:(2 * a + k + 1) * P],
                                             m_hs[:, par, a, k * KE:(k + 1) * KE], id16[:, :])
                last.then_inc(s.m_hT, 1)

            def expert_down(n, e):
                pe_.wait_ge(s.m_hTs, n + 1)
                pe_.wait_ge(s.m_y, n + 1)
                split_product(o_ps[:, 1, 0:D], lambda a, k: m_hT_sb[:, a, k, :],
                              lambda b, k: wd_sb[0:KE, k, ds(e, 1), b, :], list(range(2))).then_inc(s.m_down, 1)

            held = [pe_.alloc_register(f"expert{k}") for k in range(3)]

            def read_expert(n, k):
                pe_.reg_load(held[k], tab[0:1, 1, ds(n, 1)])

            def held_expert(k):
                return pe_.snap(held[k], min_val=0, max_val=E - 1)

            for n in range(3):
                read_expert(n, n)
            xg_transposes(0, 0, 0, 0)
            xg_transposes(1, 1, 1, 0)
            expert_up(0, 0, held_expert(0))
            xg_transposes(2, 2, 0, 0)
            expert_up(1, 1, held_expert(1))
            xg_transposes(3, 3, 1, 0)

            nc.disable_value_cache = False
            with pe_.Fori(0, NMT // XB - 1) as m:
                e = [held_expert(k) for k in range(3)]
                for q in range(XB):
                    n = m * XB + q
                    h_transposes(n, q % 2)
                    expert_up(n + 2, q % 2, e[q + 2])
                    if q + 3 < XB:
                        e.append(expert_of(n + 3))
                    else:
                        read_expert(n + 3, q + 3 - XB)
                        e.append(held_expert(q + 3 - XB))
                    xg_transposes(n + 4, (q + 4) % XB, q % 2, m + (q + 4) // XB)
                    expert_down(n, e[q])
            nc.disable_value_cache = True
            e = [held_expert(k) for k in range(3)]
            for q in range(XB):
                n = NMT - XB + q
                h_transposes(n, n % 2)
                if n + 2 < NMT:
                    expert_up(n + 2, n % 2, e[q + 2])
                if n + 3 < NMT:
                    e.append(expert_of(n + 3))
                if n + 4 < NMT:
                    xg_transposes(n + 4, (n + 4) % XB, n % 2, (n + 4) // XB)
                expert_down(n, e[q])

        @block.scalar
        def _(act):
            def copy(o, i):
                return act.copy(o, i)

            def load(dst, src, done):
                act.dma_start(dst, src).then_inc(done, 16)
            for dst, src in ((id32[:, :], ident), (probs[:, 1, 0:P], causal), (probs[:, 0, 0:P], tri),
                             (cos_sb[:, :, :], cos_t), (sin_sb[:, :, :], sin_t), (iota_e_sb[:, :], iota_e),
                             (iota_k_sb[:, :, :], iota_k), (iota_p_sb[:, :], iota_p), (dest_f[:, :], tok_ids)):
                load(dst, src, s.c_in)
            load(r_wq[:, :, NQ:], wkva.rearrange("(k p) n -> p k n", p=P), s.w_b)
            load(r_wsg, wsg.rearrange("(k p) n -> p k n", p=P), s.w_b)
            load(r_wsd[:, 0:2, :], wsd[0:2 * P, :].rearrange("(k p) n -> p k n", p=P), s.w_b)
            load(r_wsd[0:SI - 2 * P, 2, :], wsd[2 * P:SI, :], s.w_b)
            load(r_wr, gateT.rearrange("(k p) n -> p k n", p=P), s.w_b)

            act.wait_ge(s.qb_made, 1)
            copy(r_qb[:, 0, :], o_flat)
            copy(r_qb[0:QLB, 1, :], t_ps[0:QLB, :, :].rearrange("p a n -> p (a n)")).then_inc(s.qb_copied, 1)
            for m in range(KD):
                for n, c in enumerate(WQ_ORDER):
                    act.wait_ge(s.wq_made, m * 4 + n + 1)
                    copy(r_wq[:, m, c * 512:(c + 1) * 512], s_ps[:, c, :]).then_inc(s.wq_copied, 1)

            def hi_parts(splits):
                for raw, hi, lo, rows, col in splits:
                    act.activation(hi[0:rows], raw[0:rows], ACT.Copy, scale=winv[0:rows, col:col + 1]).then_inc(s.hi_made, 1)

            def out_weights(first, last):
                for hp in range(first, last):
                    act.wait_ge(s.wo_made, hp + 1)
                    copy(r_out[:, hp, :], (o_ps if hp % 4 < 2 else t_ps)[:, hp % 2, 0:D]).then_inc(s.wo_copied, 1)
            out_weights(0, 4)
            act.wait_ge(s.scales, 1)
            hi_parts(SPLITS[:FIRST])

            def x_copy(n):
                act.wait_ge(s.xT_made, n.count(1, 1))
                copy(xT[:, n.off % 2].rearrange("p a k n -> p (a k n)"), st[1][:, 0:4 * P]).then_inc(s.xT_ready, 1)

            def norm_copies(t):
                p = t.at(-1)
                if p.exists():
                    act.wait_ge(s.x2T_made, p.count(1, 1))
                    copy(x2T[:, :, :, :].rearrange("p a k n -> p (a k n)"), st[0][:, 0:4 * P]).then_inc(s.x2T_ready, 1)
                if t.at(2).exists():
                    x_copy(t.at(2))

            def latent_copies(n):
                act.wait_ge(s.q_made, n.count(5, 1))
                copy(pe[:, H, :], t_ps[:, 1, C:2 * C])
                copy(ks[:, 0, 0:C], t_ps[:, 1, 0:C]).then_inc(s.hi_q, 1)
                for g in range(2):
                    act.wait_ge(s.q_made, n.count(5, 2 + g))
                    last = copy(pe[:, 8 * g:8 * g + 8, :], s_ps[:, 2 + g, :].rearrange("p (h r) -> p h r", r=ROPE))
                last.then_inc(s.pe_ready, 1)

            def query_copies(n):
                for g in range(2):
                    act.wait_ge(s.q_made, n.count(5, 4 + g))
                    copy(qs[:, 0, 8 * g:8 * g + 8, 0:NOPE],
                         s_ps[:, g, :].rearrange("p (h r) -> p h r", r=NOPE)).then_inc(s.hi_q, 1)

            def rope_hi(n):
                act.wait_ge(s.rot_s, n.count(3, 2))
                copy(ks[:, 0, C:HD], rot[:, H, :])
                copy(qs[:, 0, :, NOPE:HD], rot[:, 0:H, :]).then_inc(s.rot_s, 1)

            def qT_copies(n, t):
                par = n.off % 2
                act.wait_ge(s.qT_made, n.count(5, 1))
                copy(qT[:, par, 0, 0:1024], tt[0]).then_inc(s.qT_act, 1)
                if t is not None:
                    out_hi(t)
                act.wait_ge(s.qT_made, n.count(5, 3))
                copy(qT[:, par, 1, 0:1024], st[2]).then_inc(s.qT_act, 1)
                act.wait_ge(s.qT_made, n.count(5, 5))
                copy(kT[:, :, n.i * P:(n.i + 1) * P], tt[0][:, 0:2 * P].rearrange("p (a n) -> p a n", a=2)).then_inc(s.qT_act, 1)

            def out_hi(p):
                act.wait_ge(s.o_ready, p.count(1, 1))
                copy(os_[:, 0, :], o_sb[:, :]).then_inc(s.hi_o, 1)

            def oT_copy(p):
                act.wait_ge(s.oT_made, p.count(2, 1))
                copy(oT[:, 0, :, :].rearrange("p k n -> p (k n)"), ot[0]).then_inc(s.oT_act, 1)

            def attention(t):
                i, G = t.i, GROUP[t.i]
                L = (i + 1) * P
                flat = s_ps[:, :, :].rearrange("p a n -> p (a n)")

                def exps(u, par, h):
                    if h == 0:
                        act.wait_ge(s.max_ready, t.units(1, u, 1))
                    if shifted(i, u):
                        half = probs[:, par, h * (G // 2) * L:(h + 1) * (G // 2) * L]
                        act.activation(half, half, ACT.Exp, scale=f_att).then_inc(s.exp_done, 1)
                        return
                    for g, j0, j1 in halves(i)[h]:
                        base = 1024 * par + s_off(i, g)
                        part = h if G == 1 else 0
                        last = act.activation(probs[:, par, g * L + j0 * P:g * L + j1 * P], flat[:, base + j0 * P:base + j1 * P],
                                              ACT.Exp, bias=nmax[:, par, g:g + 1], scale=f_att,
                                              accum_out=ssum[:, t.off % 2, part, ds(u * G + g, 1)])
                    last.then_inc(s.exp_done, 1)

                def unit(u, par):
                    if not (isinstance(u, int) and u < 2):
                        act.wait_ge(s.pv_made, t.units(1, u, -1))
                    for h in range(2):
                        w = P * len(half_tiles(i, h))
                        act.wait_ge(s.p_made, t.units(2, u, h + 1))
                        copy(pT[:, par, 0, h, 0:w], t_ps[:, h, 0:w]).then_inc(s.hi_p, 1)
                        if has_next(t, u, 1):
                            exps(u + 1, 1 - par, h)
                exps(0, 0, 0)
                exps(0, 0, 1)
                att_loop(act, t, unit)

            def shared_act(p):
                act.wait_ge(s.gu_made, p.count(1, 1))
                act.activation(gate[:, :], s_ps[:, 0, 0:SI], ACT.Tanh, scale=f_sgh).then_inc(s.gate_done, 1)
                act.wait_ge(s.hid_done, p.count(1, 1))
                copy(hs[:, 0, :], hid[:, :]).then_inc(s.hi_h, 1)

            def hT_copy(q):
                act.wait_ge(s.hT_made, q.count(1, 1))
                w = SI - 2 * P
                src = tt[0][:, 0:6 * P].rearrange("p (a k n) -> p a k n", a=2, k=3)
                copy(hT[:, :, 0:2, :], src[:, :, 0:2, :]).then_inc(s.hT_ready, 1)
                copy(hT[0:w, :, 2, :], src[0:w, :, 2, :]).then_inc(s.hT_ready, 1)

            x_copy(Tile(0))
            x_copy(Tile(1))
            out_weights(4, H // 2)
            latent_copies(Tile(0))
            query_copies(Tile(0))
            act.wait_ge(s.scales, 2)
            hi_parts(SPLITS[FIRST:FIRST + 2])
            rope_hi(Tile(0))
            qT_copies(Tile(0), None)
            hi_parts(SPLITS[FIRST + 2:])

            def section(t):
                n = t.at(1)
                if n.exists():
                    latent_copies(n)
                if t.at(-2).exists():
                    hT_copy(t.at(-2))
                if t.at(-1).exists():
                    oT_copy(t.at(-1))
                if n.exists():
                    query_copies(n)
                    if shares_rope(n):
                        rope_hi(n)
                if t.exists():
                    attention(t)
                if t.exists() and EARLY_NORMS[t.i]:
                    norm_copies(t)
                if n.exists():
                    qT_copies(n, t)
                elif t.exists():
                    out_hi(t)
                if not t.exists():
                    norm_copies(t)
                if t.at(-1).exists():
                    shared_act(t.at(-1))
            sections(act, section)

            act.wait_ge(s.used_ready, 1)
            write_pads(act, 1)

            act.wait_ge(s.c_w, 1)
            act.activation(w_e[:, :, :].rearrange("p t e -> p (t e)"), w_d[:, :, :].rearrange("p t e -> p (t e)"),
                           ACT.Exp).then_inc(s.w_exp, 1)
            act.activation(w_t[:, :], w_t[:, :], ACT.Exp).then_inc(s.w_exp, 1)

            def xg_copy(n, par):
                act.wait_ge(s.m_xT, n + 1)
                copy(xgT[:, par, :, :, :].rearrange("p a k n -> p (a k n)"), tt[par][:, 0:4 * P]).then_inc(s.m_xTs, 1)

            def expert_gate(n, par):
                act.wait_ge(s.m_gu, n + 1)
                act.activation(m_g[:, :], s_ps[:, par, 0:I_E], ACT.Tanh, scale=f_guh).then_inc(s.m_gate, 1)
                act.wait_ge(s.m_hid, n + 1)
                copy(m_hs[:, par, 0, :], m_h[:, par, :]).then_inc(s.m_hi, 1)

            def y_copy(n, q, m):
                act.wait_ge(s.m_down, n + 1)
                if not (isinstance(m, int) and n < YB):
                    act.wait_ge(m_out[(q + YB) % XB], m * 16 + (0 if q < YB else 16))
                act.activation(m_ys[:, q % YB, :], o_ps[:, 1, 0:D], ACT.Copy, scale=f_ed).then_inc(s.m_y, 1)

            xg_copy(0, 0)
            xg_copy(1, 1)
            expert_gate(0, 0)
            xg_copy(2, 0)
            expert_gate(1, 1)
            xg_copy(3, 1)

            def expert_round(m, q, n):
                last = isinstance(n, int)
                if not last or n + 2 < NMT:
                    expert_gate(n + 2, q % 2)
                if not last or n + 4 < NMT:
                    xg_copy(n + 4, q % 2)
                y_copy(n, q, m)
            for q in range(XB):
                expert_round(0, q, q)
            with act.Fori(1, NMT // XB - 1) as m:
                for q in range(XB):
                    expert_round(m, q, m * XB + q)
            for q in range(XB):
                expert_round(NMT // XB - 1, q, NMT - XB + q)

            with act.Fori(0, NC // CB) as m:
                for q in range(CB):
                    act.wait_ge(s.c_sum, m * CB + q + CB + 1)
                    first = m * (CB * CT * P) + q * CT * P
                    act.dma_start(out[ds(first, CT * P), :].rearrange("(c p) n -> p c n", p=P),
                                  dense_sb[:, ds(m * (CB * CT) + q * CT, CT), :]).then_inc(s.c_out, 16)
            act.wait_ge(s.c_out, 16 * NC)

        @block.vector
        def _(dve):
            def link(ins):
                link.n += 1
                ins.then_inc(s.prep, 1)
                dve.wait_ge(s.prep, link.n)
            link.n = 0

            def at(per, k):
                return k

            dve.wait_ge(s.c_in, 16 * 9)
            dve.tensor_copy(id16[:, :], id32[:, :])
            dve.tensor_copy(idbf[:, :], id32[:, :])
            dve.tensor_copy(maskbf[:, :], probs[:, 1, 0:P])
            dve.tensor_copy(tri16[:, :], probs[:, 0, 0:P])
            dve.memset(ones16[:, :], 1.0)
            dve.memset(ones_e[:, :], 1.0)
            dve.memset(amax_e[:, :], 0.0)
            link(dve.memset(amax[:, :], 0.0))
            dve.tensor_scalar(used[:, :], iota_e_sb[:, :], float(LIST), None, ALU.mult)
            dve.memset(lg_all[:, :, :], 0.0).then_inc(s.c_ready, 1)
            dve.memset(pad[:, 0:2 * D], 0.0)
            dve.memset(pad[:, 2 * D:ROW].bitcast(I32), 2 * NY)
            dve.sem_inc(s.m_y, 1)
            dve.sem_inc(s.c_sum, CB)

            def largest(o, src):
                return dve.tensor_reduce(o, src, AX_X, ALU.max, apply_absolute_value=True)

            def scales(cols):
                link(dve.tensor_scalar(amax_all[:, cols], amax_all[:, cols], 1e-30, None, ALU.max))
                link(dve.tensor_scalar(wamp[:, cols], amax_all[:, cols], 1.0 / WMAX, None, ALU.mult))
                link(dve.reciprocal(winv[:, cols], wamp[:, cols]))

            def lo_parts(first, last):
                for k in range(first, last):
                    raw, hi, lo, rows, col = SPLITS[k]
                    dve.wait_ge(s.hi_made, k + 1)
                    dve.scalar_tensor_tensor(lo[0:rows], raw[0:rows], winv[0:rows, col:col + 1], hi[0:rows],
                                             ALU.mult, ALU.subtract).then_inc(s.lo_made, 1)

            def first_weights():
                dve.wait_ge(s.w_b, 16 * 5)
                link(dve.memset(r_wsd[SI - 2 * P:P, 2, :], 0.0))
                largest(amax_kv[:, :], r_wq[:, :, NQ:])
                for n in range(8):
                    dve.wait_ge(s.wq_copied, n + 1)
                    last = largest(amax_q[:, n:n + 1], r_wq[:, n // 4, WQ_ORDER[n % 4] * 512:(WQ_ORDER[n % 4] + 1) * 512])
                link(last)
                largest(amax[:, A_KV:A_KV + 1], amax_kv[:, :])
                link(largest(amax[:, A_Q:A_Q + 1], amax_q[:, :]))
                dve.sem_inc(s.amax_ready, 1)
                dve.wait_ge(s.amax_reduced, 1)
                scales(slice(0, 2))
                link(dve.tensor_scalar(f_att, wamp[:, A_Q:A_Q + 1], wamp[:, A_KV:A_KV + 1], HD ** -0.5, ALU.mult, ALU.mult))
                dve.tensor_scalar(f_natt, f_att, -1.0, None, ALU.mult)
                dve.sem_inc(s.scales, 1)
                lo_parts(0, FIRST)

            def other_weights():
                for raw, col in ((r_wsg, A_SG), (r_wsd, A_SD), (r_wr, A_R)):
                    largest(amax[:, col:col + 1], raw.rearrange("p k n -> p (k n)"))
                for n in range(8):
                    dve.wait_ge(s.wo_copied, n + 1)
                    last = largest(amax_o[:, n:n + 1], r_out[:, n, :])
                link(last)
                link(largest(amax[:, A_O:A_O + 1], amax_o[:, :]))
                dve.sem_inc(s.amax_ready, 1)
                dve.wait_ge(s.amax_reduced, 2)
                scales(slice(2, 6))
                dve.tensor_scalar(f_out, wamp[:, A_KV:A_KV + 1], wamp[:, A_O:A_O + 1], None, ALU.mult)
                dve.tensor_scalar(f_sgh, wamp[:, A_SG:A_SG + 1], 0.5, None, ALU.mult)
                link(dve.tensor_scalar(f_sd, wamp[:, A_SG:A_SG + 1], wamp[:, A_SG:A_SG + 1], 0.5 / HSCALE, ALU.mult, ALU.mult))
                link(dve.tensor_scalar(f_sd, f_sd, wamp[:, A_SD:A_SD + 1], None, ALU.mult))
                dve.sem_inc(s.scales, 1)

            def expert_magnitudes(first, last):
                dve.wait_ge(s.w_gu, 16 * KD)
                dve.wait_ge(s.w_d, 16 * 2)
                for n in range(first, last):
                    src, rows = PIECES[n]
                    ins = largest(amax_e[0:rows, n:n + 1], src)
                if last == len(PIECES):
                    link(ins)
                    half = KD * E // E4
                    largest(amax[:, A_GU:A_GU + 1], amax_e[:, 0:half])
                    link(largest(amax[:, A_D:A_D + 1], amax_e[:, half:]))
                    dve.sem_inc(s.gu_amax, 1)

            def expert_scales():
                dve.wait_ge(s.gu_red, 1)
                scales(slice(6, 8))
                dve.tensor_scalar(f_guh, wamp[:, A_GU:A_GU + 1], 0.5, None, ALU.mult)
                link(dve.tensor_scalar(f_ed, wamp[:, A_GU:A_GU + 1], wamp[:, A_GU:A_GU + 1], 0.5 / HSCALE, ALU.mult, ALU.mult))
                link(dve.tensor_scalar(f_ed, f_ed, wamp[:, A_D:A_D + 1], None, ALU.mult))
                dve.sem_inc(s.gu_scale, 1)

            def expert_rows(p):
                row = xs2[:, p.off % 2]
                dve.wait_ge(s.ln2_done, p.count(2, 2))
                dve.tensor_copy(row[:, 1, 0:2 * D], row[:, 0, 0:2 * D])
                dve.tensor_copy(row[:, :, 2 * D:ROW].bitcast(I32).rearrange("p k o -> p (k o)"), dest_f[:, :]).then_inc(s.row_s, 1)
                dve.wait_ge(s.row_s, p.count(2, 1))
                dve.tensor_scalar(dest_f[:, :], dest_f[:, :], float(P), None, ALU.add).then_inc(s.row_s, 1)

            def latent_lo(n):
                dve.wait_ge(s.hi_q, n.count(3, 1))
                dve.tensor_tensor(ks[:, 1, 0:C], t_ps[:, 1, 0:C], ks[:, 0, 0:C], ALU.subtract).then_inc(s.lo_q, 1)

            def query_lo(n):
                for g in range(2):
                    dve.wait_ge(s.hi_q, n.count(3, 2 + g))
                    hs_ = slice(8 * g, 8 * g + 8)
                    dve.tensor_tensor(qs[:, 1, hs_, 0:NOPE], s_ps[:, g, :].rearrange("p (h r) -> p h r", r=NOPE),
                                      qs[:, 0, hs_, 0:NOPE], ALU.subtract).then_inc(s.lo_q, 1)

            def qT_copies(n):
                par = n.off % 2
                if n.at(-1).exists():
                    dve.wait_ge(s.pv_made, n.at(-1).units(1, UNITS[n.at(-1).i] - 1, 1))
                dve.wait_ge(s.lo_q, n.count(3, 3))
                dve.tensor_copy(ckv[:, :, n.i, :], ks[:, :, 0:C]).then_inc(s.ckv_ready, 1)
                dve.wait_ge(s.qT_made, n.count(5, 2))
                dve.tensor_copy(qT[:, par, 0, 1024:2048], tt[1]).then_inc(s.qT_dve, 1)
                dve.wait_ge(s.qT_made, n.count(5, 4))
                dve.tensor_copy(qT[:, par, 1, 1024:2048], st[3]).then_inc(s.qT_dve, 1)

            def rope_sum(n):
                dve.wait_ge(s.pe_ready, n.count(1, 1))
                dve.tensor_tensor(rot, pe, rope_cos(n), ALU.mult).then_inc(s.rot_s, 1)
                dve.wait_ge(s.rot_s, n.count(3, 1))
                dve.wait_ge(s.rope_s, n.count(6, 6))
                dve.tensor_tensor(rot, rot, rot2, ALU.add).then_inc(s.rot_s, 1)

            def rope_lo(n):
                dve.wait_ge(s.rot_s, n.count(3, 3))
                dve.tensor_tensor(ks[:, 1, C:HD], rot[:, H, :], ks[:, 0, C:HD], ALU.subtract)
                dve.tensor_tensor(qs[:, 1, :, NOPE:HD], rot[:, 0:H, :], qs[:, 0, :, NOPE:HD], ALU.subtract).then_inc(s.rope_done, 1)

            def out_norm(p):
                dve.wait_ge(s.pv_made, p.units(1, UNITS[p.i] - 1, 1))
                if p.at(-1).exists():
                    dve.wait_ge(s.lo_o, p.at(-1).count(1, 1))
                sums = ssum[:, p.off % 2, 0, :]
                if GROUP[p.i] == 1:
                    dve.tensor_tensor(sums, sums, ssum[:, p.off % 2, 1, :], ALU.add).then_inc(s.o_evs, 1)
                elif not shifted(p.i, 0):
                    dve.sem_inc(s.o_evs, 1)
                dve.wait_ge(s.o_evs, p.count(2, 1))
                dve.reciprocal(rsum[:, :], sums).then_inc(s.o_evs, 1)
                dve.wait_ge(s.o_evs, p.count(2, 2))
                dve.tensor_tensor(o_sb[:, :].rearrange("p (h c) -> p h c", c=C), o_flat.rearrange("p (h c) -> p h c", c=C),
                                  rsum[:, :].unsqueeze(2).broadcast_to([P, H, C]), ALU.mult).then_inc(s.o_ready, 1)

            def oT_copy(p):
                dve.wait_ge(s.oT_made, p.count(2, 2))
                dve.tensor_copy(oT[:, 1, :, :].rearrange("p k n -> p (k n)"), ot[1]).then_inc(s.oT_dve, 1)

            def residual(p):
                dve.wait_ge(s.proj_made, p.count(1, 1))
                dve.scalar_tensor_tensor(x1[:, p.off % 2, :], t_ps[:, 0, 0:D], f_out, x_sb[:, p.off % 4, :],
                                         ALU.mult, ALU.add).then_inc(s.x1_done, 1)

            def norm_copies(t):
                p, n = t.at(-1), t.at(2)
                if p.exists():
                    dve.wait_ge(s.x2T_made, p.count(1, 1))
                    dve.tensor_copy(x2T[:, :, :, :].rearrange("p a k n -> p (a k n)"), st[0][:, 0:4 * P]).then_inc(s.x2T_ready, 1)
                dve.wait_ge(s.xT_made, n.count(1, 1))
                dve.tensor_copy(xT[:, n.off % 2].rearrange("p a k n -> p (a k n)"), st[1][:, 0:4 * P]).then_inc(s.xT_ready, 1)

            def maxima(t, u, par):
                i, G = t.i, GROUP[t.i]
                L = (i + 1) * P
                w = s_off(i, 1) if G > 1 else L
                flat = s_ps[:, :, :].rearrange("p a n -> p (a n)")
                view = flat[:, 1024 * par:1024 * par + G * w].rearrange("p (g n) -> p g n", g=G)[:, :, 0:L]
                dve.wait_ge(s.s_made, t.units(2, u, 2))
                dve.tensor_reduce(smax[:, par, 0:G], view, AX_X, ALU.max).then_inc(s.maxs, 1)
                dve.wait_ge(s.maxs, t.units(1, u, 1))
                if shifted(i, u):
                    dve.tensor_tensor(probs[:, par, 0:G * L].rearrange("p (g n) -> p g n", g=G), view,
                                      smax[:, par, 0:G].unsqueeze(2).broadcast_to([P, G, L]),
                                      ALU.subtract).then_inc(s.max_ready, 1)
                    return
                dve.tensor_scalar(nmax[:, par, 0:G], smax[:, par, 0:G], f_natt, None, ALU.mult).then_inc(s.max_ready, 1)

            def half_maximum(t, u, par, h):
                G = GROUP[t.i]
                dve.wait_ge(s.s_made, t.units(2, u, h + 1))
                bank = s_ps[:, 2 * par + h, :]
                if G == 1:
                    _, j0, j1 = halves(t.i)[h][0]
                    last = dve.tensor_reduce(smax[:, par, h:h + 1], bank[:, 0:(j1 - j0) * P], AX_X, ALU.max)
                else:
                    n = G // 2
                    view = bank.rearrange("p (g n) -> p g n", g=n)[:, :, 0:(t.i + 1) * P]
                    last = dve.tensor_reduce(smax[:, par, h * n:(h + 1) * n], view, AX_X, ALU.max)
                if not h:
                    return
                last.then_inc(s.maxs, 1)
                dve.wait_ge(s.maxs, t.units(1, u, 1))
                if G == 1:
                    last = dve.scalar_tensor_tensor(nmax[:, par, 0:1], smax[:, par, 0:1], smax[:, par, 1:2], f_natt, ALU.max,
                                                    ALU.mult)
                else:
                    last = dve.tensor_scalar(nmax[:, par, 0:G], smax[:, par, 0:G], f_natt, None, ALU.mult)
                last.then_inc(s.max_ready, 1)

            def attention(t):
                def unit(u, par):
                    for h in range(2):
                        w = P * len(half_tiles(t.i, h))
                        dve.wait_ge(s.hi_p, t.units(2, u, h + 1))
                        dve.tensor_tensor(pT[:, par, 1, h, 0:w], t_ps[:, h, 0:w], pT[:, par, 0, h, 0:w],
                                          ALU.subtract).then_inc(s.lo_p, 1)
                        if isinstance(u, int) and u == 1 and h == 0 and not SHORT[t.i]:
                            row_stats(t.at(2), t.at(-1))
                        if has_next(t, u, 2):
                            if SPLIT_MAX[t.i]:
                                half_maximum(t, u + 2, par, h)
                            elif h == 0:
                                maxima(t, u + 2, par)
                    if shifted(t.i, u):
                        G, L = GROUP[t.i], (t.i + 1) * P
                        dve.tensor_reduce(ssum[:, t.off % 2, 0, 0:G], probs[:, par, 0:G * L].rearrange("p (g n) -> p g n", g=G),
                                          AX_X, ALU.add).then_inc(s.o_evs, 1)
                    if isinstance(u, int) and u == 0:
                        places(t.at(-2))
                        if SHORT[t.i]:
                            slots_and_means(t.at(-2), None, None)
                    if isinstance(u, int) and u == 1 and not SHORT[t.i]:
                        slots_and_means(t.at(-2), t.at(2), t.at(-1))
                    if isinstance(u, int) and u == 1:
                        if t.at(1).exists() and shares_rope(t.at(1)):
                            rope_lo(t.at(1))
                    if isinstance(u, int):
                        search(t, u)
                for u in range(2):
                    maxima(t, u, u)
                att_loop(dve, t, unit)

            def hidden(p):
                dve.wait_ge(s.gate_done, p.count(1, 1))
                dve.scalar_tensor_tensor(hid[:, :], gate[:, :], 1.0, s_ps[:, 0, 0:SI], ALU.add, ALU.mult).then_inc(s.hids, 1)
                dve.wait_ge(s.hids, p.count(1, 1))
                dve.scalar_tensor_tensor(hid[:, :], hid[:, :], HSCALE, s_ps[:, 1, 0:SI], ALU.mult, ALU.mult).then_inc(s.hid_done, 1)
                dve.wait_ge(s.hi_h, p.count(1, 1))
                dve.tensor_tensor(hs[:, 1, :], hid[:, :], hs[:, 0, :], ALU.subtract).then_inc(s.lo_h, 1)

            def tile_at(ap, p):
                return ap[:, ds(p.off if p.b is None else p.b * TB + p.off, 1), :].rearrange("p a n -> p (a n)")

            def logits(p, st_):
                dve.wait_ge(s.lgt_made, p.count(1, 1))
                st_.do(dve.tensor_scalar(lg[:, p.off % 2, :], o_ps[:, 1, 0:E], wamp[:, A_R:A_R + 1], None, ALU.mult), own_wait)

            def router(p, st_):
                par = p.off % 2
                lg_t, top_t = lg[:, par, :], top8[:, par, :]
                st_.do(dve.max(top_t, lg_t), own_wait)
                st_.do(dve.max_index(top_ix[:, par, :], top_t, lg_t))
                dve.tensor_copy(tile_at(lg_all, p), lg_t)
                dve.tensor_copy(tile_at(top_all, p), top_t[:, 0:TOPK])
                st_.do(dve.tensor_copy(ixf[:, :], top_ix[:, par, 0:2]))
                for k in range(TOPK):
                    st_.do(dve.tensor_scalar(pick[:, par, k, :], iota_e_sb[:, :], ixf[:, k:k + 1], None, ALU.is_equal))
                dve.tensor_tensor(picked[:, par, :], pick[:, par, 0, :], pick[:, par, 1, :], ALU.add).then_inc(s.mask_ready, 1)

            def dense_sum(q):
                par = q.off % 2
                dve.wait_ge(s.down_made, q.count(1, 1))
                if q.at(-2).exists():
                    dve.wait_ge(stored[par], q.at(-2).pair(16))
                dve.scalar_tensor_tensor(den[:, par, :], o_ps[:, 0, 0:D], f_sd, x1[:, par, :], ALU.mult,
                                         ALU.add).then_inc(s.dense_done, 1)

            def places(q):
                if not q.exists():
                    return
                dve.wait_ge(s.rank_made, q.count(1, 1))
                dve.tensor_tensor(place[:, :], o_ps[:, 1, 0:E], used[:, :], ALU.add).then_inc(s.slot_s, 1)
                dve.tensor_tensor(used[:, :], used[:, :], o_ps[:, 1, E:2 * E], ALU.add).then_inc(s.slot_s, 1)
                if q.b is not None or q.off < NT - 1:
                    dense_sum(q)
                else:
                    dve.wait_ge(s.slot_s, q.count(4, 2))
                    dve.tensor_copy(free_i[:, :], used[0:1, :]).then_inc(s.used_ready, 1)

            def row_stats(n, p):
                last = None
                if n.off > 0 or n.b is not None:
                    dve.wait_ge(s.normed, n.at(-1).count(1, 1))
                if n.exists():
                    dve.wait_ge(xin[n.off % 4], 16 * (n.off // 4 + 1) if n.b is None else n.b * 32 + 16 * (n.off // 4 + 1))
                    last = dve.bn_stats(ln_st[:, 0, 0:6], x_sb[:, n.off % 4, :])
                if p is not None and p.exists():
                    dve.wait_ge(s.x1_done, p.count(1, 1))
                    last = dve.bn_stats(ln_st[:, 1, 0:6], x1[:, p.off % 2, :])
                if last is not None:
                    last.then_inc(s.stat_s, 1)

            def slots_and_means(q, n, p):
                has_q, has_n, has_p = (k is not None and k.exists() for k in (q, n, p))
                if has_q:
                    par = q.off % 2
                    dve.wait_ge(s.slot_s, q.count(4, 2))
                    for k in range(TOPK):
                        dve.tensor_tensor_reduce(place_k[:, k, :], pick[:, par, k, :], place[:, :], 1.0, 0.0, ALU.mult, ALU.add,
                                                 slot_f[:, k:k + 1]).then_inc(s.slot_s, 1)
                if has_n or has_p:
                    dve.wait_ge(s.stat_s, n.count(1, 1))
                    own_wait(dve)
                    if has_n:
                        last = dve.bn_aggr(ln_mv[:, 0, :], ln_st[:, 0, 0:6])
                    if has_p:
                        last = dve.bn_aggr(ln_mv[:, 1, :], ln_st[:, 1, 0:6])
                    last.then_inc(s.stats, 1)
                if has_q:
                    dve.wait_ge(s.slot_s, q.count(4, 4))
                    if q.at(-2).exists():
                        dve.wait_ge(scattered[par], q.at(-2).pair(32))
                    dve.tensor_copy(slot[:, par, :], slot_f[:, :]).then_inc(s.slot_done, 1)

            def means(n, p):
                row_stats(n, p)
                slots_and_means(None, n, p)

            means(Tile(0), None)
            means(Tile(1), None)
            first_weights()
            other_weights()
            latent_lo(Tile(0))
            rope_sum(Tile(0))
            query_lo(Tile(0))
            rope_lo(Tile(0))
            lo_parts(FIRST, FIRST + 1)
            qT_copies(Tile(0))
            lo_parts(FIRST + 1, len(SPLITS))

            SEARCH = {0: {'end': (0, 2)}, 1: {1: (2, 3), 2: (3, 4), 3: (4, 5), 'end': (5, 7)}, 2: {1: (7, 8), 6: (8, 9), 7: (9, 10), 'end': (10, 13)}, 3: {1: (13, 15), 6: (15, 16)}}

            def search(t, at_):
                if t.b is None and t.off in SEARCH and at_ in SEARCH[t.off]:
                    expert_magnitudes(*SEARCH[t.off][at_])

            def section(t):
                n = t.at(1)
                if n.exists():
                    latent_lo(n)
                if t.at(-1).exists():
                    oT_copy(t.at(-1))
                if n.exists():
                    query_lo(n)
                if n.exists() and shares_rope(n):
                    rope_sum(n)
                search(t, "residual")
                if t.at(-1).exists():
                    residual(t.at(-1))
                if t.exists() and SHORT[t.i]:
                    means(t.at(2), t.at(-1))
                if t.exists():
                    attention(t)
                    out_norm(t)
                else:
                    places(t.at(-2))
                    if t.at(-1).exists():
                        row_stats(t.at(2), t.at(-1))
                    slots_and_means(t.at(-2), t.at(2), t.at(-1))
                    if t.at(-1).exists():
                        norm(dve, t.at(2), t.at(-1))
                if n.exists():
                    qT_copies(n)
                if t.exists() and not EARLY_NORMS[t.i]:
                    norm_copies(t)
                if t.at(-1).exists():
                    steps = Steps(dve, s.route_s, 6, t.at(-1).count)
                    logits(t.at(-1), steps)
                    if not t.exists():
                        expert_rows(t.at(-1))
                        router(t.at(-1), steps)
                    hidden(t.at(-1))
                    if t.exists():
                        expert_rows(t.at(-1))
                        router(t.at(-1), steps)
                search(t, "end")
                if t.b is None and t.off == PEEL - 1:
                    expert_scales()
            sections(dve, section)

            st_ = Steps(dve, s.tail_s, 11, at)
            st_.do(dve.tensor_scalar(cnt[:, :], iota_e_sb[:, :], -float(LIST), None, ALU.mult))
            st_.do(dve.tensor_tensor(cnt[:, :], cnt[:, :], used[:, :], ALU.add))
            st_.do(dve.tensor_tensor(cmp_k[:, :, :], cnt[:, :].unsqueeze(2).broadcast_to([P, E, NT]), iota_k_sb[:, :, :], ALU.is_gt))
            st_.do(dve.tensor_reduce(tiles_e[:, :], cmp_k[:, :, :], AX_X, ALU.add))
            st_.do(dve.tensor_tensor_scan(ends[:, :], ones_e[:, :], tiles_e[:, :], 0.0, ALU.mult, ALU.add))
            st_.do(dve.tensor_scalar(jump[:, :], tiles_e[:, :], -float(P), float(LIST), ALU.mult, ALU.add))
            st_.do(dve.tensor_scalar(ge[:, :], ends[:, :], iota_p_sb[:, 0:1], None, ALU.is_le))
            dve.tensor_reduce(t_exp, ge[:, :], AX_X, ALU.add)
            st_.do(dve.tensor_tensor_reduce(jumped[:, :], ge[:, :], jump[:, :], 1.0, 0.0, ALU.mult, ALU.add, t_row))
            st_.do(dve.scalar_tensor_tensor(t_row, iota_p_sb[:, 0:1], float(P), t_row, ALU.mult, ALU.add))
            dve.tensor_scalar(t_exp, t_exp, float(E - 1), None, ALU.min)
            st_.do(dve.tensor_scalar(t_row, t_row, float(DUMMY), None, ALU.min))
            dve.sem_inc(s.tab_made, 1)
            dense_sum(Tile(NT - 1))
            dve.wait_ge(s.tab_turned, 1)
            st_.do(dve.tensor_copy(tab[:, :, :], s_ps[0:1, 0, 0:2 * P].rearrange("p (a n) -> p a n", a=2)[:, :, 0:NMT]))
            dve.sem_inc(s.tab_ready, 1)

            link(dve.tensor_tensor(w_d[:, :, :], lg_all[:, :, :], top_all[:, :, 0:1].broadcast_to([P, NT, E]), ALU.subtract))
            link(dve.tensor_tensor(w_t[:, :], top_all[:, :, 1], top_all[:, :, 0], ALU.subtract))
            dve.sem_inc(s.c_w, 1)

            def expert_hidden(n, par):
                dve.wait_ge(s.m_gate, n + 1)
                dve.scalar_tensor_tensor(m_m[:, :], m_g[:, :], 1.0, s_ps[:, par, 0:I_E], ALU.add, ALU.mult).then_inc(s.m_q, 1)
                dve.wait_ge(s.m_q, n + 1)
                dve.scalar_tensor_tensor(m_h[:, par, :], m_m[:, :], HSCALE, s_ps[:, par, I_E:2 * I_E], ALU.mult,
                                         ALU.mult).then_inc(s.m_hid, 1)
                dve.wait_ge(s.m_hi, n + 1)
                dve.tensor_tensor(m_hs[:, par, 1, :], m_h[:, par, :], m_hs[:, par, 0, :], ALU.subtract).then_inc(s.m_lo, 1)

            def hT_copy(n):
                dve.wait_ge(s.m_hT, n + 1)
                dve.tensor_copy(m_hT_sb[:, :, :, :].rearrange("p a k n -> p (a k n)"), ot[0][0:KE, 0:4 * P]).then_inc(s.m_hTs, 1)

            expert_hidden(0, 0)
            expert_hidden(1, 1)
            with dve.Fori(0, NMT // XB - 1) as m:
                for q in range(XB):
                    n = m * XB + q
                    hT_copy(n)
                    expert_hidden(n + 2, q % 2)
            for n in range(NMT - XB, NMT):
                hT_copy(n)
                if n + 2 < NMT:
                    expert_hidden(n + 2, n % 2)

            dve.wait_ge(s.w_exp, 2)
            link(dve.tensor_reduce(w_s[:, :], w_e[:, :, :], AX_X, ALU.add))
            link(dve.reciprocal(w_k[:, :, 0], w_s[:, :]))
            link(dve.tensor_tensor(w_k[:, :, 1], w_k[:, :, 0], w_t[:, :], ALU.mult))

            dve.wait_ge(s.dense_in, 16)
            with dve.Fori(0, NC // CB) as m:
                for q in range(CB):
                    dve.wait_ge(c_loaded[q], m * 32 + 32)
                    for k in range(TOPK):
                        for c in range(CT):
                            tile = m * (CB * CT) + (q * CT + c)
                            row = dense_sb[:, ds(tile, 1), :].rearrange("p a n -> p (a n)")
                            last = dve.scalar_tensor_tensor(row, c_in[q][:, k, c, :], w_k[:, ds(tile, 1), k], row, ALU.mult, ALU.add)
                        if k == 0:
                            last.then_inc(s.c_y0, 1)
                            dve.wait_ge(s.c_y0, m * CB + q + 1)
                    last.then_inc(s.c_sum, 1)

        @block.gpsimd
        def _(pool):
            def split_expert(e):
                def step(n, ins):
                    ins.then_inc(s.split, 1)
                    pool.wait_ge(s.split, SPLIT_STEPS * e + n)
                    own_wait(pool)
                one = ds(e, 1)
                pool.wait_ge(s.gu_scale, 1)
                pool.wait_ge(s.w_gu, 16 * KD)
                pool.wait_ge(s.w_d, 16 * 2)
                for k in range(KD):
                    raw = gu_raw[:, k, one, :].rearrange("p e j -> p (e j)")
                    raw_d = d_raw[0:KE, k, one, :].rearrange("p e j -> p (e j)")
                    gu, d = (w[:, k, one].rearrange("p e s j -> p s (e j)") for w in (wgu_sb, wd_sb))
                    pool.tensor_tensor(gu_w, raw, winv[:, A_GU:A_GU + 1].broadcast_to([P, 2 * I_E]), ALU.mult)
                    step(3 * k + 1, pool.tensor_tensor(d_w[0:KE], raw_d, winv[0:KE, A_D:A_D + 1].broadcast_to([KE, D]), ALU.mult))
                    pool.tensor_copy(gu[:, 0, :], gu_w)
                    step(3 * k + 2, pool.tensor_copy(d[0:KE, 0, :], d_w[0:KE]))
                    pool.tensor_tensor(gu[:, 1, :], gu_w, gu[:, 0, :], ALU.subtract)
                    step(3 * k + 3, pool.tensor_tensor(d[0:KE, 1, :], d_w[0:KE], d[0:KE, 0, :], ALU.subtract))

            def rope(n):
                st_ = Steps(pool, s.rope_s, 6, n.count)
                shared = shares_rope(n)
                pool.wait_ge(s.pe_ready, n.count(1, 1))
                if not shared:
                    st_.do(pool.tensor_tensor(rot, pe, rope_cos(n), ALU.mult))
                for k in range(2):
                    sin_b = sin_sb[:, n.i, k:ROPE:2].unsqueeze(1).broadcast_to([P, H + 1, ROPE // 2])
                    st_.do(pool.tensor_tensor(rot2[:, :, k:ROPE:2], pe[:, :, 1 - k:ROPE:2], sin_b, ALU.mult))
                if shared:
                    pool.sem_inc(s.rope_s, 4)
                    return
                pool.sem_inc(s.rot_s, 3)
                st_.do(pool.tensor_tensor(rot, rot, rot2, ALU.add), own_wait)
                st_.do(pool.tensor_copy(ks[:, 0, C:HD], rot[:, H, :]), own_wait)
                st_.do(pool.tensor_copy(qs[:, 0, :, NOPE:HD], rot[:, 0:H, :]))
                pool.tensor_tensor(ks[:, 1, C:HD], rot[:, H, :], ks[:, 0, C:HD], ALU.subtract)
                pool.tensor_tensor(qs[:, 1, :, NOPE:HD], rot[:, 0:H, :], qs[:, 0, :, NOPE:HD], ALU.subtract).then_inc(s.rope_done, 1)

            def out_lo(p):
                pool.wait_ge(s.hi_o, p.count(1, 1))
                pool.tensor_tensor(os_[:, 1, :], o_sb[:, :], os_[:, 0, :], ALU.subtract).then_inc(s.lo_o, 1)

            def scatter(q):
                par = q.off % 2
                pool.wait_ge(s.slot_done, q.count(1, 1))
                own_wait(pool)
                for k in range(TOPK):
                    pool.indirect_dma_start(lists, bass.IndirectOffsetOnAxis(slot[:, par, k:k + 1], 0), xs2[:, par, k, :],
                                            None).then_inc(scattered[par], 16)

            norm(pool, Tile(0), None)
            norm(pool, Tile(1), None)
            pool.wait_ge(s.amax_ready, 1)
            pool.partition_all_reduce(amax_all[:, 0:2], amax[:, 0:2], P, bass.bass_isa.ReduceOp.max).then_inc(s.amax_reduced, 1)
            pool.wait_ge(s.amax_ready, 2)
            pool.partition_all_reduce(amax_all[:, 2:6], amax[:, 2:6], P, bass.bass_isa.ReduceOp.max).then_inc(s.amax_reduced, 1)
            rope(Tile(0))

            def section(t):
                n = t.at(1)
                if n.exists():
                    rope(n)
                if t.b is not None or t.off < NT:
                    norm(pool, t.at(2), t.at(-1))
                if t.at(-2).exists():
                    scatter(t.at(-2))
                if t.exists() and t.i >= TB // 2:
                    split_expert((TB // 2) * (t.off // TB) + t.i - TB // 2 if t.b is None else t.b * (TB // 2) + (t.i - TB // 2))
                if t.b is None and t.off == PEEL - 1:
                    pool.wait_ge(s.gu_amax, 1)
                    pool.partition_all_reduce(amax_all[:, 6:8], amax[:, 6:8], P, bass.bass_isa.ReduceOp.max).then_inc(s.gu_red, 1)
                if t.exists():
                    out_lo(t)
            sections(pool, section)

            def send(n, q):
                pool.wait_ge(s.m_y, n + 2)
                own_wait(pool)
                pool.indirect_dma_start(y_exp, bass.IndirectOffsetOnAxis(xg[:, q, 2 * D:ROW].bitcast(I32), 0), m_ys[:, q % YB, :],
                                        None, bounds_check=NY - 1, oob_is_err=False).then_inc(m_out[q], 16)
            with pool.Fori(0, NMT // XB) as m:
                for q in range(XB):
                    send(m * XB + q, q)


def kernel(**inputs):
    import concourse.bacc as bacc
    from concourse import mybir as mb
    from concourse.bass_utils import run_bass_kernel_spmd

    g = {n: np.asarray(a) for n, a in inputs.items()}
    tr = lambda a, *ax: np.ascontiguousarray(np.transpose(a, ax))
    wqb = g["L0_attn_Wqb"].reshape(QL, H, HD)
    wkvb = g["L0_attn_Wkvb"].reshape(C, H, NOPE + VD)
    inv_freq = np.float32(1.0) / np.float32(10000.0) ** (np.arange(ROPE // 2, dtype=np.float32) * np.float32(2.0) / np.float32(ROPE))
    ang = np.arange(S, dtype=np.float32)[:, None] * inv_freq[None, :].astype(np.float32)
    cos = np.repeat(np.cos(ang), 2, axis=1).astype(np.float32)
    sin = np.stack([-np.sin(ang), np.sin(ang)], axis=-1).reshape(S, ROPE).astype(np.float32)
    q_at, k_at = np.arange(P)[:, None], np.arange(P)[None, :]
    arrays = {
        "x": np.ascontiguousarray(g["L0_attn_hidden_states"].reshape(NT * P, D)),
        "wqaT": tr(g["L0_attn_Wqa"], 1, 0),
        "wqb_peT": np.ascontiguousarray(wqb[:, :, NOPE:].reshape(QL, H * ROPE)),
        "wqb_nopeT": tr(wqb[:, :, :NOPE], 2, 1, 0),
        "wkva": np.ascontiguousarray(g["L0_attn_Wkva"]),
        "wkT": tr(wkvb[:, :, :NOPE], 2, 1, 0),
        "wvT": tr(wkvb[:, :, NOPE:], 2, 1, 0),
        "wo": np.ascontiguousarray(g["L0_attn_Wo"]),
        "gateT": tr(g["L0_ffn_gate_w"], 1, 0),
        "wgu": np.ascontiguousarray(g["L0_ffn_w_gate_up"]),
        "wd": np.ascontiguousarray(g["L0_ffn_w_down"]),
        "wsg": np.ascontiguousarray(g["L0_ffn_shared_gate_up"]),
        "wsd": np.ascontiguousarray(g["L0_ffn_shared_down"]),
        "cos_t": tr(cos.reshape(TB, P, ROPE), 1, 0, 2),
        "sin_t": tr(sin.reshape(TB, P, ROPE), 1, 0, 2),
        "ident": np.eye(P, dtype=np.float32),
        "causal": np.where(k_at > q_at, np.float32(-3e38), np.float32(0)).astype(np.float32),
        "tri": (q_at < k_at).astype(np.float32),
        "iota_e": np.tile(np.arange(E, dtype=np.float32), (P, 1)),
        "iota_k": np.tile((np.arange(NT, dtype=np.float32) * P), (P, E, 1)),
        "iota_p": np.arange(P, dtype=np.float32)[:, None],
        "tok_ids": (np.arange(P)[:, None] + np.arange(TOPK)[None, :] * (NT * P)).astype(np.float32),
    }
    nc = bacc.Bacc("TRN2", target_bir_lowering=False, num_devices=1)
    aps = [nc.dram_tensor(n, a.shape, mb.dt.from_np(a.dtype), kind="ExternalInput").ap() for n, a in arrays.items()]
    out = nc.dram_tensor("layer_out", (NT * P, D), F32, kind="ExternalOutput").ap()
    build(nc, *aps, out)
    r = run_bass_kernel_spmd(nc, [arrays], core_ids=[0])
    return r.results[0]["layer_out"].reshape(B, S, D)
```
